# Optimizing a Trainium2 kernel written in Bass

```python
import numpy as np
import jax
import jax.numpy as jnp

def _softmax(x, axis=-1):
    return jax.nn.softmax(x, axis=axis)

def _gelu(x):
    return jax.nn.gelu(x, approximate=True)

def _silu(x):
    return jax.nn.silu(x)

def _sigmoid(x):
    return jax.nn.sigmoid(x)

def _layernorm(x, axis=-1, eps=1e-05):
    m = jnp.mean(x, axis=axis, keepdims=True)
    v = jnp.var(x, axis=axis, keepdims=True)
    return (x - m) / jnp.sqrt(v + eps)

def _scatter_add(tgt, idx, src, axis=0):
    return tgt.at[idx].add(src)

def _segment_sum(src, seg, n):
    return jax.ops.segment_sum(src, seg, n)
kernel_name = 'mk_gnn_resnorm_d4_gnn_r8_0a070f'

def setup_inputs(seed: int=0):
    np.random.seed(seed)
    _w = jnp.asarray

    def _rec_inputs():
        import jax
        import jax.numpy as jnp
        _gk = jax.random.key(seed)
        x = -0.0002928 + 1 * jax.random.normal(jax.random.fold_in(_gk, 1), (1024, 512), jnp.float32)
        src = jax.random.randint(jax.random.fold_in(_gk, 2), (16384,), 0, 1024, jnp.int32)
        dst = jnp.minimum((1024 * jax.random.uniform(jax.random.fold_in(_gk, 3), (16384,)) ** 2.0).astype(jnp.int32), 8191)
        _o = jnp.argsort(dst, stable=True)
        src = src[_o]
        dst = dst[_o]
        return (x, src, dst)
    x, src, dst = _rec_inputs()

    def _L0_gnn_setup():
        import jax, jax.numpy as jnp
        import numpy as np
        N = 1024
        D = 512
        E = 32768
        STEPS = 3
        key = jax.random.key(seed)
        k1, k2, k3 = jax.random.split(key, 3)
        x = jax.random.normal(k1, (N, D), dtype=jnp.float32)
        edge_index = jax.random.randint(k2, (2, E), 0, N, dtype=jnp.int32)
        W = jax.random.normal(k3, (D, D), dtype=jnp.float32) / np.sqrt(D)
        b = jnp.zeros((D,), dtype=jnp.float32)
        diffusion_weights = jnp.ones((STEPS + 1,), dtype=jnp.float32) / (STEPS + 1)
        return {'x': x, 'edge_index': edge_index, 'W': W, 'b': b, 'diffusion_weights': diffusion_weights}
    _L0_gnn_all = _L0_gnn_setup()
    _L0_gnn_in = {k: v for k, v in _L0_gnn_all.items() if k in ('W', 'b', 'diffusion_weights')}
    del _L0_gnn_all

    def _L1_gnn_setup():
        import jax, jax.numpy as jnp
        import numpy as np
        N_SRC = 6250
        N_EDGES = 18750
        D_IN = 512
        D_OUT = 512
        key = jax.random.key(seed)
        k1, k2, k3, k4, k5 = jax.random.split(key, 5)
        src_h = jax.random.normal(k1, (N_SRC, D_IN), dtype=jnp.float32)
        W = jax.random.normal(k2, (D_OUT, D_IN), dtype=jnp.float32) * (1.0 / np.sqrt(D_IN))
        b = jax.random.normal(k3, (D_OUT,), dtype=jnp.float32) * 0.01
        src_idx = jax.random.randint(k4, (N_EDGES,), 0, N_SRC, dtype=jnp.int64) if jax.config.jax_enable_x64 else jax.random.randint(k4, (N_EDGES,), 0, N_SRC, dtype=jnp.int32)
        dst_idx = jax.random.randint(k5, (N_EDGES,), 0, N_SRC, dtype=src_idx.dtype)
        return {'src_h': src_h, 'W': W, 'b': b, 'src_idx': src_idx, 'dst_idx': dst_idx, 'n_dst': N_SRC}
    _L1_gnn_all = _L1_gnn_setup()
    _L1_gnn_in = {k: v for k, v in _L1_gnn_all.items() if k in ('W', 'b')}
    del _L1_gnn_all

    def _L2_gnn_setup():
        import jax, jax.numpy as jnp
        import numpy as np
        N = 6250
        IN_CH = 512
        OUT_CH = 512
        DEG = 32
        E = N * DEG
        key = jax.random.key(seed)
        kx, kwc, kwn, kb, ke = jax.random.split(key, 5)
        x = jax.random.normal(kx, (N, IN_CH), dtype=jnp.float32)
        bound = 1.0 / np.sqrt(IN_CH)
        wc = jax.random.uniform(kwc, (IN_CH, OUT_CH), minval=-bound, maxval=bound, dtype=jnp.float32)
        wn = jax.random.uniform(kwn, (IN_CH, OUT_CH), minval=-bound, maxval=bound, dtype=jnp.float32)
        bias = jax.random.uniform(kb, (OUT_CH,), minval=-bound, maxval=bound, dtype=jnp.float32)
        src = jnp.repeat(jnp.arange(N, dtype=jnp.int64), DEG)
        dst = jax.random.randint(ke, (E,), 0, N, dtype=jnp.int64)
        edge_index = jnp.stack([src, dst], axis=0)
        return {'x': x, 'wc': wc, 'wn': wn, 'bias': bias, 'edge_index': edge_index}
    _L2_gnn_all = _L2_gnn_setup()
    _L2_gnn_in = {k: v for k, v in _L2_gnn_all.items() if k in ('wc', 'wn', 'bias')}
    del _L2_gnn_all

    def _L3_gnn_setup():
        import jax, jax.numpy as jnp
        import numpy as np
        N, E, H, D_IN, D_PRIME = (6250, 100000, 8, 512, 64)

        def _segment_softmax(scores, seg, num_segments):
            smax = jax.ops.segment_max(scores, seg, num_segments=num_segments)
            ex = jnp.exp(scores - smax[seg])
            denom = jax.ops.segment_sum(ex, seg, num_segments=num_segments)
            return ex / denom[seg]
        key = jax.random.key(seed)
        ks = jax.random.split(key, 6)
        x = jax.random.normal(ks[0], (N, D_IN), dtype=jnp.float32)
        edge_index = jax.random.randint(ks[1], (2, E), 0, N)
        Ws = jax.random.normal(ks[2], (H, D_IN, D_PRIME), dtype=jnp.float32) * 0.05
        Wb = jax.random.normal(ks[3], (H, D_PRIME), dtype=jnp.float32) * 0.05
        a_w = jax.random.normal(ks[4], (H, 2 * D_PRIME), dtype=jnp.float32) * 0.05
        a_b = jax.random.normal(ks[5], (H,), dtype=jnp.float32) * 0.05
        return dict(x=x, edge_index=edge_index, Ws=Ws, Wb=Wb, a_w=a_w, a_b=a_b)
    _L3_gnn_all = _L3_gnn_setup()
    _L3_gnn_in = {k: v for k, v in _L3_gnn_all.items() if k in ('Ws', 'Wb', 'a_w', 'a_b')}
    del _L3_gnn_all
    return {'x': x, 'src': src, 'dst': dst, 'L0_gnn_W': _L0_gnn_in['W'], 'L0_gnn_b': _L0_gnn_in['b'], 'L0_gnn_diffusion_weights': _L0_gnn_in['diffusion_weights'], 'L1_gnn_W': _L1_gnn_in['W'], 'L1_gnn_b': _L1_gnn_in['b'], 'L2_gnn_wc': _L2_gnn_in['wc'], 'L2_gnn_wn': _L2_gnn_in['wn'], 'L2_gnn_bias': _L2_gnn_in['bias'], 'L3_gnn_Ws': _L3_gnn_in['Ws'], 'L3_gnn_Wb': _L3_gnn_in['Wb'], 'L3_gnn_a_w': _L3_gnn_in['a_w'], 'L3_gnn_a_b': _L3_gnn_in['a_b']}

def reference(x, src, dst, L0_gnn_W, L0_gnn_b, L0_gnn_diffusion_weights, L1_gnn_W, L1_gnn_b, L2_gnn_wc, L2_gnn_wn, L2_gnn_bias, L3_gnn_Ws, L3_gnn_Wb, L3_gnn_a_w, L3_gnn_a_b):
    import jax
    import jax.numpy as jnp

    def _L0_gnn_ref(x, edge_index, W, b, diffusion_weights):
        import jax, jax.numpy as jnp
        import numpy as np
        N = 1024
        D = 512
        E = 32768
        STEPS = 3
        h = x @ W + b
        row, col = (edge_index[0], edge_index[1])
        adj = jnp.zeros((N, N), dtype=h.dtype)
        adj = adj.at[row, col].set(1.0)
        adj = adj.at[col, row].set(1.0)
        adj = adj + jnp.eye(N, dtype=h.dtype)
        row_sum = adj.sum(axis=1, keepdims=True)
        adj = adj / jnp.maximum(row_sum, 1.0)
        out = diffusion_weights[0] * h
        cur = h
        for i in range(STEPS):
            cur = adj @ cur
            out = out + diffusion_weights[i + 1] * cur
        return jax.nn.relu(out)

    def _L1_gnn_ref(src_h, W, b, src_idx, dst_idx, n_dst):
        import jax, jax.numpy as jnp
        import numpy as np
        N_SRC = 6250
        N_EDGES = 18750
        D_IN = 512
        D_OUT = 512
        msgs = src_h[src_idx]
        agg = jax.ops.segment_sum(msgs, dst_idx, num_segments=n_dst)
        return agg @ W.T + b

    def _L2_gnn_ref(x, wc, wn, bias, edge_index):
        import jax, jax.numpy as jnp
        import numpy as np
        N = 6250
        IN_CH = 512
        OUT_CH = 512
        DEG = 32
        E = N * DEG
        alpha = x @ wc
        beta = x @ wn
        src, dst = (edge_index[0], edge_index[1])
        sums = jax.ops.segment_sum(beta[dst], src, num_segments=x.shape[0])
        counts = jax.ops.segment_sum(jnp.ones_like(src, dtype=beta.dtype), src, num_segments=x.shape[0])
        gamma = sums / counts[:, None]
        return alpha + gamma + bias

    def _L3_gnn_ref(x, edge_index, Ws, Wb, a_w, a_b):
        import jax, jax.numpy as jnp
        import numpy as np
        N, E, H, D_IN, D_PRIME = (6250, 100000, 8, 512, 64)

        def _segment_softmax(scores, seg, num_segments):
            smax = jax.ops.segment_max(scores, seg, num_segments=num_segments)
            ex = jnp.exp(scores - smax[seg])
            denom = jax.ops.segment_sum(ex, seg, num_segments=num_segments)
            return ex / denom[seg]
        v_src, v_tgt = (edge_index[0], edge_index[1])
        n = x.shape[0]
        outs = []
        for h in range(Ws.shape[0]):
            Wx = x @ Ws[h] + Wb[h]
            d = Wx.shape[-1]
            s = Wx[v_tgt] @ a_w[h, :d] + Wx[v_src] @ a_w[h, d:] + a_b[h]
            s = jax.nn.leaky_relu(s, negative_slope=0.2)
            alpha = _segment_softmax(s, v_tgt, n)
            outs.append(jax.ops.segment_sum(alpha[:, None] * Wx[v_src], v_tgt, num_segments=n))
        return jnp.stack(outs, axis=1).reshape(n, -1)
    edge_index = jnp.stack([src, dst])
    x = _layernorm(x + _L0_gnn_ref(x, edge_index, L0_gnn_W, L0_gnn_b, L0_gnn_diffusion_weights), axis=-1)
    x = _layernorm(x + _L1_gnn_ref(x, L1_gnn_W, L1_gnn_b, src, dst, 1024), axis=-1)
    x = _layernorm(x + _L2_gnn_ref(x, L2_gnn_wc, L2_gnn_wn, L2_gnn_bias, edge_index), axis=-1)
    x = _layernorm(x + _L3_gnn_ref(x, edge_index, L3_gnn_Ws, L3_gnn_Wb, L3_gnn_a_w, L3_gnn_a_b), axis=-1)
    return x

_drawn_inputs = setup_inputs


def setup_inputs(seed=0):
    import zlib

    import numpy as np

    out = dict(_drawn_inputs(seed))
    spreads = {'L0_gnn_b': (0.0, 0.1), 'L0_gnn_diffusion_weights': (0.25, 0.6)}
    factors = {'L1_gnn_b': 8.0, 'L3_gnn_a_b': 8.0}
    for name, (base, spread) in spreads.items():
        noise = np.random.default_rng([zlib.crc32(name.encode()), seed]).standard_normal(out[name].shape)
        drawn = base * np.exp(spread * noise) if base else spread * noise
        out[name] = jnp.asarray(drawn.astype(out[name].dtype))
    for name, factor in factors.items():
        out[name] = (out[name] * factor).astype(out[name].dtype)
    return out
```

```python
from contextlib import ExitStack

import concourse.bass as bass
from concourse import mybir
from concourse.alu_op_type import AluOpType as ALU

F32 = mybir.dt.float32
F16 = mybir.dt.float16
I32 = mybir.dt.int32
ACT = mybir.ActivationFunctionType
AX = mybir.AxisListType.X

P = 128
N = 1024
D = 512
E = 16384
NT = N // P
KT = D // P
HALF = 512
H = 8
DH = D // H
STEPS = 3
EPS = 1e-5
SLOPE = 0.2

GROUP = 256
NG = E // GROUP
NC = GROUP // P
WIN = 48
KEYS = NT * WIN

WSCALE = 64.0
ASCALE = 1.0 / 32
VCOL = 32


def build(nc, x, xT, src, dst, W0, b0, dw, W1T, b1, wc, wn, b2, W3, W3T, b3, b3T, aw, ab, out):
    with ExitStack() as ctx:
        def sb(name, shape, dt):
            return ctx.enter_context(nc.sbuf_tensor(name, shape, dt))

        def sem(name):
            return ctx.enter_context(nc.semaphore(name))

        ps = ctx.enter_context(nc.psum_tensor("ps", [P, NT, HALF], F32))

        c32 = sb("c32", [P, NT, N], F32)
        cst = sb("cst", [P, NT, N], F16)
        cts = sb("cts", [P, NT, N], F16)
        adj = sb("adj", [P, NT, N], F16)
        gT = adj[:].rearrange("p a b -> p (a b)").rearrange("p (v k n) -> p v k n", v=2, k=KT)
        xcur = sb("xcur", [P, NT, D], F32)
        acc = sb("acc", [P, NT, D], F32)
        xTraw = acc[:].rearrange("p a b -> p (a b)").rearrange("p (k n) -> p k n", k=KT)
        ub = acc[:].rearrange("p a b -> p (a b)").rearrange("p (q v n) -> p q v n", q=2, v=2)
        xTs = sb("xTs", [P, 2, KT, N], F16)
        cur = sb("cur", [P, 2, 2, NT, D], F16)
        stage = cur[:, 1].rearrange("p v a b -> p (v a b)").bitcast(F32).rearrange(
            "p (s k n) -> p s k n", s=2, k=KT)
        tep = cur[:].rearrange("p s v a b -> p (s v a b)").bitcast(F32).rearrange(
            "p (f n) -> p f n", n=N)
        wx = cts[:].rearrange("p a b -> p (a b)").bitcast(F32).rearrange("p (a b) -> p a b", a=NT)
        ws = sb("ws", [P, 4, 2, KT, D], F16)
        SLOT = {"W0": 0, "W1": 1, "wc": 2, "wn": 3, "W3": 0}

        iota_lo = sb("iota_lo", [P, P], F16)
        iota_key = sb("iota_key", [P, KEYS], F16)
        id32 = sb("id32", [P, P], F32)
        id16 = sb("id16", [P, P], F16)
        ones16 = sb("ones16", [P, P], F16)
        sel = sb("sel", [H, H + 1, P], F16)
        epsc = sb("epsc", [P, 1], F32)

        cflat = cst[:].rearrange("p a b -> p (a b)")
        oh_end = 2 * NC * (P + KEYS)
        oh_lo = cflat[:, NT * N - oh_end:NT * N - 2 * NC * KEYS].rearrange("p (b n) -> p b n", n=P)
        oh_key = cflat[:, NT * N - 2 * NC * KEYS:NT * N].rearrange("p (b n) -> p b n", n=KEYS)
        tmp = cst[0:NG].rearrange("p a b -> p (a b)").bitcast(F32).rearrange("p (f e) -> p f e", e=GROUP)
        tmpi = cst[0:NG].rearrange("p a b -> p (a b)").bitcast(I32).rearrange("p (f e) -> p f e", e=GROUP)
        e_dst, e_src, i_hi, i_lo = (tmpi[:, i, :] for i in range(4))
        f_dst, f_hi, f_lo, f_rel, f_key, f_bad = (tmp[:, i, :] for i in range(4, 10))
        base = sb("base", [NG, 2], F32)
        base_i = sb("base_i", [1, NG + 1], I32)
        slo = sb("slo", [P, NC, NG], F32)
        slo_g = sb("slo_g", [P, 2, NC], F32)
        key = sb("key", [P, NC, NG + 1], F32)

        b0f = cts[0:1, 0, :].bitcast(F32)
        b0s = cts[0:1, 1, :].rearrange("p (v d) -> p v d", v=2)
        bb = sb("bb", [P, 3, D], F32)
        dwb = sb("dwb", [P, STEPS + 1], F32)
        hb = cts[:, 2, :].bitcast(F32)
        deg = sb("deg", [P, NT], F32)
        invdeg = sb("invdeg", [P, NT], F32)
        winv = sb("winv", [P, STEPS, NT], F32)
        cnt = sb("cnt", [P, NT], F32)
        cnt1 = sb("cnt1", [P, NT], F32)
        gsc = sb("gsc", [P, NT], F32)
        nan = sb("nan", [P, NT], F32)
        st = sb("st", [P, 2, 6], F32)
        mv = sb("mv", [P, 2, 2], F32)
        std = sb("std", [P, NT], F32)
        rstd = sb("rstd", [P, NT], F32)
        abT = sb("abT", [P, KT, VCOL + H], F32)
        wa = sb("wa", [P, 2, KT, VCOL + H], F16)
        wbc = sb("wbc", [P, KT], F32)
        abc = sb("abc", [H, 1], F32)
        crow = sb("crow", [H, 3], F32)
        vc = sb("vc", [P, 2, NT * H], F32)
        wxh = xTs[:].rearrange("p v k n -> p (v k n)").bitcast(F32)[:, 0:2 * NT * (DH + 1)].rearrange(
            "p (q t d) -> p q t d", q=2, t=NT)
        rden = sb("rden", [P, 2, 4], F32)
        rows = tep[0:H]
        z0, vrow, zrow, mrow = (rows[:, i, :] for i in range(4))
        urow = tep[0:H, 4:6, :]
        us = adj[0:H].rearrange("p a b -> p (a b)")[:, 0:4 * N].rearrange(
            "p (v a n) -> p v a n", v=2, a=2)
        T, EX, PR = (tep[:, 2 * i:2 * i + 2, :] for i in range(3))
        oT = tep[0:DH + 1, 6, :]
        att = tep[:, 7, 0:HALF].rearrange("p (t d) -> p t d", d=DH)

        class Semaphores(dict):
            def __missing__(self, name):
                self[name] = sem(name)
                return self[name]

        S = Semaphores()

        def settle(pool):
            pool.wait_ge(S["const_ready"], 11)

        def bank16(t):
            return ps[:, t, :].bitcast(F16)

        block = ctx.enter_context(nc.Block())

        @block.sync
        def _(sp):
            sp.dma_start(e_dst, dst.rearrange("(g e) -> g e", e=GROUP)).then_inc(S["edges"], 16)
            sp.dma_start(e_src, src.rearrange("(g e) -> g e", e=GROUP)).then_inc(S["edges"], 16)
            sp.dma_start(xTraw, xT.rearrange("(k p) n -> p k n", p=P)).then_inc(S["xT_in"], 16)
            sp.dma_start(stage[:, 0], W0.rearrange("(k p) n -> p k n", p=P)).then_inc(S["w_in0"], 16)
            sp.dma_start(b0f, b0.rearrange("(a d) -> a d", a=1)).then_inc(S["small_in"], 16)
            sp.dma_start(dwb[:], dw.rearrange("(a d) -> a d", a=1).broadcast_to([P, STEPS + 1])).then_inc(S["small_in"], 16)
            sp.dma_start(stage[:, 1], W1T.rearrange("(k p) n -> p k n", p=P)).then_inc(S["w_in1"], 16)
            sp.dma_start(xcur[:], x.rearrange("(t p) d -> p t d", p=P)).then_inc(S["x_in"], 16)
            for i, b in enumerate((b1, b2, b3)):
                sp.dma_start(bb[:, i, :], b.rearrange("(a d) -> a d", a=1).broadcast_to([P, D])).then_inc(S["small_in"], 16)
            sp.dma_start(wbc[:], b3T).then_inc(S["small_in"], 16)
            sp.dma_start(abc[:], ab.rearrange("(h a) -> h a", a=1)).then_inc(S["small_in"], 16)
            sp.wait_ge(S["const_ready"], 8)
            step = VCOL + H + 2
            flat = abT[:].rearrange("p k c -> p (k c)")
            for q in range(2):
                for u in range(2):
                    c0 = VCOL * u + q
                    sp.dma_start(flat[q * DH:(q + 1) * DH, c0:c0 + 3 * step + 1:step],
                                 aw.rearrange("(j q) (u p) -> q u p j", q=2, p=DH)[q, u],
                                 allow_slow_non_contiguous=True).then_inc(S["small_in"], 16)
            for n, w in enumerate((wc, wn, W3, W3T)):
                sp.wait_ge(S["w_lo"], n + 1)
                sp.dma_start(stage[:, n % 2], w.rearrange("(k p) n -> p k n", p=P)).then_inc(
                    S[f"w_in{n + 2}"], 16)
            for t in range(NT):
                sp.wait_ge(S["x_ready"], 3 * NT + t + 1)
                sp.dma_start(out.rearrange("(t p) d -> t p d", p=P)[t], xcur[:, t, :]).then_inc(S["out_done"], 16)
            sp.wait_ge(S["out_done"], 16 * NT)
        SMALL = 16 * 11

        @block.gpsimd
        def _(pool):
            pool.iota(iota_lo[:], [[1, P]], base=0, channel_multiplier=0,
                      allow_small_or_imprecise_dtypes=True).then_inc(S["const_ready"], 1)
            pool.iota(iota_key[:], [[1, KEYS]], base=0, channel_multiplier=0,
                      allow_small_or_imprecise_dtypes=True).then_inc(S["const_ready"], 1)
            pool.memset(id32[:], 0.0).then_inc(S["const_ready"], 1)
            pool.memset(id16[:], 0.0).then_inc(S["const_ready"], 1)
            pool.memset(sel[:], 0.0).then_inc(S["const_ready"], 1)
            pool.memset(ones16[:], 1.0).then_inc(S["const_ready"], 1)
            pool.memset(epsc[:], EPS).then_inc(S["const_ready"], 1)
            pool.memset(abT[:], 0.0).then_inc(S["const_ready"], 1)
            pool.wait_ge(S["const_ready"], 8)
            for ident in (id32, id16):
                pool.affine_select(out=ident[:], in_=ident[:], compare_op=ALU.not_equal, fill=1.0, base=0,
                                   pattern=[[-1, P]], channel_multiplier=1).then_inc(S["const_ready"], 1)
            pool.affine_select(out=sel[:], in_=sel[:], compare_op=ALU.not_equal, fill=1.0, base=0,
                               pattern=[[-1, H + 1], [0, P]], channel_multiplier=1).then_inc(S["const_ready"], 1)
            pool.memset(c32[:, NT // 2:NT, :], 0.0).then_inc(S["c32z"], 1)

            pool.sem_inc(S["acc0"], 1)
            pool.wait_ge(S["xT_in"], 16)
            pool.wait_ge(S["xT_hi"], 1)
            pool.tensor_tensor(xTs[:, 1], xTraw, xTs[:, 0], ALU.subtract).then_inc(S["xT_lo"], 1)

            def split_lo(n, name):
                pool.wait_ge(S["w_hi"], n + 1)
                pool.tensor_tensor(ws[:, SLOT[name], 1], stage[:, n % 2], ws[:, SLOT[name], 0],
                                   ALU.subtract).then_inc(S["w_lo"], 1)
            split_lo(0, "W0")
            pool.wait_ge(S["b0_ready"], 2)
            pool.tensor_tensor(b0s[:, 1, :], b0f, b0s[:, 0, :], ALU.subtract).then_inc(S["b0_ready"], 1)

            pool.wait_ge(S["key_in"], 5)
            pool.wait_ge(S["small_in"], SMALL)
            with pool.Fori(0, NT) as t:
                for i in range(NT):
                    g = t * NT + i
                    pool.wait_ge(S["hot_free"], g + 1)
                    settle(pool)
                    pool.tensor_copy(slo_g[:, i % 2, :], slo[:, :, bass.ds(g, 1)]).then_inc(S["slo_g"], 1)
                    pool.drain()
                    for c in range(NC):
                        pool.tensor_scalar(oh_lo[:, i % 2 * NC + c, :], iota_lo[:], slo_g[:, i % 2, c:c + 1], None,
                                           ALU.is_equal).then_inc(S["lo_ready"], 1)
                pool.wait_ge(S["h_cp"], t + 1)
                settle(pool)
                pool.tensor_tensor(cur[:, 0, 1, t, :], hb, cur[:, 0, 0, t, :],
                                   ALU.subtract).then_inc(S["h_lo"], 1)
                pool.tensor_tensor(acc[:, t, :], hb, dwb[:, 0:1].broadcast_to([P, D]), ALU.mult).then_inc(S["acc0"], 1)
            for n, name in enumerate(("W1", "wc", "wn", "W3")):
                split_lo(n + 1, name)

            for layer in range(3):
                with pool.Fori(0, NT) as t:
                    pool.wait_ge(S["x_hi"], t + (layer * NT + 1))
                    settle(pool)
                    pool.tensor_tensor(cur[:, 1, 1, t, :], xcur[:, t, :], cur[:, 1, 0, t, :],
                                       ALU.subtract).then_inc(S["x_lo"], 1)
                    if layer < 2:
                        pool.tensor_tensor(xcur[:, t, :], xcur[:, t, :], bb[:, layer, :],
                                           ALU.add).then_inc(S["xb_ready"], 1)
            pool.wait_ge(S["wx_in"], NT)
            pool.memset(wxh[:, :, :, DH:DH + 1], 1.0).then_inc(S["ones_wxh"], 1)
            pool.wait_ge(S["ones_wxh"], 1)
            with pool.Fori(0, H // 2) as hp:
                for q in range(2):
                    h = hp * 2 + q
                    pool.wait_ge(S["back_done"], h + 1)
                    pool.tensor_copy(wxh[:, q, :, 0:DH], wx[:, :, bass.ds(h * DH, DH)]).then_inc(S["wxh_ready"], 1)

        @block.scalar
        def _(act):
            def copy(o, i, scale=1.0, **kw):
                return act.activation(o, i, ACT.Copy, scale=scale, **kw)

            act.wait_ge(S["xT_in"], 16)
            copy(xTs[:, 0], xTraw).then_inc(S["xT_hi"], 1)

            def split_hi(n, name):
                act.wait_ge(S[f"w_in{n}"], 16)
                copy(stage[:, n % 2], stage[:, n % 2], WSCALE).then_inc(S["w64"], 1)
                act.wait_ge(S["w64"], n + 1)
                copy(ws[:, SLOT[name], 0], stage[:, n % 2]).then_inc(S["w_hi"], 1)
            split_hi(0, "W0")
            act.wait_ge(S["small_in"], SMALL)
            copy(b0f, b0f, WSCALE).then_inc(S["b0_ready"], 1)
            act.wait_ge(S["b0_ready"], 1)
            copy(b0s[:, 0, :], b0f).then_inc(S["b0_ready"], 1)
            split_hi(1, "W1")
            with act.Fori(0, NT) as t:
                act.wait_ge(S["h_done"], t + 1)
                copy(cur[:, 0, 0, t, :], ps[:, 2, :], 1 / WSCALE).then_inc(S["h_hi"], 1)
                copy(hb, ps[:, 2, :], 1 / WSCALE).then_inc(S["h_cp"], 1)
                act.wait_ge(S["acc0"], t + 2)
            for n, name in enumerate(("wc", "wn", "W3")):
                split_hi(n + 2, name)

            act.wait_ge(S["win_free"], NG + 2)
            for j in range(NT):
                copy(cst[:, j, :], c32[:, j, :], accum_out=cnt[:, j:j + 1]).then_inc(S["cst_ready"], 1)
            with act.Fori(0, NT) as t:
                act.wait_ge(S["ct_done"], t + 1)
                copy(cts[:, t, :], bank16(t)).then_inc(S["cts_ready"], 1)

            act.wait_ge(S["inv_r"], 1)
            act.wait_ge(S["w_lo"], 5)
            act.wait_ge(S["wa_done"], 1)
            for k in range(1, STEPS):
                with act.Fori(0, NT) as t:
                    act.wait_ge(S["step_done"], t + ((k - 1) * NT + 1))
                    copy(cur[:, k % 2, 0, t, :], ps[:, t, :], invdeg[:, bass.ds(t, 1)]).then_inc(S["step_hi"], 1)

            def sqrt(layer, t, i):
                act.wait_ge(S["moments"], t + (layer * NT + 1))
                act.activation(std[:, bass.ds(t, 1)], mv[:, i, 1:2], ACT.Sqrt,
                               bias=epsc[:]).then_inc(S["std_ready"], 1)

            def x_hi(layer, t):
                act.wait_ge(S["x_ready"], t + (layer * NT + 1))
                copy(cur[:, 1, 0, t, :], xcur[:, t, :]).then_inc(S["x_hi"], 1)

            def xT_evict(layer, t):
                act.wait_ge(S["xT_done"], t + ((layer - 1) * NT + 1))
                copy(xTs[:, :, :, bass.ds(t * P, P)].rearrange("p v k n -> p (v k) n"),
                     bank16(t).rearrange("p (a n) -> p a n", n=P)).then_inc(S["xT_in2"], 1)

            def chains_hi(n):
                with act.Fori(0, 2) as half:
                    with act.Fori(0, KT) as k:
                        c = half * KT + k
                        act.wait_ge(S["chain_done"], c + (n * NT + 1))
                        copy(gT[:, 0, k, bass.ds(half * HALF, HALF)], ps[:, c, :], ASCALE).then_inc(S["chain_hi"], 1)

            for layer in range(3):
                with act.Fori(0, NT // 2) as r:
                    for i in range(2):
                        sqrt(layer, r * 2 + i, i)
                        x_hi(layer, r * 2 + i)
                if layer:
                    with act.Fori(0, NT) as t:
                        xT_evict(layer, t)
                if layer < 2:
                    chains_hi(layer)

            act.sem_inc(S["e_ready"], 2)
            def u_copy(h, q):
                act.wait_ge(S["u_done"], h + 1)
                copy(ub[:, q], ps[:, 0:4, :].rearrange("p (v a) n -> p v (a n)", v=2)).then_inc(S["ub_ready"], 1)

            def exps(h, q, j):
                n = h * NT + j
                act.wait_ge(S["t_ready"], n + 1)
                act.wait_ge(S["p_ready"], n + 1)
                act.activation(EX[:, j % 2, :], T[:, j % 2, :], ACT.Exp,
                               bias=vc[:, 1, bass.ds(j * H + h, 1)]).then_inc(S["e_ready"], 1)

            def o_evict(h):
                act.wait_ge(S["p_free"], h * NT + (NT + 2))
                act.wait_ge(S["back_done"], h + 2)
                copy(oT, ps[0:DH + 1, 4:6, :].rearrange("p a n -> p (a n)")).then_inc(S["oT_in"], 1)

            u_copy(0, 0)
            with act.Fori(0, H // 2) as hp:
                for q in range(2):
                    h = hp * 2 + q
                    for j in range(NT):
                        exps(h, q, j)
                        if j == 3:
                            u_copy(h + 1, 1 - q)
                    o_evict(h)
            with act.Fori(0, NT // 2) as r:
                for i in range(2):
                    sqrt(3, r * 2 + i, i)

        @block.tensor
        def _(pe):
            mm = pe.matmul

            def three(bank, lhs, rhs, start=True, stop=True):
                ins = None
                for k in range(KT):
                    lh, ll = lhs(k)
                    rh, rl = rhs(k)
                    for n, (a, b) in enumerate(((lh, rh), (lh, rl), (ll, rh))):
                        ins = mm(bank, a, b, start=start and k == 0 and n == 0, stop=stop and k == KT - 1 and n == 2)
                return ins

            pe.sem_inc(S["hot_free"], 2)
            pe.sem_inc(S["p_free"], 2)
            pe.sem_inc(S["back_done"], 2)
            pe.wait_ge(S["const_ready"], 11)
            pe.wait_ge(S["idx"], 2)
            for c in range(NC):
                pe.transpose(ps[:, 2, c * NG:(c + 1) * NG], f_lo[:, c * P:(c + 1) * P], id32[0:NG, 0:NG])
                pe.transpose(ps[:, 3, c * NG:(c + 1) * NG], f_key[:, c * P:(c + 1) * P], id32[0:NG, 0:NG])
            pe.transpose(ps[0:1, 4, 0:NG], base[:, 0:1], id32[0:NG, 0:NG]).then_inc(S["tr"], 1)

            pe.wait_ge(S["key_in"], 5)
            with pe.Fori(0, NT) as t:
                for i in range(NT):
                    g = t * NT + i
                    pe.wait_ge(S["lo_ready"], g * NC + NC)
                    pe.wait_ge(S["key_ready"], g * NC + NC)
                    pe.wait_ge(S["win_free"], g + 1)
                    for c in range(NC):
                        b = i % 2 * NC + c
                        ins = mm(ps[:, i % 2, 0:KEYS], oh_lo[:, b, :], oh_key[:, b, :], start=c == 0, stop=c == NC - 1)
                    ins.then_inc(S["hot_free"], 1)
                pe.wait_ge(S["xT_lo"], 1)
                pe.wait_ge(S["w_lo"], 1)
                pe.wait_ge(S["b0_ready"], 3)
                pe.wait_ge(S["acc0"], t + 1)
                three(ps[:, 2, :], lambda k: [xTs[:, v, k, bass.ds(t * P, P)] for v in range(2)],
                      lambda k: [ws[:, SLOT["W0"], v, k, :] for v in range(2)], stop=False)
                for v in range(2):
                    ins = mm(ps[:, 2, :], ones16[0:1, :], b0s[:, v, :], start=False, stop=v == 1)
                ins.then_inc(S["h_done"], 1)

            pe.wait_ge(S["w_in5"], 16)
            pe.wait_ge(S["small_in"], SMALL)
            for k in range(KT):
                for j in range(KT):
                    mm(ps[:, 3, k * 64:k * 64 + VCOL + H], stage[:, 1, j, k * P:(k + 1) * P], abT[:, j, :],
                       start=j == 0, stop=j == KT - 1)
            for v in range(2):
                for j in range(KT):
                    ins = mm(ps[0:H, 3, 256:257], abT[:, j, VCOL * v:VCOL * v + H], wbc[:, j:j + 1],
                             start=v == 0 and j == 0, stop=v == 1 and j == KT - 1)
            ins.then_inc(S["wa_done"], 1)

            pe.wait_ge(S["cst_ready"], NT)
            pe.wait_ge(S["h_cp"], NT)
            pe.wait_ge(S["crow_r"], 1)
            with pe.Fori(0, NT) as t:
                for j in range(NT):
                    ins = pe.transpose(bank16(t)[:, j * P:(j + 1) * P], cst[:, j, bass.ds(t * P, P)], id16[:])
                ins.then_inc(S["ct_done"], 1)
            pe.wait_ge(S["adj_ready"], NT)
            pe.wait_ge(S["cts_ready"], NT)
            for t in range(NT):
                for j in range(NT):
                    ins = mm(ps[:, 0, t:t + 1], adj[:, j, t * P:(t + 1) * P], ones16[:, 0:1],
                             start=j == 0, stop=j == NT - 1)
            ins.then_inc(S["deg_done"], 1)

            pe.wait_ge(S["h_lo"], NT)
            pe.wait_ge(S["h_hi"], NT)
            pe.wait_ge(S["inv_r"], 1)
            for k in range(1, STEPS + 1):
                def step(t, first):
                    for j in range(NT):
                        if first and k > 1:
                            pe.wait_ge(S["step_lo"], (k - 2) * NT + j + 1)
                        for v in range(2):
                            ins = mm(ps[:, t, :], adj[:, j, bass.ds(t * P, P)], cur[:, (k - 1) % 2, v, j, :],
                                     start=j == 0 and v == 0, stop=j == NT - 1 and v == 1)
                    ins.then_inc(S["step_done"], 1)
                if k > 1:
                    pe.wait_ge(S["acc_r"], (k - 2) * NT + 1)
                step(0, True)
                with pe.Fori(1, NT) as t:
                    if k > 1:
                        pe.wait_ge(S["acc_r"], t + ((k - 2) * NT + 1))
                    step(t, False)

            def chains(n, c16):
                with pe.Fori(0, 2) as half:
                    with pe.Fori(0, KT) as k:
                        c = half * KT + k
                        if n:
                            pe.wait_ge(S["xT_in2"], c + 1)
                        for j in range(NT):
                            for v in range(2):
                                ins = mm(ps[:, c, :], cur[:, 1, v, j, bass.ds(k * P, P)],
                                         c16[:, j, bass.ds(half * HALF, HALF)],
                                         start=j == 0 and v == 0, stop=j == NT - 1 and v == 1)
                        ins.then_inc(S["chain_done"], 1)

            def times(src_, name, done, before):
                with pe.Fori(0, 2) as half:
                    with pe.Fori(0, NT // 2) as r:
                        t = half * (NT // 2) + r
                        before(half, t)
                        three(ps[:, t, :], lambda k: [src_[:, v, k, bass.ds(t * P, P)] for v in range(2)],
                              lambda k: [ws[:, SLOT[name], v, k, :] for v in range(2)]).then_inc(S[done], 1)

            def chains_split(n):
                def f(half, t):
                    pe.wait_ge(S["chain_hi"], half * KT + (n * NT + KT))
                    pe.wait_ge(S["chain_lo"], half * KT + (n * NT + KT))
                return f

            def x_transposes(layer):
                with pe.Fori(0, NT) as t:
                    pe.wait_ge(S["x_lo"], t + (layer * NT + 1))
                    for v in range(2):
                        for k in range(KT):
                            a = v * KT + k
                            ins = pe.transpose(bank16(t)[:, a * P:(a + 1) * P], cur[:, 1, v, t, k * P:(k + 1) * P], id16[:])
                    ins.then_inc(S["xT_done"], 1)

            pe.wait_ge(S["x_lo"], NT)
            chains(0, cst)
            times(gT, "W1", "prod1_done", chains_split(0))
            x_transposes(1)
            chains(1, cts)

            def bank_read(half, t):
                pe.wait_ge(S["chain_lo"], t + (NT + 1))
                pe.wait_ge(S["chain_hi"], t + (NT + 1))
                pe.wait_ge(S["xT_in2"], NT)
            times(xTs, "wc", "alpha_done", bank_read)

            def alpha_read(half, t):
                chains_split(1)(half, t)
                pe.wait_ge(S["alpha_in"], t + 1)
            times(gT, "wn", "prod2_done", alpha_read)
            x_transposes(2)
            pe.wait_ge(S["xT_in2"], 2 * NT)
            pe.wait_ge(S["wa_lo"], 1)
            for half in range(2):
                ins = three(ps[0:VCOL + H, half, :], lambda k: [wa[:, v, k, :] for v in range(2)],
                            lambda k: [xTs[:, v, k, half * HALF:(half + 1) * HALF] for v in range(2)])
            ins.then_inc(S["uv_done"], 1)
            with pe.Fori(2, NT) as t:
                three(ps[:, t, :], lambda k: [xTs[:, v, k, bass.ds(t * P, P)] for v in range(2)],
                      lambda k: [ws[:, SLOT["W3"], v, k, :] for v in range(2)]).then_inc(S["wx_done"], 1)
            pe.wait_ge(S["uv_in"], 2)
            for j in range(NT):
                ins = pe.transpose(ps[:, 0, j * H:(j + 1) * H], vrow[:, j * P:(j + 1) * P], id32[0:H, 0:H])
            ins.then_inc(S["v_done"], 1)
            for t in (1, 0):
                if t == 0:
                    pe.wait_ge(S["vc_ready"], 2)
                three(ps[:, t, :], lambda k: [xTs[:, v, k, t * P:(t + 1) * P] for v in range(2)],
                      lambda k: [ws[:, SLOT["W3"], v, k, :] for v in range(2)]).then_inc(S["wx_done"], 1)

            def u_spread(h):
                for a in range(4):
                    for v in range(2):
                        ins = mm(ps[:, a, :], sel[:, h, :], us[:, v, a // 2, a % 2 * HALF:(a % 2 + 1) * HALF],
                                 start=v == 0, stop=v == 1)
                ins.then_inc(S["u_done"], 1)

            def back(h):
                pe.wait_ge(S["oT_in"], h + 1)
                pe.wait_ge(S["back_free"], h + 1)
                for t in range(NT):
                    ins = pe.transpose(ps[:, 6 + t // 4, t % 4 * (DH + 1):(t % 4 + 1) * (DH + 1)],
                                       oT[:, t * P:(t + 1) * P], id32[0:DH + 1, 0:DH + 1])
                ins.then_inc(S["back_done"], 1)

            pe.wait_ge(S["us_lo"], 1)
            pe.wait_ge(S["wx_in"], NT)
            u_spread(0)
            with pe.Fori(0, H // 2) as hp:
                for q in range(2):
                    h = hp * 2 + q
                    pe.wait_ge(S["wxh_ready"], h + 1)
                    for j in range(NT):
                        pe.wait_ge(S["p_ready"], h * NT + (j + 3))
                        for half in range(2):
                            ins = mm(ps[0:DH + 1, 4 + half, :], wxh[:, q, j, :], PR[:, j % 2, half * HALF:(half + 1) * HALF],
                                     start=j == 0, stop=j == NT - 1)
                        ins.then_inc(S["p_free"], 1)
                        if j == 2:
                            pe.wait_ge(S["ub_ready"], h + 1)
                            u_spread(h + 1)
                    back(h)

        @block.vector
        def _(dve):
            stt, ts, tt = dve.scalar_tensor_tensor, dve.tensor_scalar, dve.tensor_tensor
            dve.sem_inc(S["win_free"], 2)
            dve.sem_inc(S["p_ready"], 2)
            dve.sem_inc(S["back_free"], 1)
            links = [0]

            def link(ins):
                links[0] += 1
                ins.then_inc(S["link"], 1)
                dve.wait_ge(S["link"], links[0])

            dve.memset(c32[:, 0:NT // 2, :], 0.0).then_inc(S["c32z"], 1)
            dve.memset(key[:, :, NG:NG + 1], -1.0).then_inc(S["key_in"], 1)
            dve.memset(base_i[:, NG:NG + 1], 0).then_inc(S["key_in"], 1)
            dve.wait_ge(S["edges"], 32)
            ts(i_hi, e_src, 7, None, ALU.arith_shift_right).then_inc(S["ints"], 1)
            ts(i_lo, e_src, P - 1, None, ALU.bitwise_and).then_inc(S["ints"], 1)
            link(dve.tensor_copy(f_dst, e_dst))
            dve.wait_ge(S["ints"], 2)
            dve.tensor_copy(f_lo, i_lo).then_inc(S["idx"], 1)
            dve.tensor_copy(f_hi, i_hi).then_inc(S["ints"], 1)
            link(dve.tensor_reduce(base[:, 1:2], f_dst, AX, ALU.min))
            link(ts(base[:, 0:1], base[:, 1:2], float(N - WIN), None, ALU.min))
            link(ts(f_rel, f_dst, base[:, 0:1], None, ALU.subtract))
            ts(f_bad, f_rel, float(WIN), None, ALU.is_ge).then_inc(S["ints"], 1)
            dve.wait_ge(S["ints"], 4)
            link(stt(f_hi, f_hi, float(WIN), f_rel, ALU.mult, ALU.add))
            stt(f_key, f_bad, 1000.0, f_hi, ALU.mult, ALU.add).then_inc(S["idx"], 1)
            dve.wait_ge(S["tr"], 1)
            dve.tensor_copy(slo[:], ps[:, 2, 0:E // P].rearrange("p (c g) -> p c g", c=NC)).then_inc(S["key_in"], 1)
            dve.tensor_copy(key[:, :, 0:NG], ps[:, 3, 0:E // P].rearrange("p (c g) -> p c g", c=NC)).then_inc(S["key_in"], 1)
            dve.tensor_copy(base_i[:, 0:NG], ps[0:1, 4, 0:NG]).then_inc(S["key_in"], 1)
            dve.wait_ge(S["key_in"], 5)
            dve.wait_ge(S["const_ready"], 11)
            dve.wait_ge(S["c32z"], 2)

            def key_hot(g, i):
                dve.wait_ge(S["hot_free"], g + 1)
                for c in range(NC):
                    ts(oh_key[:, i % 2 * NC + c, :], iota_key[:], key[:, c, bass.ds(g, 1)], None,
                       ALU.is_equal).then_inc(S["key_ready"], 1)

            def add_window(g, i):
                first = dve.value_load(base_i[0:1, bass.ds(g, 1)], min_val=0, max_val=N - WIN)
                dve.wait_ge(S["hot_free"], g + 3)
                dve.wait_ge(S["win_free"], g + 2)
                c = c32[:, :, bass.ds(first, WIN)]
                tt(c, c, ps[:, i % 2, 0:KEYS].rearrange("p (a w) -> p a w", w=WIN), ALU.add).then_inc(S["win_free"], 1)

            key_hot(0, 0)
            with dve.Fori(0, NT) as t:
                for i in range(NT):
                    g = t * NT + i
                    key_hot(g + 1, i + 1)
                    add_window(g, i)

            dve.wait_ge(S["wa_done"], 1)
            link(ts(abT[:], ps[:, 3, 0:256].rearrange("p (k c) -> p k c", c=64)[:, :, 0:VCOL + H], WSCALE, None, ALU.mult))
            link(dve.tensor_copy(wa[:, 0], abT[:]))
            tt(wa[:, 1], abT[:], wa[:, 0], ALU.subtract).then_inc(S["wa_lo"], 1)
            tt(crow[:, 0:1], ps[0:H, 3, 256:257], abc[:], ALU.add).then_inc(S["crow_r"], 1)

            with dve.Fori(0, NT) as t:
                dve.wait_ge(S["cts_ready"], t + 1)
                tt(adj[:, t, :], cts[:, t, :], cst[:, t, :], ALU.add).then_inc(S["adj_a"], 1)
                dve.wait_ge(S["adj_a"], t * 2 + 1)
                ts(adj[:, t, :], adj[:, t, :], 1.0, None, ALU.min).then_inc(S["adj_a"], 1)
                dve.wait_ge(S["adj_a"], t * 2 + 2)
                diag = adj[:, t, bass.ds(t * P, P)]
                tt(diag, diag, id16[:], ALU.add).then_inc(S["adj_ready"], 1)
            link(ts(cnt1[:], cnt[:], 1.0, None, ALU.max))
            link(dve.reciprocal(gsc[:], cnt1[:]))
            link(ts(gsc[:], gsc[:], 1 / (WSCALE * ASCALE), None, ALU.mult))
            link(dve.reciprocal(nan[:], cnt[:]))
            link(ts(nan[:], nan[:], 0.0, None, ALU.mult))
            dve.wait_ge(S["deg_done"], 1)
            link(ts(deg[:], ps[:, 0, 0:NT], 1.0, None, ALU.max))
            dve.reciprocal(invdeg[:], deg[:]).then_inc(S["inv_r"], 1)
            dve.wait_ge(S["inv_r"], 1)
            dve.wait_ge(S["small_in"], SMALL)
            for k in range(STEPS):
                ts(winv[:, k, :], invdeg[:], dwb[:, k + 1:k + 2], None, ALU.mult).then_inc(S["winv_r"], 1)
            dve.wait_ge(S["winv_r"], STEPS)
            dve.wait_ge(S["acc0"], NT + 1)
            dve.wait_ge(S["h_lo"], NT)

            def normalise(layer, t, i):
                dve.wait_ge(S["std_ready"], t + (layer * NT + 1))
                dve.reciprocal(rstd[:, bass.ds(t, 1)], std[:, bass.ds(t, 1)]).then_inc(S["rstd_ready"], 1)
                dve.wait_ge(S["rstd_ready"], t + (layer * NT + 1))
                r = rstd[:, bass.ds(t, 1)]
                if layer == 3:
                    tt(r, r, nan[:, bass.ds(t, 1)], ALU.add).then_inc(S["nan_r"], 1)
                    dve.wait_ge(S["nan_r"], t + 1)
                ts(xcur[:, t, :], xcur[:, t, :], mv[:, i, 0:1], r, ALU.subtract, ALU.mult).then_inc(S["x_ready"], 1)

            def moments(layer, t, i):
                dve.drain()
                dve.bn_stats(st[:, i, :], xcur[:, t, :]).then_inc(S["st_a"], 1)
                dve.drain()
                dve.bn_aggr(mv[:, i, :], st[:, i, :]).then_inc(S["moments"], 1)

            def norm_loop(layer, total):
                total(0)
                moments(layer, 0, 0)
                with dve.Fori(0, NT // 2 - 1) as r:
                    for i in (1, 0):
                        t = r * 2 + (2 - i)
                        total(t)
                        moments(layer, t, i)
                        normalise(layer, t - 1, 1 - i)
                total(NT - 1)
                moments(layer, NT - 1, 1)
                normalise(layer, NT - 2, 0)
                normalise(layer, NT - 1, 1)

            for k in range(1, STEPS):
                with dve.Fori(0, NT) as t:
                    n = t + ((k - 1) * NT + 1)
                    dve.wait_ge(S["step_hi"], n)
                    stt(cur[:, k % 2, 1, t, :], ps[:, t, :], invdeg[:, bass.ds(t, 1)], cur[:, k % 2, 0, t, :],
                        ALU.mult, ALU.subtract).then_inc(S["step_lo"], 1)
                    stt(acc[:, t, :], ps[:, t, :], winv[:, k - 1, bass.ds(t, 1)], acc[:, t, :],
                        ALU.mult, ALU.add).then_inc(S["acc_r"], 1)

            def total0(t):
                dve.wait_ge(S["step_done"], t + ((STEPS - 1) * NT + 1))
                stt(acc[:, t, :], ps[:, t, :], winv[:, STEPS - 1, bass.ds(t, 1)], acc[:, t, :],
                    ALU.mult, ALU.add).then_inc(S["acc_r"], 1)
                dve.wait_ge(S["acc_r"], t + ((STEPS - 1) * NT + 1))
                stt(xcur[:, t, :], acc[:, t, :], 0.0, xcur[:, t, :], ALU.max, ALU.add).then_inc(S["y_ready"], 1)
            dve.wait_ge(S["x_in"], 16)
            norm_loop(0, total0)

            def chains_lo(n):
                with dve.Fori(0, 2) as half:
                    with dve.Fori(0, KT) as k:
                        c = half * KT + k
                        dve.wait_ge(S["chain_hi"], c + (n * NT + 1))
                        cols = bass.ds(half * HALF, HALF)
                        stt(gT[:, 1, k, cols], ps[:, c, :], ASCALE, gT[:, 0, k, cols],
                            ALU.mult, ALU.subtract).then_inc(S["chain_lo"], 1)

            def total1(t):
                dve.wait_ge(S["prod1_done"], t + 1)
                dve.wait_ge(S["xb_ready"], t + 1)
                stt(xcur[:, t, :], ps[:, t, :], 1 / (WSCALE * ASCALE), xcur[:, t, :],
                    ALU.mult, ALU.add).then_inc(S["y_ready"], 1)
            chains_lo(0)
            norm_loop(1, total1)

            def total2(t):
                dve.wait_ge(S["prod2_done"], t + 1)
                stt(xcur[:, t, :], ps[:, t, :], gsc[:, bass.ds(t, 1)], xcur[:, t, :],
                    ALU.mult, ALU.add).then_inc(S["y_ready"], 1)
            chains_lo(1)
            with dve.Fori(0, NT) as t:
                dve.wait_ge(S["alpha_done"], t + 1)
                dve.wait_ge(S["xb_ready"], t + (NT + 1))
                stt(xcur[:, t, :], ps[:, t, :], 1 / WSCALE, xcur[:, t, :],
                    ALU.mult, ALU.add).then_inc(S["alpha_in"], 1)
            dve.wait_ge(S["alpha_in"], NT)
            norm_loop(2, total2)

            uv = ps[:, 0:2, :].rearrange("p a n -> p (a n)")
            dve.wait_ge(S["uv_done"], 1)
            ts(z0, uv[0:H], 1 / WSCALE, crow[:, 0:1], ALU.mult, ALU.add).then_inc(S["uv_in"], 1)
            ts(vrow, uv[VCOL:VCOL + H], 1 / WSCALE, None, ALU.mult).then_inc(S["uv_in"], 1)
            dve.wait_ge(S["uv_in"], 2)
            link(dve.tensor_reduce(crow[:, 1:2], vrow, AX, ALU.max))
            link(ts(zrow, z0, crow[:, 1:2], None, ALU.add))
            link(stt(mrow, zrow, SLOPE, zrow, ALU.mult, ALU.max))
            tt(urow[:, 0, :], z0, mrow, ALU.subtract).then_inc(S["ints"], 1)
            stt(urow[:, 1, :], z0, SLOPE, mrow, ALU.mult, ALU.subtract).then_inc(S["ints"], 1)
            dve.wait_ge(S["ints"], 6)
            link(dve.tensor_copy(us[:, 0], urow))
            tt(us[:, 1], urow, us[:, 0], ALU.subtract).then_inc(S["us_lo"], 1)
            dve.wait_ge(S["v_done"], 1)
            for i, f in enumerate((1 - SLOPE, SLOPE)):
                ts(vc[:, i, :], ps[:, 0, 0:NT * H], f, None, ALU.mult).then_inc(S["vc_ready"], 1)

            def wx_evict(t):
                stt(wx[:, t, :], ps[:, t, :], 1 / WSCALE, bb[:, 2, :], ALU.mult, ALU.add).then_inc(S["wx_in"], 1)
            with dve.Fori(2, NT) as t:
                dve.wait_ge(S["wx_done"], t - 1)
                wx_evict(t)
            for t in (1, 0):
                dve.wait_ge(S["wx_done"], NT - t)
                wx_evict(t)
            dve.wait_ge(S["us_lo"], 1)
            dve.wait_ge(S["vc_ready"], 2)

            def scores(h, q, j):
                if j == 0:
                    dve.wait_ge(S["ub_ready"], h + 1)
                dve.wait_ge(S["e_ready"], h * NT + (j + 1))
                stt(T[:, j % 2, :], ub[:, q, 0, :], vc[:, 0, bass.ds(j * H + h, 1)], ub[:, q, 1, :],
                    ALU.add, ALU.max).then_inc(S["t_ready"], 1)

            def weights(h, j):
                n = h * NT + j
                dve.wait_ge(S["e_ready"], n + 3)
                dve.wait_ge(S["p_free"], n + 1)
                stt(PR[:, j % 2, :], EX[:, j % 2, :], 2.0, c32[:, j, :], ALU.min, ALU.mult).then_inc(S["p_ready"], 1)

            def head_out(h):
                o = ps[:, 6:8, 0:4 * (DH + 1)].rearrange("p a (b d) -> p a b d", b=4)
                dve.wait_ge(S["back_done"], h + 3)
                ts(rden[:], o[:, :, :, DH], 1e-37, None, ALU.max).then_inc(S["rd_r"], 1)
                dve.wait_ge(S["rd_r"], h * 2 + 1)
                dve.reciprocal(rden[:], rden[:]).then_inc(S["rd_r"], 1)
                dve.wait_ge(S["rd_r"], h * 2 + 2)
                tt(att.rearrange("p (a b) d -> p a b d", a=2), o[:, :, :, 0:DH],
                   rden[:].unsqueeze(3).broadcast_to([P, 2, 4, DH]), ALU.mult).then_inc(S["back_free"], 1)
                dve.wait_ge(S["back_free"], h + 2)
                xs = xcur[:, :, bass.ds(h * DH, DH)]
                tt(xs, xs, att, ALU.add).then_inc(S["att_added"], 1)

            scores(0, 0, 0)
            with dve.Fori(0, H // 2) as hp:
                for q in range(2):
                    h = hp * 2 + q
                    for j in range(NT):
                        if j < NT - 1:
                            scores(h, q, j + 1)
                        else:
                            scores(h + 1, 1 - q, 0)
                        weights(h, j)
                    head_out(h)
            dve.wait_ge(S["att_added"], H)
            norm_loop(3, lambda t: dve.sem_inc(S["y_ready"], 1))


def kernel(**inputs):
    import numpy as np
    import concourse.bacc as bacc
    from concourse.bass_utils import run_bass_kernel_spmd

    g = {k: np.asarray(v) for k, v in inputs.items()}
    laid = {
        "x": g["x"], "xT": g["x"].T, "src": g["src"], "dst": g["dst"],
        "W0": g["L0_gnn_W"], "b0": g["L0_gnn_b"], "dw": g["L0_gnn_diffusion_weights"],
        "W1T": g["L1_gnn_W"].T, "b1": g["L1_gnn_b"],
        "wc": g["L2_gnn_wc"], "wn": g["L2_gnn_wn"], "b2": g["L2_gnn_bias"],
        "W3": g["L3_gnn_Ws"].transpose(1, 0, 2).reshape(D, D),
        "W3T": g["L3_gnn_Ws"].transpose(0, 2, 1).reshape(D, D),
        "b3": g["L3_gnn_Wb"].reshape(D), "b3T": g["L3_gnn_Wb"].reshape(KT, P).T, "aw": g["L3_gnn_a_w"], "ab": g["L3_gnn_a_b"],
    }
    laid = {k: np.ascontiguousarray(v) for k, v in laid.items()}
    nc = bacc.Bacc("TRN2", target_bir_lowering=False, num_devices=1)
    aps = {k: nc.dram_tensor(f"in_{k}", v.shape, mybir.dt.from_np(v.dtype), kind="ExternalInput").ap()
           for k, v in laid.items()}
    out = nc.dram_tensor("out", (N, D), F32, kind="ExternalOutput").ap()
    build(nc, **aps, out=out)
    r = run_bass_kernel_spmd(nc, [{f"in_{k}": v for k, v in laid.items()}], core_ids=[0])
    return r.results[0]["out"]
```

```python
from contextlib import ExitStack

import concourse.bass as bass
from concourse import mybir
from concourse.alu_op_type import AluOpType as ALU

F32 = mybir.dt.float32
F16 = mybir.dt.float16
I32 = mybir.dt.int32
ACT = mybir.ActivationFunctionType
AX = mybir.AxisListType.X

P = 128
N = 1024
D = 512
E = 16384
NT = N // P
KT = D // P
HALF = 512
H = 8
DH = D // H
STEPS = 3
EPS = 1e-5
SLOPE = 0.2

GROUP = 256
NG = E // GROUP
NC = GROUP // P
WIN = 48
KEYS = NT * WIN

WSCALE = 64.0
ASCALE = 1.0 / 32
EXACT = 2048.0
YW = 2 * (DH + 1)
OS = 9
VMAX, UMAX, WXMAX = 3.5, 20.0, 120.0
LN16 = 2.772588722239781
HT = NT // 2 - 1
VCOL = 32


def build(nc, x, xT, src, dst, W0, b0, dw, W1T, b1, wc, wn, b2, W3, W3T, b3, b3T, aw, ab, out):
    with ExitStack() as ctx:
        def sb(name, shape, dt):
            return ctx.enter_context(nc.sbuf_tensor(name, shape, dt))

        def sem(name):
            return ctx.enter_context(nc.semaphore(name))

        ps = ctx.enter_context(nc.psum_tensor("ps", [P, NT, HALF], F32))

        c32 = sb("c32", [P, NT, N], F32)
        cst = sb("cst", [P, NT, N], F16)
        cts = sb("cts", [P, NT, N], F16)
        adj = sb("adj", [P, NT, N], F16)
        xcur = sb("xcur", [P, NT, D], F32)
        acc = sb("acc", [P, NT, D], F32)
        xTraw = acc[:].rearrange("p a b -> p (a b)").rearrange("p (k n) -> p k n", k=KT)
        ub = acc[:].rearrange("p a b -> p (a b)").rearrange("p (q v n) -> p q v n", q=2, v=2)
        xTs = sb("xTs", [P, 2, KT, N], F16)
        big = sb("big", [P, 4 * 2 * KT * D + 4 * NT * D], F16)
        WS = 4 * 2 * KT * D
        ws = big[:, 0:WS].rearrange("p (s v k n) -> p s v k n", s=4, v=2, k=KT)
        cur = big[:, WS:].rearrange("p (s v a b) -> p s v a b", s=2, v=2, a=NT)
        spare = cur[:, 1, 1].rearrange("p a b -> p (a b)").bitcast(F32)
        w0raw = cur[:, 1, 0].rearrange("p a b -> p (a b)").bitcast(F32).rearrange("p (k n) -> p k n", k=KT)
        stage = xTs[:].rearrange("p v k n -> p (v k n)").bitcast(F32).rearrange(
            "p (s k n) -> p s k n", s=2, k=KT)
        tep = cur.rearrange("p s v a b -> p (s v a b)").bitcast(F32).rearrange(
            "p (f n) -> p f n", n=N)
        wx = cts[:].rearrange("p a b -> p (a b)").bitcast(F32).rearrange("p (a b) -> p a b", a=NT)
        SLOT = {"W0": 0, "W1": 1, "wc": 2, "wn": 3, "W3": 0}

        c_left = adj
        ct_left = acc[:].rearrange("p a b -> p (a b)").bitcast(F16).rearrange("p (a n) -> p a n", a=NT)

        y0 = 2 * KT * D
        yh = big[:, y0:y0 + NT * 2 * H * YW].rearrange("p (t v h n) -> p t v h n", t=NT, v=2, h=H)
        yf = acc[:].rearrange("p a b -> p (a b)")[:, 0:2 * H * YW].rearrange(
            "p (q h e d) -> p q h e d", q=2, h=H, e=2)
        cz = (adj, ct_left)
        xflat = xTs[:].rearrange("p v k n -> p (v k n)").bitcast(F32)
        uf = xflat[:, 0:2 * N].rearrange("p (q n) -> p q n", q=2)
        OW = OS * (DH + 1)
        comb = xflat[:, 2 * N:2 * N + 2 * OW].rearrange("p (q t d) -> p q t d", q=2, t=OS)
        attf = xflat[:, 2 * N + 2 * OW:2 * N + 2 * OW + D].rearrange("p (t d) -> p t d", d=DH)

        iota_lo = sb("iota_lo", [P, P], F16)
        iota_key = sb("iota_key", [P, KEYS], F16)
        id32 = sb("id32", [P, P], F32)
        id16 = sb("id16", [P, P], F16)
        ones16 = sb("ones16", [P, P], F16)
        sel = sb("sel", [H, H + 1, P], F16)
        epsc = sb("epsc", [P, 1], F32)

        cflat = cst[:].rearrange("p a b -> p (a b)")
        oh_end = 2 * NC * (P + KEYS)
        oh_lo = cflat[:, NT * N - oh_end:NT * N - 2 * NC * KEYS].rearrange("p (b n) -> p b n", n=P)
        oh_lo1 = cflat[:, 2 * N:3 * N].rearrange("p (b n) -> p b n", n=P)
        oh_key = cflat[:, NT * N - 2 * NC * KEYS:NT * N].rearrange("p (b n) -> p b n", n=KEYS)
        tmp = cst[0:NG].rearrange("p a b -> p (a b)").bitcast(F32).rearrange("p (f e) -> p f e", e=GROUP)
        tmpi = cst[0:NG].rearrange("p a b -> p (a b)").bitcast(I32).rearrange("p (f e) -> p f e", e=GROUP)
        e_dst, e_src, i_hi, i_lo = (tmpi[:, i, :] for i in range(4))
        f_dst, f_hi, f_lo, f_rel, f_key, f_bad, f_far = (tmp[:, i, :] for i in range(4, 11))
        base = sb("base", [NG, 2], F32)
        base_i = sb("base_i", [1, NG], I32)
        slo = sb("slo", [P, NC, NG + 1], F32)
        slo_g = sb("slo_g", [P, NT], F32)
        key = sb("key", [P, NC, NG + 1], F32)
        far = spare[:, 3 * D:3 * D + NC * (NG + 1)].rearrange(
            "p (c g) -> p c g", c=NC)
        far_at = sb("far_at", [P, 2], F32)
        flags = sb("flags", [1, 4], I32)
        f_flag = sb("f_flag", [1, 2], F32)
        iota_n = cflat[:, 0:N]
        oh_far = cflat[:, N:2 * N]

        b0f = spare[0:1, D:2 * D]
        b0s = spare[0:1, 2 * D:3 * D].bitcast(F16).rearrange("p (v d) -> p v d", v=2)
        bb = sb("bb", [P, 3, D], F32)
        dwb = sb("dwb", [P, STEPS + 1], F32)
        hb = spare[:, 0:D]
        deg = sb("deg", [P, NT], F32)
        invdeg = sb("invdeg", [P, NT], F32)
        winv = sb("winv", [P, STEPS, NT], F32)
        cnt = sb("cnt", [P, NT], F32)
        cnt1 = sb("cnt1", [P, NT], F32)
        gsc = sb("gsc", [P, NT], F32)
        nan = sb("nan", [P, NT], F32)
        st = sb("st", [P, 2, 6], F32)
        mv = sb("mv", [P, 2, 2], F32)
        std = sb("std", [P, NT], F32)
        rstd = sb("rstd", [P, NT], F32)
        nmr = sb("nmr", [P, NT], F32)
        abT = sb("abT", [P, KT, VCOL + H], F32)
        wa = sb("wa", [P, 2, KT, VCOL + H], F16)
        wbc = sb("wbc", [P, KT], F32)
        abc = sb("abc", [H, 1], F32)
        crow = sb("crow", [H, 3], F32)
        vc = sb("vc", [P, 2, NT * H], F32)
        wxh = xTs[:].rearrange("p v k n -> p (v k n)").bitcast(F32)[:, 0:2 * NT * (DH + 1)].rearrange(
            "p (q t d) -> p q t d", q=2, t=NT)
        rden = sb("rden", [P, 2, 4], F32)
        nv = sb("nv", [P, NT, H], F32)
        qc = sb("qc", [P, H, OS], F32)
        rdf = sb("rdf", [P, 2, OS], F32)
        ln16 = sb("ln16", [P, 1], F32)
        st8 = sb("st8", [P, NT, 6], F32)
        mv8 = sb("mv8", [P, NT, 2], F32)
        mcol = sb("mcol", [P, NT, H], F32)
        wm = sb("wm", [P, NT], F32)
        lim = sb("lim", [P, 4], F32)
        rows = tep[0:H]
        zrow, mrow, _, _, z0, vrow, qrow = (rows[:, i, :] for i in range(7))
        urow = rows[:, 2:4, :]
        wrow = qrow
        usf = rows[:, 7, :].bitcast(F16).rearrange("p (v n) -> p v n", v=2)
        seen, most = tep[:, 2, :], tep[:, 3, :]
        us = adj[0:H].rearrange("p a b -> p (a b)")[:, 0:4 * N].rearrange(
            "p (v a n) -> p v a n", v=2, a=2)
        T, EX, PR = (tep[:, 2 * i:2 * i + 2, :] for i in range(3))
        oT = tep[0:DH + 1, 6, :]
        att = tep[:, 7, 0:HALF].rearrange("p (t d) -> p t d", d=DH)

        class Semaphores(dict):
            def __missing__(self, name):
                self[name] = sem(name)
                return self[name]

        S = Semaphores()

        def settle(pool):
            pool.wait_ge(S["const_ready"], 12)

        def flag(engine, i):
            return engine.value_load(flags[0:1, i:i + 1], min_val=0, max_val=1) > 0

        def bank16(t):
            return ps[:, t, :].bitcast(F16)

        block = ctx.enter_context(nc.Block())

        @block.sync
        def _(sp):
            sp.dma_start(e_dst, dst.rearrange("(g e) -> g e", e=GROUP)).then_inc(S["edges"], 16)
            sp.dma_start(e_src, src.rearrange("(g e) -> g e", e=GROUP)).then_inc(S["edges"], 16)
            sp.dma_start(xTraw, xT.rearrange("(k p) n -> p k n", p=P)).then_inc(S["xT_in"], 16)
            sp.dma_start(w0raw, W0.rearrange("(k p) n -> p k n", p=P)).then_inc(S["w_in0"], 16)
            sp.dma_start(b0f, b0.rearrange("(a d) -> a d", a=1)).then_inc(S["small_in"], 16)
            sp.dma_start(dwb[:], dw.rearrange("(a d) -> a d", a=1).broadcast_to([P, STEPS + 1])).then_inc(S["small_in"], 16)
            sp.dma_start(xcur[:], x.rearrange("(t p) d -> p t d", p=P)).then_inc(S["x_in"], 16)
            for i, b in enumerate((b1, b2, b3)):
                sp.dma_start(bb[:, i, :], b.rearrange("(a d) -> a d", a=1).broadcast_to([P, D])).then_inc(S["small_in"], 16)
            sp.dma_start(wbc[:], b3T).then_inc(S["small_in"], 16)
            sp.dma_start(abc[:], ab.rearrange("(h a) -> h a", a=1)).then_inc(S["small_in"], 16)
            sp.wait_ge(S["const_ready"], 9)
            step = VCOL + H + 2
            flat = abT[:].rearrange("p k c -> p (k c)")
            for q in range(2):
                for u in range(2):
                    c0 = VCOL * u + q
                    sp.dma_start(flat[q * DH:(q + 1) * DH, c0:c0 + 3 * step + 1:step],
                                 aw.rearrange("(j q) (u p) -> q u p j", q=2, p=DH)[q, u],
                                 allow_slow_non_contiguous=True).then_inc(S["small_in"], 16)
            sp.wait_ge(S["h_done"], NT)
            for n, w in enumerate((W1T, wc, wn, W3, W3T)):
                if n >= 2:
                    sp.wait_ge(S["w_lo"], n)
                sp.dma_start(stage[:, n % 2], w.rearrange("(k p) n -> p k n", p=P)).then_inc(S[f"w_in{n + 1}"], 16)
            for t in range(NT):
                sp.wait_ge(S["out_odd" if t % 2 else "out_even"], t // 2 + 1)
                sp.dma_start(out.rearrange("(t p) d -> t p d", p=P)[t], xcur[:, t, :]).then_inc(S["out_done"], 16)
            sp.wait_ge(S["out_done"], 16 * NT)
        SMALL = 16 * 11

        @block.gpsimd
        def _(pool):
            pool.iota(iota_lo[:], [[1, P]], base=0, channel_multiplier=0,
                      allow_small_or_imprecise_dtypes=True).then_inc(S["const_ready"], 1)
            pool.iota(iota_key[:], [[1, KEYS]], base=0, channel_multiplier=0,
                      allow_small_or_imprecise_dtypes=True).then_inc(S["const_ready"], 1)
            pool.memset(id32[:], 0.0).then_inc(S["const_ready"], 1)
            pool.memset(id16[:], 0.0).then_inc(S["const_ready"], 1)
            pool.memset(sel[:], 0.0).then_inc(S["const_ready"], 1)
            pool.memset(ones16[:], 1.0).then_inc(S["const_ready"], 1)
            pool.memset(epsc[:], EPS).then_inc(S["const_ready"], 1)
            pool.memset(ln16[:], LN16).then_inc(S["const_ready"], 1)
            pool.memset(abT[:], 0.0).then_inc(S["const_ready"], 1)
            pool.wait_ge(S["const_ready"], 9)
            for ident in (id32, id16):
                pool.affine_select(out=ident[:], in_=ident[:], compare_op=ALU.not_equal, fill=1.0, base=0,
                                   pattern=[[-1, P]], channel_multiplier=1).then_inc(S["const_ready"], 1)
            pool.affine_select(out=sel[:], in_=sel[:], compare_op=ALU.not_equal, fill=1.0, base=0,
                               pattern=[[-1, H + 1], [0, P]], channel_multiplier=1).then_inc(S["const_ready"], 1)
            pool.memset(c32[:, NT // 2:NT, :], 0.0).then_inc(S["c32z"], 1)

            def split_lo(n, name, raw):
                pool.wait_ge(S["w_hi"], n + 1)
                pool.tensor_tensor(ws[:, SLOT[name], 1], raw, ws[:, SLOT[name], 0], ALU.subtract).then_inc(S["w_lo"], 1)

            def source_hots(t):
                for half in range(0, NT, NT // 2):
                    part = slice(half, half + NT // 2)
                    if not (isinstance(t, int) and t == 0):
                        pool.wait_ge(S["hot_free"], t * NT + (half - 2))
                    pool.tensor_copy(slo_g[:, part], slo[:, 1, bass.ds(t * NT + half, NT // 2)]).then_inc(S["slo_g"], 1)
                    pool.drain()
                    for i in range(half, half + NT // 2):
                        pool.tensor_scalar(oh_lo1[:, i, :], iota_lo[:], slo_g[:, i:i + 1], None,
                                           ALU.is_equal).then_inc(S["lo_ready"], 1)

            def h_lower(t):
                pool.wait_ge(S["h_cp"], t + 2)
                settle(pool)
                pool.tensor_tensor(cur[:, 0, 1, t, :], hb, cur[:, 0, 0, t, :],
                                   ALU.subtract).then_inc(S["h_lo"], 1)

            pool.wait_ge(S["key_in"], 5)
            source_hots(0)
            pool.wait_ge(S["xT_hi"], 1)
            pool.tensor_tensor(xTs[:, 1, 0:KT // 2], xTraw[:, 0:KT // 2], xTs[:, 0, 0:KT // 2], ALU.subtract).then_inc(S["xT_lo"], 1)
            split_lo(0, "W0", w0raw)
            pool.wait_ge(S["b0_ready"], 2)
            pool.tensor_tensor(b0s[:, 1, :], b0f, b0s[:, 0, :], ALU.subtract).then_inc(S["b0_ready"], 1)
            source_hots(1)
            source_hots(2)
            with pool.Fori(1, HT) as r:
                h_lower(r - 1)
                source_hots(r * 2 + 1)
                source_hots(r * 2 + 2)
            h_lower(HT - 1)
            source_hots(NT - 1)
            with pool.Fori(HT, NT) as t:
                h_lower(t)
            for n, name in enumerate(("W1", "wc", "wn", "W3")):
                split_lo(n + 1, name, stage[:, n % 2])

            for layer in range(3):
                with pool.Fori(0, NT) as t:
                    pool.wait_ge(S["x_ready"], t + (layer * NT + 1))
                    settle(pool)
                    pool.tensor_tensor(cur[:, 1, 1, t, :], xcur[:, t, :], cur[:, 1, 0, t, :],
                                       ALU.subtract).then_inc(S["x_lo"], 1)
                    if layer < 2:
                        pool.tensor_tensor(xcur[:, t, :], xcur[:, t, :], bb[:, layer, :],
                                           ALU.add).then_inc(S["xb_ready"], 1)
                if layer == 1:
                    pool.wait_ge(S["gather1_done"], NT)
                    for t in range(NT):
                        pool.tensor_scalar(cst[:, t, :], cst[:, t, :], -1.0, None, ALU.mult).then_inc(S["neg_ready"], 1)
            with pool.Fori(0, NT // 2) as r:
                for i in range(2):
                    t = r * 2 + i
                    pool.wait_ge(S["y_hi"], t + 1)
                    settle(pool)
                    pool.tensor_tensor(yh[:, t, 1], yf[:, i].rearrange("p h e d -> p h (e d)"), yh[:, t, 0],
                                       ALU.subtract).then_inc(S["y_lo"], 1)

            pool.wait_ge(S["mode"], 1)
            with pool.If(flag(pool, 2)):
                pool.wait_ge(S["wx_in"], NT + 2)
                pool.memset(wxh[:, :, :, DH:DH + 1], 1.0).then_inc(S["ones_wxh"], 1)
                pool.wait_ge(S["ones_wxh"], 1)
                with pool.Fori(0, H // 2) as hp:
                    for q in range(2):
                        h = hp * 2 + q
                        pool.wait_ge(S["back_done"], h + 1)
                        pool.tensor_copy(wxh[:, q, :, 0:DH], wx[:, :, bass.ds(h * DH, DH)]).then_inc(S["wxh_ready"], 1)
            with pool.Else():
                with pool.Fori(0, H // 2) as hp:
                    for q in range(2):
                        h = hp * 2 + q
                        pool.wait_ge(S["att_in"], h + 2)
                        pool.wait_ge(S["den_ready"], h * 2 + 2)
                        settle(pool)
                        pool.tensor_tensor(attf, comb[:, q, 0:NT, 0:DH],
                                           rdf[:, q, 0:NT].unsqueeze(2).broadcast_to([P, NT, DH]),
                                           ALU.mult).then_inc(S["att_ready"], 1)
                        pool.wait_ge(S["att_ready"], h + 1)
                        settle(pool)
                        xs = xcur[:, :, bass.ds(h * DH, DH)]
                        pool.tensor_tensor(xs, xs, attf, ALU.add).then_inc(S["att_in"], 1)

        @block.scalar
        def _(act):
            def copy(o, i, scale=1.0, **kw):
                return act.activation(o, i, ACT.Copy, scale=scale, **kw)

            act.wait_ge(S["xT_in"], 16)
            copy(xTs[:, 0], xTraw).then_inc(S["xT_hi"], 1)

            def split_hi(n, name, raw):
                act.wait_ge(S[f"w_in{n}"], 16)
                copy(raw, raw, WSCALE).then_inc(S["w64"], 1)
                act.wait_ge(S["w64"], n + 1)
                copy(ws[:, SLOT[name], 0], raw).then_inc(S["w_hi"], 1)
            split_hi(0, "W0", w0raw)
            act.wait_ge(S["small_in"], SMALL)
            copy(b0f, b0f, WSCALE).then_inc(S["b0_ready"], 1)
            act.wait_ge(S["b0_ready"], 1)
            copy(b0s[:, 0, :], b0f).then_inc(S["b0_ready"], 1)
            act.sem_inc(S["h_cp"], 1)
            act.sem_inc(S["h_lo"], 1)

            def h_upper(t, bank):
                act.wait_ge(S["h_done"], t + 1)
                act.wait_ge(S["acc0"], t + 1)
                copy(cur[:, 0, 0, t, :], ps[:, bank, :], 1 / WSCALE).then_inc(S["h_hi"], 1)
                act.wait_ge(S["h_lo"], t + 1)
                copy(hb, ps[:, bank, :], 1 / WSCALE).then_inc(S["h_cp"], 1)
                act.wait_ge(S["h_cp"], t + 2)
                copy(acc[:, t, :], hb, dwb[:, 0:1]).then_inc(S["acc0"], 1)

            with act.Fori(0, HT) as t:
                h_upper(t, 2)
            h_upper(HT, 2)
            act.wait_ge(S["counted"], 1)
            for j in range(3):
                copy(cst[:, j, :], c32[:, j, :]).then_inc(S["cst_ready"], 1)
            for t in range(HT + 1, NT - 2):
                h_upper(t, t - 1)
            for r in range(2):
                for a in range(NT // 2):
                    act.wait_ge(S["ct_done"], r * (NT // 2) + (a + 1))
                    copy(cts[:, r * (NT // 2) + a, :], bank16(a % 2)).then_inc(S["cts_ready"], 1)
                h_upper(r + (NT - 2), r + (NT - 3))

            act.wait_ge(S["inv_r"], 1)
            for k in range(1, STEPS):
                for n in (2 * k - 1, 2 * k):
                    split_hi(n, ("W1", "wc", "wn", "W3")[n - 1], stage[:, (n - 1) % 2])
                with act.Fori(0, NT) as t:
                    act.wait_ge(S["step_done"], t + ((k - 1) * NT + 1))
                    copy(cur[:, k % 2, 0, t, :], ps[:, t, :], invdeg[:, bass.ds(t, 1)]).then_inc(S["step_hi"], 1)

            def norm(layer, t, i):
                n = t + (layer * NT + 1)
                act.wait_ge(S["moments"], n)
                act.activation(std[:, bass.ds(t, 1)], mv[:, i, 1:2], ACT.Sqrt, bias=epsc[:]).then_inc(S["std_ready"], 1)
                act.wait_ge(S["nmr_ready"], n)
                r, b = rstd[:, bass.ds(t, 1)], nmr[:, bass.ds(t, 1)]
                if layer < 3:
                    act.activation(cur[:, 1, 0, t, :], xcur[:, t, :], ACT.Identity, bias=b, scale=r).then_inc(S["x_hi"], 1)
                act.activation(xcur[:, t, :], xcur[:, t, :], ACT.Identity, bias=b, scale=r).then_inc(S["x_ready"], 1)

            def xT_evict(layer, t, i):
                act.wait_ge(S["xT_done"], t + (layer * NT + 1))
                copy(xTs[:, :, :, bass.ds(t * P, P)].rearrange("p v k n -> p (v k) n"),
                     bank16(i).rearrange("p (a n) -> p a n", n=P)).then_inc(S["xT_in2"], 1)

            def z_hi(layer, t, i):
                if layer == 2:
                    act.wait_ge(S["uvc_done"], t + 1)
                    act.wait_ge(S["y_lo"], t + 1)
                    for e, f in enumerate((1.0, SLOPE)):
                        act.activation(yf[:, i, :, e, DH], ps[:, 2 + i, VCOL:VCOL + H], ACT.Exp, scale=f / WSCALE,
                                       bias=ln16[:]).then_inc(S["exp_in"], 1)
                    act.wait_ge(S["y_ready3"], t + 1)
                    copy(yh[:, t, 0], yf[:, i].rearrange("p h e d -> p h (e d)")).then_inc(S["y_hi"], 1)
                else:
                    act.wait_ge(S["z_done"], t + (layer * NT + 1))
                    copy(cur[:, 0, 0, t, :], ps[:, 4 + i, :], 1 / WSCALE).then_inc(S["z_hi"], 1)

            act.activation(std[:, 0:1], epsc[:], ACT.Sqrt).then_inc(S["warm"], 1)
            act.wait_ge(S["warm"], 1)
            for layer in range(3):
                with act.Fori(0, NT // 2 - 1) as r:
                    for i in range(2):
                        norm(layer, r * 2 + i, i)
                if layer == 0:
                    act.wait_ge(S["wa_done"], 1)
                xT_evict(layer, 0, 0)
                norm(layer, NT - 2, 0)
                xT_evict(layer, 1, 1)
                norm(layer, NT - 1, 1)
                if layer == 2:
                    act.activation(std[:, 0:1], epsc[:], ACT.Exp).then_inc(S["warm"], 1)
                    act.wait_ge(S["warm"], 2)
                z_hi(layer, 0, 0)
                with act.Fori(0, NT // 2 - 1) as r:
                    for i in (1, 0):
                        t = r * 2 + (2 - i)
                        xT_evict(layer, t + 1, 1 - i)
                        z_hi(layer, t, i)
                z_hi(layer, NT - 1, 1)

            act.sem_inc(S["e_ready"], 2)
            act.wait_ge(S["uv_in"], 1)
            act.activation(qrow, z0, ACT.Exp, scale=1 - SLOPE).then_inc(S["q_row"], 1)
            act.wait_ge(S["mode"], 1)
            with act.If(flag(act, 2)):
                def u_copy(h, q):
                    act.wait_ge(S["u_done"], h + 1)
                    copy(ub[:, q], ps[:, 0:4, :].rearrange("p (v a) n -> p v (a n)", v=2)).then_inc(S["ub_ready"], 1)

                def exps(h, q, j):
                    n = h * NT + j
                    act.wait_ge(S["t_ready"], n + 1)
                    act.wait_ge(S["p_ready"], n + 1)
                    act.activation(EX[:, j % 2, :], T[:, j % 2, :], ACT.Exp,
                                   bias=vc[:, 1, bass.ds(j * H + h, 1)]).then_inc(S["e_ready"], 1)

                def o_evict(h):
                    act.wait_ge(S["p_free"], h * NT + (NT + 2))
                    act.wait_ge(S["back_done"], h + 2)
                    copy(oT, ps[0:DH + 1, 4:6, :].rearrange("p a n -> p (a n)")).then_inc(S["oT_in"], 1)

                u_copy(0, 0)
                with act.Fori(0, H // 2) as hp:
                    for q in range(2):
                        h = hp * 2 + q
                        for j in range(NT):
                            exps(h, q, j)
                            if j == 3:
                                u_copy(h + 1, 1 - q)
                        o_evict(h)
            with act.Else():
                act.wait_ge(S["wx_done"], NT)
                with act.Fori(0, H // 2) as hp:
                    for q in range(2):
                        h = hp * 2 + q
                        act.wait_ge(S["uf_done"], h + 1)
                        act.wait_ge(S["cz_ready"], h * NT + NT)
                        copy(uf[:, q], ps[:, 0:2, :].rearrange("p a n -> p (a n)")).then_inc(S["uf_ready"], 1)
            act.activation(std[:, 0:1], epsc[:], ACT.Sqrt).then_inc(S["warm"], 1)
            act.wait_ge(S["warm"], 3)
            act.wait_ge(S["mv8_in"], NT)
            act.activation(std[:], mv8[:, :, 1], ACT.Sqrt, bias=epsc[:]).then_inc(S["std8"], 1)
            act.wait_ge(S["scale8"], 1)
            for t in range(0, NT, 2):
                act.activation(xcur[:, t, :], xcur[:, t, :], ACT.Identity, bias=nmr[:, t:t + 1], scale=rstd[:, t:t + 1]).then_inc(S["out_even"], 1)

        @block.tensor
        def _(pe):
            mm = pe.matmul

            def three(bank, lhs, rhs, start=True, stop=True):
                for k in range(KT):
                    for n in range(3):
                        ins = part(bank, lhs, rhs, k, n, start, stop)
                return ins

            def part(bank, lhs, rhs, k, n, start=True, stop=True):
                a, b = ((0, 0), (0, 1), (1, 0))[n]
                return mm(bank, lhs(k)[a], rhs(k)[b], start=start and k == 0 and n == 0,
                          stop=stop and k == KT - 1 and n == 2)

            def cols(buf, t):
                return lambda k: [buf[:, v, k, bass.ds(t * P, P)] for v in range(2)]

            def weight(name):
                return lambda k: [ws[:, SLOT[name], v, k, :] for v in range(2)]

            pe.sem_inc(S["hot_free"], 2)
            pe.sem_inc(S["cts_ready"], 2)
            pe.sem_inc(S["p_free"], 2)
            pe.sem_inc(S["back_done"], 2)
            pe.wait_ge(S["const_ready"], 12)
            pe.wait_ge(S["idx"], 3)
            for c in range(NC):
                pe.transpose(ps[:, 2, c * NG:(c + 1) * NG], f_lo[:, c * P:(c + 1) * P], id32[0:NG, 0:NG])
                pe.transpose(ps[:, 3, c * NG:(c + 1) * NG], f_key[:, c * P:(c + 1) * P], id32[0:NG, 0:NG])
                pe.transpose(ps[:, 5, c * NG:(c + 1) * NG], f_far[:, c * P:(c + 1) * P], id32[0:NG, 0:NG])
            pe.transpose(ps[0:1, 4, NG:2 * NG], far_at[0:NG, 0:1], id32[0:NG, 0:NG])
            pe.transpose(ps[0:1, 4, 0:NG], base[:, 0:1], id32[0:NG, 0:NG]).then_inc(S["tr"], 1)

            pe.wait_ge(S["key_in"], 5)
            xw = [(k, n) for k in range(KT) for n in range(3)]

            def h_part(t, bank, n):
                part(ps[:, bank, :], cols(xTs, t), weight("W0"), *xw[n], stop=False)
                if n == len(xw) - 1:
                    for v in range(2):
                        ins = mm(ps[:, bank, :], ones16[0:1, :], b0s[:, v, :], start=False, stop=v == 1)
                    ins.then_inc(S["h_done"], 1)

            def groups(t, h_tile=None, first=0):
                for i in range(NT):
                    g = t * NT + i
                    pe.wait_ge(S["lo_ready"], g + 1)
                    pe.wait_ge(S["key_ready"], g * (NC + 1) + NC + 1)
                    pe.wait_ge(S["win_free"], g + 1)
                    for c in range(NC):
                        b = i % 2 * NC + c
                        ins = mm(ps[:, i % 2, 0:KEYS], oh_lo1[:, i, :] if c else oh_lo[:, b, :], oh_key[:, b, :], start=c == 0, stop=c == NC - 1)
                    ins.then_inc(S["hot_free"], 1)
                    if h_tile is not None and first + i < len(xw):
                        if first + i == 0:
                            pe.wait_ge(S["h_cp"], h_tile + 1)
                        h_part(h_tile, 2, first + i)

            groups(0)
            pe.wait_ge(S["xT_lo"], 2)
            pe.wait_ge(S["w_lo"], 1)
            pe.wait_ge(S["b0_ready"], 3)
            with pe.Fori(0, HT) as r:
                groups(r * 2 + 1, r)
                groups(r * 2 + 2, r, NT)
            groups(NT - 1, HT)
            for n in range(NT, len(xw)):
                h_part(HT, 2, n)
            for t in range(HT + 1, NT - 2):
                for n in range(len(xw)):
                    h_part(t, t - 1, n)

            pe.wait_ge(S["far_in"], 3)
            with pe.If(flag(pe, 0)):
                pe.wait_ge(S["win_free"], NG + 2)
                pe.wait_ge(S["far_iota"], NT)
                pe.sem_inc(S["far_free"], 1)
                with pe.Fori(0, NT) as a:
                    for b in range(2):
                        mm(ps[:, b, :], sel[:, H, :], iota_n[0:H, 0:HALF], start=True, stop=False)
                    with pe.Fori(0, NC * (NG + 1)) as e:
                        n = a * (NC * (NG + 1)) + e
                        pe.wait_ge(S["far_hot"], n * 2 + 2)
                        for b in range(2):
                            ins = mm(ps[:, b, :], oh_lo[:, 0, :], oh_far[:, b * HALF:(b + 1) * HALF], start=False, stop=False)
                        ins.then_inc(S["far_free"], 1)
                    for b in range(2):
                        ins = mm(ps[:, b, :], sel[:, H, :], iota_n[0:H, 0:HALF], start=False, stop=True)
                    ins.then_inc(S["far_done"], 1)
                    pe.wait_ge(S["far_added"], a * 2 + 2)
            pe.wait_ge(S["cst_ready"], NT)
            pe.wait_ge(S["win_free"], NG + 2)
            with pe.Fori(0, 2) as r:
                for a in range(NT // 2):
                    t = r * (NT // 2) + a
                    pe.wait_ge(S["cts_ready"], t + 1)
                    for j in range(NT):
                        ins = pe.transpose(bank16(a % 2)[:, j * P:(j + 1) * P], cst[:, j, bass.ds(t * P, P)], id16[:])
                    ins.then_inc(S["ct_done"], 1)
                    for n in range(3 * a, 3 * a + 3):
                        h_part(r + (NT - 2), r + (NT - 3), n)
            pe.wait_ge(S["adj_ready"], NT)
            pe.wait_ge(S["cts_ready"], NT + 2)
            for t in range(NT):
                for j in range(NT):
                    ins = mm(ps[:, 7, t:t + 1], adj[:, j, t * P:(t + 1) * P], ones16[:, 0:1],
                             start=j == 0, stop=j == NT - 1)
            ins.then_inc(S["deg_done"], 1)

            pe.wait_ge(S["h_lo"], NT + 1)
            pe.wait_ge(S["h_hi"], NT)
            for k in range(1, STEPS + 1):
                def step(t, first):
                    for j in range(NT):
                        if first and k > 1:
                            pe.wait_ge(S["step_lo"], (k - 2) * NT + j + 1)
                        for v in range(2):
                            ins = mm(ps[:, t, :], adj[:, j, bass.ds(t * P, P)], cur[:, (k - 1) % 2, v, j, :],
                                     start=j == 0 and v == 0, stop=j == NT - 1 and v == 1)
                    ins.then_inc(S["step_done"], 1)
                if k > 1:
                    pe.wait_ge(S["acc_r"], (k - 2) * NT + 1)
                step(0, True)
                with pe.Fori(1, NT if k > 1 else NT - 1) as t:
                    if k > 1:
                        pe.wait_ge(S["acc_r"], t + ((k - 2) * NT + 1))
                    step(t, False)
                if k == 1:
                    pe.wait_ge(S["inv_r"], 1)
                    step(NT - 1, False)

            pe.wait_ge(S["acc_r"], (STEPS - 1) * NT + 7)
            pe.wait_ge(S["w_in5"], 16)
            pe.wait_ge(S["small_in"], SMALL)
            for k in range(KT):
                for j in range(KT):
                    mm(ps[:, 6, k * 64:k * 64 + VCOL + H], stage[:, 0, j, k * P:(k + 1) * P], abT[:, j, :],
                       start=j == 0, stop=j == KT - 1)
            for v in range(2):
                for j in range(KT):
                    ins = mm(ps[0:H, 6, 256:257], abT[:, j, VCOL * v:VCOL * v + H], wbc[:, j:j + 1],
                             start=v == 0 and j == 0, stop=v == 1 and j == KT - 1)
            pe.transpose(ps[0:1, 6, 320:320 + P], far_at[:, 1:2], id32[:]).then_inc(S["wa_done"], 1)

            def transposes(layer, t, i):
                pe.wait_ge(S["x_lo"], t + (layer * NT + 1))
                for v in range(2):
                    for k in range(KT):
                        a = v * KT + k
                        ins = pe.transpose(bank16(i)[:, a * P:(a + 1) * P], cur[:, 1, v, t, k * P:(k + 1) * P], id16[:])
                ins.then_inc(S["xT_done"], 1)

            def per_tile(layer, products):
                transposes(layer, 0, 0)
                transposes(layer, 1, 1)
                pe.wait_ge(S["y_ready"], layer * NT + 6)
                products(0, 0)
                with pe.Fori(0, NT // 2 - 1) as r:
                    for i in (1, 0):
                        t = r * 2 + (2 - i)
                        transposes(layer, t + 1, 1 - i)
                        products(t, i)

            def product(layer, name, bank, done, free, n, t):
                pe.wait_ge(S["xT_in2"], t + (layer * NT + 1))
                pe.wait_ge(S[free], n)
                three(ps[:, bank, :], cols(xTs, t), weight(name)).then_inc(S[done], 1)

            def gather(layer, c16, left, done):
                pe.wait_ge(S["z_lo"], (layer + 1) * NT + 2)
                pe.wait_ge(S["y_ready"], (layer + 1) * NT)

                def tiles(parts):
                    with pe.Fori(0, NT) as t:
                        for c in parts:
                            for j in range(NT):
                                for v in range(2):
                                    ins = mm(ps[:, t, :], c[:, j, bass.ds(t * P, P)], cur[:, 0, v, j, :],
                                             start=c is c16 and j == 0 and v == 0,
                                             stop=c is parts[-1] and j == NT - 1 and v == 1)
                        ins.then_inc(S[done], 1)

                pe.wait_ge(S["big_in"], 1)
                with pe.If(flag(pe, 1)):
                    if layer == 0:
                        pe.wait_ge(S["left_in"], NT)
                        with pe.Fori(0, NT) as t:
                            pe.wait_ge(S["left_t"], t + 1)
                            for j in range(NT):
                                ins = pe.transpose(bank16(7)[:, j * P:(j + 1) * P], c_left[:, j, bass.ds(t * P, P)], id16[:])
                            ins.then_inc(S["left_done"], 1)
                        pe.wait_ge(S["left_t"], NT + 1)
                    tiles((c16, left))
                with pe.Else():
                    tiles((c16,))

            def products1(t, i):
                product(0, "W1", 4 + i, "z_done", "z_lo", t + 1, t)
            per_tile(0, products1)
            products1(NT - 1, 1)
            gather(0, cst, c_left, "gather1_done")

            def products2(t, i):
                product(1, "wc", 2 + i, "alpha_done", "alpha_in", t + 1, t)
                product(1, "wn", 4 + i, "z_done", "z_lo", t + (NT + 1), t)
            per_tile(1, products2)
            products2(NT - 1, 1)
            pe.wait_ge(S["alpha_in"], NT + 2)
            gather(1, cts, ct_left, "gather2_done")

            def products3(t, i):
                pe.wait_ge(S["xT_in2"], t + (2 * NT + 1))
                pe.wait_ge(S["nv_in"], t + 1)
                pe.wait_ge(S["exp_in"], t * 2 + 2)
                three(ps[:, 2 + i, 0:VCOL + H], cols(xTs, t), lambda k: [wa[:, v, k, :] for v in range(2)]).then_inc(S["uvc_done"], 1)
                product(2, "W3", 4 + i, "wx_done", "wx_in", t + 1, t)
            pe.wait_ge(S["wa_lo"], 1)
            per_tile(2, products3)
            pe.wait_ge(S["xT_in2"], 3 * NT)
            pe.wait_ge(S["y_ready"], 3 * NT)
            for half in range(2):
                ins = three(ps[0:VCOL + H, 6 + half, :], lambda k: [wa[:, v, k, :] for v in range(2)],
                            lambda k: [xTs[:, v, k, half * HALF:(half + 1) * HALF] for v in range(2)])
            ins.then_inc(S["uv_done"], 1)
            products3(NT - 1, 1)
            def uf_spread(h):
                for a in range(2):
                    for v in range(2):
                        ins = mm(ps[:, a, :], sel[:, h, :], usf[:, v, a * HALF:(a + 1) * HALF], start=v == 0, stop=v == 1)
                ins.then_inc(S["uf_done"], 1)

            pe.wait_ge(S["usf_in"], 2)
            uf_spread(0)
            pe.wait_ge(S["q_row"], 1)
            pe.wait_ge(S["nv_in"], NT - 1 + 2)
            pe.wait_ge(S["exp_in"], 2 * (NT - 1) + 2)
            for t in range(NT):
                ins = pe.transpose(ps[:, 2, t * H:(t + 1) * H], qrow[:, t * P:(t + 1) * P], id32[0:H, 0:H])
            ins.then_inc(S["q_done"], 1)
            pe.wait_ge(S["lim_in"], 1)
            pe.transpose(ps[0:1, 3, P:2 * P], lim[:, 0:1], id32[:]).then_inc(S["lim_done"], 1)
            pe.wait_ge(S["mode"], 1)
            with pe.If(flag(pe, 2)):
                pe.wait_ge(S["wx_in"], NT + 2)
                pe.wait_ge(S["w_row"], 1)
                for j in range(NT):
                    ins = pe.transpose(ps[:, 0, j * H:(j + 1) * H], wrow[:, j * P:(j + 1) * P], id32[0:H, 0:H])
                ins.then_inc(S["w_done"], 1)
                with pe.Fori(0, H) as h:
                    pe.wait_ge(S["most_ready"], h + 1)
                    for t in range(NT):
                        ins = pe.transpose(ps[:, 2 + t // 4, t % 4 * P:(t % 4 + 1) * P], most[:, t * P:(t + 1) * P], id32[:])
                    ins.then_inc(S["most_done"], 1)
                pe.wait_ge(S["most_in"], H)
                for t in range(NT):
                    ins = pe.transpose(ps[0:H, t // 4, t % 4 * P:(t % 4 + 1) * P], mcol[:, t, :], id32[:])
                ins.then_inc(S["m_done"], 1)
                pe.wait_ge(S["m_in"], 1)
                for j in range(NT):
                    ins = pe.transpose(ps[:, 0, j * H:(j + 1) * H], vrow[:, j * P:(j + 1) * P], id32[0:H, 0:H])
                ins.then_inc(S["v_done"], 1)
                def u_spread(h):
                    for a in range(4):
                        for v in range(2):
                            ins = mm(ps[:, a, :], sel[:, h, :], us[:, v, a // 2, a % 2 * HALF:(a % 2 + 1) * HALF],
                                     start=v == 0, stop=v == 1)
                    ins.then_inc(S["u_done"], 1)

                def back(h):
                    pe.wait_ge(S["oT_in"], h + 1)
                    pe.wait_ge(S["back_free"], h + 1)
                    for t in range(NT):
                        ins = pe.transpose(ps[:, 6 + t // 4, t % 4 * (DH + 1):(t % 4 + 1) * (DH + 1)],
                                           oT[:, t * P:(t + 1) * P], id32[0:DH + 1, 0:DH + 1])
                    ins.then_inc(S["back_done"], 1)

                pe.wait_ge(S["us_lo"], 1)
                pe.wait_ge(S["wx_in"], NT + 2)
                pe.wait_ge(S["vc_ready"], 2)
                u_spread(0)
                with pe.Fori(0, H // 2) as hp:
                    for q in range(2):
                        h = hp * 2 + q
                        pe.wait_ge(S["wxh_ready"], h + 1)
                        for j in range(NT):
                            pe.wait_ge(S["p_ready"], h * NT + (j + 3))
                            for half in range(2):
                                ins = mm(ps[0:DH + 1, 4 + half, :], wxh[:, q, j, :], PR[:, j % 2, half * HALF:(half + 1) * HALF],
                                         start=j == 0, stop=j == NT - 1)
                            ins.then_inc(S["p_free"], 1)
                            if j == 2:
                                pe.wait_ge(S["ub_ready"], h + 1)
                                u_spread(h + 1)
                        back(h)
            with pe.Else():
                pe.wait_ge(S["wx_in"], NT + 2)
                pe.wait_ge(S["uv_in"], 2)
                for b in (4, 7):
                    mm(ps[:, b, 2 * YW:3 * YW], sel[:, H, :], usf[:, 0, 0:YW], start=True, stop=True)
                pe.wait_ge(S["y_lo"], NT + 2)
                pe.wait_ge(S["y_hi"], NT)
                pe.wait_ge(S["neg_ready"], NT)
                pe.wait_ge(S["q_in"], 1)

                pe.wait_ge(S["uf_ready"], 1)
                uf_spread(1)

                def head(h, q, following):
                    if following:
                        pe.wait_ge(S["uf_ready"], h + 2)
                        uf_spread(h + 2)
                    pe.wait_ge(S["cz_ready"], h * NT + 3 * NT)
                    pe.wait_ge(S["comb_ready"], h * 2 + 2)
                    for t in range(NT):
                        o = ps[:, 2 + 3 * q + t // 3, t % 3 * YW:(t % 3 + 1) * YW]
                        for j in range(NT):
                            for v in range(2):
                                mm(o, cz[q][:, j, t * P:(t + 1) * P], yh[:, j, v, bass.ds(h, 1), :],
                                   start=j == 0 and v == 0, stop=False)
                            for v in range(2):
                                ins = mm(o[:, DH + 1:YW], cst[:, j, t * P:(t + 1) * P], yh[:, j, v, bass.ds(h, 1), DH + 1:YW],
                                         start=False, stop=j == NT - 1 and v == 1)
                    ins.then_inc(S["head_done"], 1)
                with pe.Fori(0, H // 2 - 1) as hp:
                    for q in range(2):
                        head(hp * 2 + q, q, True)
                head(H - 2, 0, False)
                head(H - 1, 1, False)

        @block.vector
        def _(dve):
            stt, ts, tt = dve.scalar_tensor_tensor, dve.tensor_scalar, dve.tensor_tensor
            dve.sem_inc(S["win_free"], 2)
            dve.sem_inc(S["acc0"], 1)
            dve.sem_inc(S["p_ready"], 2)
            dve.sem_inc(S["back_free"], 1)
            dve.sem_inc(S["z_lo"], 2)
            dve.sem_inc(S["alpha_in"], 2)
            dve.sem_inc(S["wx_in"], 2)
            dve.sem_inc(S["left_t"], 1)
            dve.sem_inc(S["y_lo"], 2)
            dve.sem_inc(S["nv_in"], 2)
            dve.sem_inc(S["exp_in"], 4)
            dve.sem_inc(S["cz_ready"], 2 * NT)
            dve.sem_inc(S["comb_ready"], 4)
            dve.sem_inc(S["att_in"], 2)
            dve.sem_inc(S["head_done"], 2)
            dve.sem_inc(S["most_free"], 1)
            links = [0]

            def link(ins):
                links[0] += 1
                ins.then_inc(S["link"], 1)
                dve.wait_ge(S["link"], links[0])

            dve.memset(c32[:, 0:NT // 2, :], 0.0).then_inc(S["c32z"], 1)
            dve.memset(key[:, :, NG:NG + 1], -1.0).then_inc(S["key_in"], 1)
            dve.memset(slo[:, :, NG:NG + 1], -1.0).then_inc(S["key_in"], 1)
            dve.memset(far[:, :, NG:NG + 1], -1.0).then_inc(S["far_in"], 1)
            dve.wait_ge(S["edges"], 32)
            ts(i_hi, e_src, 7, None, ALU.arith_shift_right).then_inc(S["ints"], 1)
            ts(i_lo, e_src, P - 1, None, ALU.bitwise_and).then_inc(S["ints"], 1)
            link(dve.tensor_copy(f_dst, e_dst))
            dve.wait_ge(S["ints"], 2)
            dve.tensor_copy(f_lo, i_lo).then_inc(S["idx"], 1)
            dve.tensor_copy(f_hi, i_hi).then_inc(S["ints"], 1)
            link(dve.tensor_reduce(base[:, 1:2], f_dst, AX, ALU.min))
            link(ts(base[:, 0:1], base[:, 1:2], float(N - WIN), None, ALU.min))
            link(ts(f_rel, f_dst, base[:, 0:1], None, ALU.subtract))
            ts(f_bad, f_rel, float(WIN), None, ALU.is_ge).then_inc(S["ints"], 1)
            dve.wait_ge(S["ints"], 4)
            link(stt(f_far, f_hi, float(N), f_dst, ALU.mult, ALU.add))
            link(stt(f_far, f_far, 1.0, f_bad, ALU.add, ALU.mult))
            ts(f_far, f_far, -1.0, None, ALU.add).then_inc(S["idx"], 1)
            link(dve.tensor_reduce(far_at[0:NG, 0:1], f_bad, AX, ALU.max))
            link(stt(f_hi, f_hi, float(WIN), f_rel, ALU.mult, ALU.add))
            stt(f_key, f_bad, 1000.0, f_hi, ALU.mult, ALU.add).then_inc(S["idx"], 1)
            dve.wait_ge(S["tr"], 1)
            dve.tensor_copy(slo[:, :, 0:NG], ps[:, 2, 0:E // P].rearrange("p (c g) -> p c g", c=NC)).then_inc(S["key_in"], 1)
            dve.tensor_copy(key[:, :, 0:NG], ps[:, 3, 0:E // P].rearrange("p (c g) -> p c g", c=NC)).then_inc(S["key_in"], 1)
            dve.tensor_copy(base_i[:], ps[0:1, 4, 0:NG]).then_inc(S["key_in"], 1)
            dve.tensor_copy(far[:, :, 0:NG], ps[:, 5, 0:E // P].rearrange("p (c g) -> p c g", c=NC)).then_inc(S["far_in"], 1)
            link(dve.tensor_reduce(f_flag[:, 0:1], ps[0:1, 4, NG:2 * NG], AX, ALU.max))
            dve.tensor_copy(flags[:, 0:1], f_flag[:, 0:1]).then_inc(S["far_in"], 1)
            dve.wait_ge(S["key_in"], 5)
            dve.wait_ge(S["const_ready"], 12)
            dve.wait_ge(S["c32z"], 2)

            def key_hot(g, i):
                dve.wait_ge(S["hot_free"], g + 1)
                ts(oh_lo[:, i % 2 * NC, :], iota_lo[:], slo[:, 0, bass.ds(g, 1)], None,
                   ALU.is_equal).then_inc(S["key_ready"], 1)
                for c in range(NC):
                    ts(oh_key[:, i % 2 * NC + c, :], iota_key[:], key[:, c, bass.ds(g, 1)], None,
                       ALU.is_equal).then_inc(S["key_ready"], 1)

            def add_window(g, i):
                first = dve.value_load(base_i[0:1, bass.ds(g, 1)], min_val=0, max_val=N - WIN)
                dve.wait_ge(S["hot_free"], g + 3)
                dve.wait_ge(S["win_free"], g + 2)
                c = c32[:, :, bass.ds(first, WIN)]
                tt(c, c, ps[:, i % 2, 0:KEYS].rearrange("p (a w) -> p a w", w=WIN), ALU.add).then_inc(S["win_free"], 1)

            def groups(t):
                for i in range(NT):
                    g = t * NT + i
                    key_hot(g + 1, i + 1)
                    add_window(g, i)

            key_hot(0, 0)
            groups(0)
            dve.wait_ge(S["xT_hi"], 1)
            tt(xTs[:, 1, KT // 2:], xTraw[:, KT // 2:], xTs[:, 0, KT // 2:], ALU.subtract).then_inc(S["xT_lo"], 1)
            with dve.Fori(1, NT) as t:
                groups(t)

            dve.wait_ge(S["win_free"], NG + 2)
            dve.wait_ge(S["far_in"], 3)
            with dve.If(flag(dve, 0)):
                for a in range(NT):
                    ts(iota_n[:, a * P:(a + 1) * P], iota_lo[:], float(a * P), None, ALU.add).then_inc(S["far_iota"], 1)
                dve.wait_ge(S["far_iota"], NT)
                cols_s = slo[:].rearrange("p c g -> p (c g)")
                cols_f = far.rearrange("p c g -> p (c g)")
                CHUNKS = NC * (NG + 1)
                with dve.Fori(0, NT) as a:
                    with dve.Fori(0, CHUNKS) as e:
                        n = a * CHUNKS + e
                        dve.wait_ge(S["far_free"], n + 1)
                        ts(oh_far, iota_n, cols_f[:, bass.ds(e, 1)], None, ALU.is_equal).then_inc(S["far_hot"], 1)
                        ts(oh_lo[:, 0, :], iota_lo[:], cols_s[:, bass.ds(e, 1)], None, ALU.is_equal).then_inc(S["far_hot"], 1)
                    dve.wait_ge(S["far_done"], a + 1)
                    ts(far, far, -float(N), None, ALU.add).then_inc(S["far_added"], 1)
                    tt(c32[:, a, :], c32[:, a, :], ps[:, 0:2, :].rearrange("p a n -> p (a n)"), ALU.add).then_inc(S["far_added"], 1)
                    dve.wait_ge(S["far_added"], a * 2 + 2)
            dve.sem_inc(S["counted"], 1)
            for j in range(3, NT):
                dve.tensor_copy(cst[:, j, :], c32[:, j, :]).then_inc(S["cst_ready"], 1)

            def either(t):
                dve.wait_ge(S["cts_ready"], t + 3)
                tt(adj[:, t, :], cts[:, t, :], cst[:, t, :], ALU.add).then_inc(S["adj_sum"], 1)

            def one(t):
                dve.wait_ge(S["adj_sum"], t + 1)
                ts(adj[:, t, :], adj[:, t, :], 1.0, None, ALU.min).then_inc(S["adj_one"], 1)

            def diagonal(t):
                dve.wait_ge(S["adj_one"], t + 1)
                diag = adj[:, t, bass.ds(t * P, P)]
                tt(diag, diag, id16[:], ALU.add).then_inc(S["adj_ready"], 1)

            either(0)
            one(0)
            with dve.Fori(1, NT) as t:
                either(t)
                diagonal(t - 1)
                one(t)
            diagonal(NT - 1)
            dve.wait_ge(S["deg_done"], 1)
            link(ts(deg[:], ps[:, 7, 0:NT], 1.0, None, ALU.max))
            dve.reciprocal(invdeg[:], deg[:]).then_inc(S["inv_r"], 1)
            dve.wait_ge(S["inv_r"], 1)
            dve.wait_ge(S["small_in"], SMALL)
            for k in range(STEPS):
                ts(winv[:, k, :], invdeg[:], dwb[:, k + 1:k + 2], None, ALU.mult).then_inc(S["winv_r"], 1)
            dve.wait_ge(S["winv_r"], STEPS)
            dve.wait_ge(S["acc0"], NT + 1)
            dve.wait_ge(S["h_lo"], NT + 1)

            def scales(layer, t, i):
                c = bass.ds(t, 1)
                dve.wait_ge(S["std_ready"], t + (layer * NT + 1))
                dve.reciprocal(rstd[:, c], std[:, c]).then_inc(S["rstd_ready"], 1)
                dve.wait_ge(S["rstd_ready"], t + (layer * NT + 1))
                ts(nmr[:, c], mv[:, i, 0:1], rstd[:, c], -1.0, ALU.mult, ALU.mult).then_inc(S["nmr_ready"], 1)

            def moments(layer, t, i):
                dve.drain()
                dve.bn_stats(st[:, i, :], xcur[:, t, :]).then_inc(S["st_a"], 1)
                dve.drain()
                dve.bn_aggr(mv[:, i, :], st[:, i, :]).then_inc(S["moments"], 1)

            def norm_loop(layer, total):
                total(0)
                moments(layer, 0, 0)
                with dve.Fori(0, NT // 2 - 1) as r:
                    for i in (1, 0):
                        t = r * 2 + (2 - i)
                        total(t)
                        moments(layer, t, i)
                        scales(layer, t - 1, 1 - i)
                total(NT - 1)
                moments(layer, NT - 1, 1)
                scales(layer, NT - 2, 0)
                scales(layer, NT - 1, 1)

            for k in range(1, STEPS):
                if k == 2:
                    link(dve.tensor_reduce(cnt[:], c32[:], AX, ALU.add))
                    link(dve.tensor_reduce(far_at[:, 1:2], cnt[:], AX, ALU.max))
                    link(ts(cnt1[:], cnt[:], 1.0, None, ALU.max))
                    link(dve.reciprocal(gsc[:], cnt1[:]))
                    link(dve.reciprocal(nan[:], cnt[:]))
                    link(ts(nan[:], nan[:], 0.0, None, ALU.mult))
                with dve.Fori(0, NT) as t:
                    n = t + ((k - 1) * NT + 1)
                    dve.wait_ge(S["step_hi"], n)
                    stt(cur[:, k % 2, 1, t, :], ps[:, t, :], invdeg[:, bass.ds(t, 1)], cur[:, k % 2, 0, t, :],
                        ALU.mult, ALU.subtract).then_inc(S["step_lo"], 1)
                    stt(acc[:, t, :], ps[:, t, :], winv[:, k - 1, bass.ds(t, 1)], acc[:, t, :],
                        ALU.mult, ALU.add).then_inc(S["acc_r"], 1)

            def total0(t):
                dve.wait_ge(S["step_done"], t + ((STEPS - 1) * NT + 1))
                stt(acc[:, t, :], ps[:, t, :], winv[:, STEPS - 1, bass.ds(t, 1)], acc[:, t, :],
                    ALU.mult, ALU.add).then_inc(S["acc_r"], 1)
                dve.wait_ge(S["acc_r"], t + ((STEPS - 1) * NT + 1))
                stt(xcur[:, t, :], acc[:, t, :], 0.0, xcur[:, t, :], ALU.max, ALU.add).then_inc(S["y_ready"], 1)
            dve.wait_ge(S["x_in"], 16)
            norm_loop(0, total0)

            dve.wait_ge(S["wa_done"], 1)
            link(dve.tensor_reduce(f_flag[:, 1:2], ps[0:1, 6, 320:320 + P], AX, ALU.max))
            ts(flags[:, 1:2], f_flag[:, 1:2], EXACT, None, ALU.is_gt).then_inc(S["big_in"], 1)
            link(ts(abT[:], ps[:, 6, 0:256].rearrange("p (k c) -> p k c", c=64)[:, :, 0:VCOL + H], WSCALE, None, ALU.mult))
            link(dve.tensor_copy(wa[:, 0], abT[:]))
            tt(wa[:, 1], abT[:], wa[:, 0], ALU.subtract).then_inc(S["wa_lo"], 1)
            tt(crow[:, 0:1], ps[0:H, 6, 256:257], abc[:], ALU.add).then_inc(S["crow_r"], 1)

            def z_lo(layer, t, i):
                dve.wait_ge(S["z_hi"], t + (layer * NT + 1))
                stt(cur[:, 0, 1, t, :], ps[:, 4 + i, :], 1 / WSCALE, cur[:, 0, 0, t, :],
                    ALU.mult, ALU.subtract).then_inc(S["z_lo"], 1)

            with dve.Fori(0, NT // 2) as r:
                for i in range(2):
                    z_lo(0, r * 2 + i, i)

            dve.wait_ge(S["big_in"], 1)
            with dve.If(flag(dve, 1)):
                dve.wait_ge(S["y_ready"], NT)
                with dve.Fori(0, NT) as t:
                    tt(c_left[:, t, :], c32[:, t, :], cst[:, t, :], ALU.subtract).then_inc(S["left_in"], 1)
                with dve.Fori(0, NT) as t:
                    dve.wait_ge(S["left_done"], t + 1)
                    dve.tensor_copy(ct_left[:, t, :], bank16(7)).then_inc(S["left_t"], 1)

            def total1(t):
                dve.wait_ge(S["gather1_done"], t + 1)
                dve.wait_ge(S["xb_ready"], t + 1)
                tt(xcur[:, t, :], ps[:, t, :], xcur[:, t, :], ALU.add).then_inc(S["y_ready"], 1)
            norm_loop(1, total1)

            with dve.Fori(0, NT // 2) as r:
                for i in range(2):
                    t = r * 2 + i
                    dve.wait_ge(S["alpha_done"], t + 1)
                    dve.wait_ge(S["xb_ready"], t + (NT + 1))
                    stt(xcur[:, t, :], ps[:, 2 + i, :], 1 / WSCALE, xcur[:, t, :],
                        ALU.mult, ALU.add).then_inc(S["alpha_in"], 1)
                    z_lo(1, t, i)
            dve.wait_ge(S["alpha_in"], NT + 2)

            def total2(t):
                dve.wait_ge(S["gather2_done"], t + 1)
                stt(xcur[:, t, :], ps[:, t, :], gsc[:, bass.ds(t, 1)], xcur[:, t, :],
                    ALU.mult, ALU.add).then_inc(S["y_ready"], 1)
            norm_loop(2, total2)

            def wx_evict(t, i):
                dve.wait_ge(S["wx_done"], t + 1)
                stt(wx[:, t, :], ps[:, 4 + i, :], 1 / WSCALE, bb[:, 2, :], ALU.mult, ALU.add).then_inc(S["wx_in"], 1)
                dve.wait_ge(S["exp_in"], t * 2 + 6)
                ts(nv[:, t, :], ps[:, 2 + i, VCOL:VCOL + H], -1 / WSCALE, None, ALU.mult).then_inc(S["nv_in"], 1)
                dve.wait_ge(S["wx_in"], t + 3)
                tt(yf[:, i, :, :, 0:DH], wx[:, t, :].rearrange("p (h d) -> p h d", h=H).unsqueeze(2).broadcast_to([P, H, 2, DH]),
                   yf[:, i, :, :, DH:DH + 1].broadcast_to([P, H, 2, DH]), ALU.mult).then_inc(S["y_ready3"], 1)
                dve.tensor_reduce(wm[:, bass.ds(t, 1)], wx[:, t, :], AX, ALU.max, apply_absolute_value=True).then_inc(S["wm_in"], 1)
            with dve.Fori(0, NT // 2 - 1) as r:
                for i in range(2):
                    wx_evict(r * 2 + i, i)
            wx_evict(NT - 2, 0)

            uv = ps[:, 6:8, :].rearrange("p a n -> p (a n)")
            dve.wait_ge(S["uv_done"], 1)
            ts(z0, uv[0:H], 1 / WSCALE, crow[:, 0:1], ALU.mult, ALU.add).then_inc(S["uv_in"], 1)
            ts(vrow, uv[VCOL:VCOL + H], 1 / WSCALE, None, ALU.mult).then_inc(S["uv_in"], 1)
            dve.wait_ge(S["uv_in"], 2)
            dve.tensor_copy(usf[:, 0], z0).then_inc(S["usf_in"], 1)
            dve.wait_ge(S["usf_in"], 1)
            tt(usf[:, 1], z0, usf[:, 0], ALU.subtract).then_inc(S["usf_in"], 1)
            wx_evict(NT - 1, 1)

            dve.tensor_reduce(lim[0:H, 2:3], z0, AX, ALU.max, apply_absolute_value=True).then_inc(S["wm_in"], 1)
            dve.tensor_reduce(lim[0:H, 3:4], vrow, AX, ALU.max, apply_absolute_value=True).then_inc(S["wm_in"], 1)
            dve.wait_ge(S["wm_in"], NT + 2)
            link(dve.tensor_reduce(lim[:, 1:2], wm[:], AX, ALU.max))
            link(ts(lim[:, 0:1], lim[:, 1:2], 1 / WXMAX, None, ALU.mult))
            link(stt(lim[0:H, 0:1], lim[0:H, 2:3], 1 / UMAX, lim[0:H, 0:1], ALU.mult, ALU.max))
            stt(lim[0:H, 0:1], lim[0:H, 3:4], 1 / VMAX, lim[0:H, 0:1], ALU.mult, ALU.max).then_inc(S["lim_in"], 1)
            dve.wait_ge(S["q_done"], 1)
            dve.memset(qc[:, :, NT:OS], 0.0).then_inc(S["qz"], 1)
            dve.tensor_copy(qc[:, :, 0:NT], ps[:, 2, 0:NT * H].rearrange("p (t h) -> p h t", h=H)).then_inc(S["q_in"], 1)
            dve.wait_ge(S["lim_done"], 1)
            link(dve.tensor_reduce(lim[0:1, 1:2], ps[0:1, 3, P:2 * P], AX, ALU.max))
            link(stt(lim[0:1, 2:3], f_flag[:, 1:2], 1 / EXACT, lim[0:1, 1:2], ALU.mult, ALU.max))
            ts(flags[:, 2:3], lim[0:1, 2:3], 1.0, None, ALU.is_gt).then_inc(S["mode"], 1)
            dve.wait_ge(S["mode"], 1)
            with dve.If(flag(dve, 2)):
                dve.wait_ge(S["y_lo"], NT + 2)
                dve.wait_ge(S["q_in"], 1)
                glinks = [0]

                def glink(ins):
                    glinks[0] += 1
                    ins.then_inc(S["glink"], 1)
                    dve.wait_ge(S["glink"], glinks[0])

                glink(dve.tensor_reduce(crow[:, 1:2], vrow, AX, ALU.min))
                ts(wrow, vrow, crow[:, 1:2], 1.0, ALU.subtract, ALU.add).then_inc(S["w_row"], 1)
                dve.wait_ge(S["w_done"], 1)
                wcol = vc[:, 0, :]
                glink(dve.tensor_copy(wcol, ps[:, 0, 0:NT * H]))
                with dve.Fori(0, H) as h:
                    dve.wait_ge(S["most_free"], h + 1)
                    dve.memset(most, 0.0).then_inc(S["most_a"], 1)
                    for j in range(NT):
                        dve.wait_ge(S["most_a"], h * (2 * NT + 1) + (2 * j + 1))
                        ts(seen, c32[:, j, :], 1.0, wcol[:, bass.ds(j * H + h, 1)], ALU.min, ALU.mult).then_inc(S["most_a"], 1)
                        dve.wait_ge(S["most_a"], h * (2 * NT + 1) + (2 * j + 2))
                        tt(most, most, seen, ALU.max).then_inc(S["most_a"], 1)
                    dve.wait_ge(S["most_a"], h * (2 * NT + 1) + (2 * NT + 1))
                    dve.sem_inc(S["most_ready"], 1)
                    dve.wait_ge(S["most_done"], h + 1)
                    dve.tensor_reduce(mcol[:, :, bass.ds(h, 1)].rearrange("p t a -> p (t a)"),
                                      ps[:, 2:4, :].rearrange("p a (b n) -> p (a b) n", n=P), AX, ALU.max).then_inc(S["most_in"], 1)
                    dve.wait_ge(S["most_in"], h + 1)
                    dve.sem_inc(S["most_free"], 1)
                dve.wait_ge(S["m_done"], 1)
                glink(ts(mrow, ps[0:H, 0:2, :].rearrange("p a n -> p (a n)"), crow[:, 1:2], -1.0, ALU.add, ALU.add))
                glink(tt(zrow, z0, mrow, ALU.add))
                ins = stt(mrow, zrow, SLOPE, zrow, ALU.mult, ALU.max)
                ins.then_inc(S["m_in"], 1)
                dve.wait_ge(S["m_in"], 1)
                glink(tt(urow[:, 0, :], z0, mrow, ALU.subtract))
                glink(stt(urow[:, 1, :], z0, SLOPE, mrow, ALU.mult, ALU.subtract))
                glink(dve.tensor_copy(us[:, 0], urow))
                tt(us[:, 1], urow, us[:, 0], ALU.subtract).then_inc(S["us_lo"], 1)
                dve.wait_ge(S["v_done"], 1)
                for i, f in enumerate((1 - SLOPE, SLOPE)):
                    ts(vc[:, i, :], ps[:, 0, 0:NT * H], f, None, ALU.mult).then_inc(S["vc_ready"], 1)
                dve.wait_ge(S["us_lo"], 1)
                dve.wait_ge(S["vc_ready"], 2)

                def scores(h, q, j):
                    if j == 0:
                        dve.wait_ge(S["ub_ready"], h + 1)
                    dve.wait_ge(S["e_ready"], h * NT + (j + 1))
                    stt(T[:, j % 2, :], ub[:, q, 0, :], vc[:, 0, bass.ds(j * H + h, 1)], ub[:, q, 1, :],
                        ALU.add, ALU.max).then_inc(S["t_ready"], 1)

                def weights(h, j):
                    n = h * NT + j
                    dve.wait_ge(S["e_ready"], n + 3)
                    dve.wait_ge(S["p_free"], n + 1)
                    stt(PR[:, j % 2, :], EX[:, j % 2, :], 2.0, c32[:, j, :], ALU.min, ALU.mult).then_inc(S["p_ready"], 1)

                def head_out(h):
                    o = ps[:, 6:8, 0:4 * (DH + 1)].rearrange("p a (b d) -> p a b d", b=4)
                    dve.wait_ge(S["back_done"], h + 3)
                    ts(rden[:], o[:, :, :, DH], 1e-37, None, ALU.max).then_inc(S["rd_r"], 1)
                    dve.wait_ge(S["rd_r"], h * 2 + 1)
                    dve.reciprocal(rden[:], rden[:]).then_inc(S["rd_r"], 1)
                    dve.wait_ge(S["rd_r"], h * 2 + 2)
                    tt(att.rearrange("p (a b) d -> p a b d", a=2), o[:, :, :, 0:DH],
                       rden[:].unsqueeze(3).broadcast_to([P, 2, 4, DH]), ALU.mult).then_inc(S["back_free"], 1)
                    dve.wait_ge(S["back_free"], h + 2)
                    xs = xcur[:, :, bass.ds(h * DH, DH)]
                    tt(xs, xs, att, ALU.add).then_inc(S["att_added"], 1)

                scores(0, 0, 0)
                with dve.Fori(0, H // 2) as hp:
                    for q in range(2):
                        h = hp * 2 + q
                        for j in range(NT):
                            if j < NT - 1:
                                scores(h, q, j + 1)
                            else:
                                scores(h + 1, 1 - q, 0)
                            weights(h, j)
                        head_out(h)
                dve.wait_ge(S["att_added"], H)
            with dve.Else():
                dve.wait_ge(S["q_in"], 1)
                dve.wait_ge(S["qz"], 1)

                def mask(h, q, j):
                    if j == 0:
                        dve.wait_ge(S["uf_ready"], h + 1)
                        dve.wait_ge(S["head_done"], h + 1)
                    stt(cz[q][:, j, :], uf[:, q], nv[:, j, bass.ds(h, 1)], c32[:, j, :],
                        ALU.is_gt, ALU.mult).then_inc(S["cz_ready"], 1)

                def combine(h, q, n):
                    o = ps[:, 2 + 3 * q:5 + 3 * q, 0:3 * YW].rearrange("p a (b d) -> p a b d", b=3)
                    c = comb[:, q].rearrange("p (a b) d -> p a b d", a=3)
                    if n == 0:
                        dve.wait_ge(S["head_done"], h + 3)
                        dve.wait_ge(S["att_in"], h + 1)
                        qh = qc[:, bass.ds(h, 1), :].rearrange("p o (a b) -> p (o a) b", a=3)
                        tt(c, o[:, :, :, 0:DH + 1], qh.unsqueeze(3).broadcast_to([P, 3, 3, DH + 1]),
                           ALU.mult).then_inc(S["comb_ready"], 1)
                    if n == 1:
                        dve.wait_ge(S["comb_ready"], h * 2 + 5)
                        tt(c, c, o[:, :, :, DH + 1:YW], ALU.subtract).then_inc(S["comb_ready"], 1)
                    if n == 2:
                        dve.wait_ge(S["comb_ready"], h * 2 + 6)
                        ts(rdf[:, q], comb[:, q, :, DH], 1e-37, None, ALU.max).then_inc(S["den_ready"], 1)
                    if n == 3:
                        dve.wait_ge(S["den_ready"], h * 2 + 1)
                        dve.reciprocal(rdf[:, q], rdf[:, q]).then_inc(S["den_ready"], 1)

                for q in range(2):
                    for j in range(NT):
                        mask(q, q, j)
                with dve.Fori(0, H // 2 - 1) as hp:
                    for q in range(2):
                        h = hp * 2 + q
                        for j in range(NT):
                            mask(h + 2, q, j)
                            if j < 4:
                                combine(h, q, j)
                for q in range(2):
                    for n in range(4):
                        combine(H - 2 + q, q, n)
                dve.wait_ge(S["att_in"], H + 2)
            for t in range(NT):
                dve.bn_stats(st8[:, t, :], xcur[:, t, :]).then_inc(S["st8_in"], 1)
            dve.drain()
            for t in range(NT):
                dve.bn_aggr(mv8[:, t, :], st8[:, t, :]).then_inc(S["mv8_in"], 1)
            dve.wait_ge(S["std8"], 1)
            link(dve.reciprocal(rstd[:], std[:]))
            link(tt(rstd[:], rstd[:], nan[:], ALU.add))
            stt(nmr[:], mv8[:, :, 0], -1.0, rstd[:], ALU.mult, ALU.mult).then_inc(S["scale8"], 1)
            dve.wait_ge(S["scale8"], 1)
            for t in range(1, NT, 2):
                ts(xcur[:, t, :], xcur[:, t, :], rstd[:, t:t + 1], nmr[:, t:t + 1], ALU.mult, ALU.add).then_inc(S["out_odd"], 1)


def kernel(**inputs):
    import numpy as np
    import concourse.bacc as bacc
    from concourse.bass_utils import run_bass_kernel_spmd

    g = {k: np.asarray(v) for k, v in inputs.items()}
    laid = {
        "x": g["x"], "xT": g["x"].T, "src": g["src"], "dst": g["dst"],
        "W0": g["L0_gnn_W"], "b0": g["L0_gnn_b"], "dw": g["L0_gnn_diffusion_weights"],
        "W1T": g["L1_gnn_W"].T, "b1": g["L1_gnn_b"],
        "wc": g["L2_gnn_wc"], "wn": g["L2_gnn_wn"], "b2": g["L2_gnn_bias"],
        "W3": g["L3_gnn_Ws"].transpose(1, 0, 2).reshape(D, D),
        "W3T": g["L3_gnn_Ws"].transpose(0, 2, 1).reshape(D, D),
        "b3": g["L3_gnn_Wb"].reshape(D), "b3T": g["L3_gnn_Wb"].reshape(KT, P).T, "aw": g["L3_gnn_a_w"], "ab": g["L3_gnn_a_b"],
    }
    laid = {k: np.ascontiguousarray(v) for k, v in laid.items()}
    nc = bacc.Bacc("TRN2", target_bir_lowering=False, num_devices=1)
    aps = {k: nc.dram_tensor(f"in_{k}", v.shape, mybir.dt.from_np(v.dtype), kind="ExternalInput").ap()
           for k, v in laid.items()}
    out = nc.dram_tensor("out", (N, D), F32, kind="ExternalOutput").ap()
    build(nc, **aps, out=out)
    r = run_bass_kernel_spmd(nc, [{f"in_{k}": v for k, v in laid.items()}], core_ids=[0])
    return r.results[0]["out"]
```

```python
from contextlib import ExitStack

import concourse.bass as bass
from concourse import mybir
from concourse.alu_op_type import AluOpType as ALU

F32 = mybir.dt.float32
F16 = mybir.dt.float16
I32 = mybir.dt.int32
ACT = mybir.ActivationFunctionType
AX = mybir.AxisListType.X

P = 128
N = 1024
D = 512
E = 16384
NT = N // P
KT = D // P
HALF = 512
H = 8
DH = D // H
STEPS = 3
EPS = 1e-5
SLOPE = 0.2

GROUP = 256
NG = E // GROUP
NC = GROUP // P
WIN = 48
KEYS = NT * WIN

WSCALE = 64.0
ASCALE = 1.0 / 32
EXACT = 2048.0
YW = 2 * (DH + 1)
OS = 9
VMAX, WXMAX = 3.5, 120.0
QMAX, QMIN = 8e6, 1e-30
LN16 = 2.772588722239781
CA = 2
HT = NT // 2 - 1
VCOL = 32


def build(nc, x, xT, src, dst, W0, b0, dw, W1T, b1, wc, wn, b2, W3, W3T, b3, b3T, aw, ab, out):
    with ExitStack() as ctx:
        def sb(name, shape, dt):
            return ctx.enter_context(nc.sbuf_tensor(name, shape, dt))

        def sem(name):
            return ctx.enter_context(nc.semaphore(name))

        ps = ctx.enter_context(nc.psum_tensor("ps", [P, NT, HALF], F32))

        c32 = sb("c32", [P, NT, N], F32)
        cst = sb("cst", [P, NT, N], F16)
        cts = sb("cts", [P, NT, N], F16)
        adj = sb("adj", [P, NT, N], F16)
        xcur = sb("xcur", [P, NT, D], F32)
        acc = sb("acc", [P, NT, D], F32)
        xTraw = acc[:].rearrange("p a b -> p (a b)").rearrange("p (k n) -> p k n", k=KT)
        ub = acc[:].rearrange("p a b -> p (a b)").rearrange("p (q v n) -> p q v n", q=2, v=2)
        xTs = sb("xTs", [P, 2, KT, N], F16)
        big = sb("big", [P, 4 * 2 * KT * D + 4 * NT * D], F16)
        WS = 4 * 2 * KT * D
        ws = big[:, 0:WS].rearrange("p (s v k n) -> p s v k n", s=4, v=2, k=KT)
        cur = big[:, WS:].rearrange("p (s v a b) -> p s v a b", s=2, v=2, a=NT)
        spare = cur[:, 1, 1].rearrange("p a b -> p (a b)").bitcast(F32)
        w0raw = cur[:, 1, 0].rearrange("p a b -> p (a b)").bitcast(F32).rearrange("p (k n) -> p k n", k=KT)
        stage = xTs[:].rearrange("p v k n -> p (v k n)").bitcast(F32).rearrange(
            "p (s k n) -> p s k n", s=2, k=KT)
        tep = cur.rearrange("p s v a b -> p (s v a b)").bitcast(F32).rearrange(
            "p (f n) -> p f n", n=N)
        wx = cts[:].rearrange("p a b -> p (a b)").bitcast(F32).rearrange("p (a b) -> p a b", a=NT)
        SLOT = {"W0": 0, "W1": 1, "wc": 2, "wn": 3, "W3": 0}

        c_left = adj
        ct_left = acc[:].rearrange("p a b -> p (a b)").bitcast(F16).rearrange("p (a n) -> p a n", a=NT)

        y0 = 2 * KT * D
        yh = big[:, y0:y0 + NT * 2 * H * YW].rearrange("p (t v h n) -> p t v h n", t=NT, v=2, h=H)
        yq = [b.rearrange("p (t v n) -> p t v n", t=NT, v=2) for b in
              (big[:, 0:NT * 2 * YW], big[:, y0 + NT * 2 * H * YW:y0 + NT * 2 * (H + 1) * YW])]
        yf = acc[:].rearrange("p a b -> p (a b)")[:, 0:2 * H * YW].rearrange(
            "p (q h e d) -> p q h e d", q=2, h=H, e=2)
        cz = (adj, ct_left)
        xflat = xTs[:].rearrange("p v k n -> p (v k n)").bitcast(F32)
        uf = xflat[:, 0:2 * N].rearrange("p (q n) -> p q n", q=2)
        uf0 = acc[:].rearrange("p a b -> p (a b)")[:, 2 * H * YW:2 * H * YW + N]
        OW = OS * (DH + 1)
        comb = xflat[:, 2 * N:2 * N + 2 * OW].rearrange("p (q t d) -> p q t d", q=2, t=OS)
        attf = xflat[:, 2 * N + 2 * OW:2 * N + 2 * OW + D].rearrange("p (t d) -> p t d", d=DH)

        iota_lo = sb("iota_lo", [P, P], F16)
        iota_key = sb("iota_key", [P, KEYS], F16)
        id32 = sb("id32", [P, P], F32)
        id16 = sb("id16", [P, P], F16)
        ones16 = sb("ones16", [P, P], F16)
        sel = sb("sel", [H, H + 1, P], F16)
        epsc = sb("epsc", [P, 1], F32)

        cflat = cst[:].rearrange("p a b -> p (a b)")
        oh_end = 2 * NC * (P + KEYS)
        oh_lo = cflat[:, NT * N - oh_end:NT * N - 2 * NC * KEYS].rearrange("p (b n) -> p b n", n=P)
        oh_lo1 = cflat[:, 2 * N:3 * N].rearrange("p (b n) -> p b n", n=P)
        oh_lo0 = cflat[:, 3 * N:3 * N + NT // 2 * P].rearrange("p (b n) -> p b n", n=P)
        oh_key = cflat[:, NT * N - 2 * NC * KEYS:NT * N].rearrange("p (b n) -> p b n", n=KEYS)
        tmp = cst[0:NG].rearrange("p a b -> p (a b)").bitcast(F32).rearrange("p (f e) -> p f e", e=GROUP)
        tmpi = cst[0:NG].rearrange("p a b -> p (a b)").bitcast(I32).rearrange("p (f e) -> p f e", e=GROUP)
        e_dst, e_src, i_hi, i_lo = (tmpi[:, i, :] for i in range(4))
        f_dst, f_hi, f_lo, f_rel, f_key, f_bad, f_far = (tmp[:, i, :] for i in range(4, 11))
        base = sb("base", [NG, 2], F32)
        base_f = sb("base_f", [1, NG], F32)
        base_i = sb("base_i", [1, NG // 2], I32)
        slo = sb("slo", [P, NC, NG + 1], F32)
        slo_g = sb("slo_g", [P, NC, NT], F32)
        key = sb("key", [P, NC, NG + 1], F32)
        far = spare[:, 3 * D:3 * D + NC * (NG + 1)].rearrange(
            "p (c g) -> p c g", c=NC)
        far_at = sb("far_at", [P, 2], F32)
        flags = sb("flags", [1, 4], I32)
        f_flag = sb("f_flag", [1, 2], F32)
        iota_n = cflat[:, 0:N]
        oh_far = cflat[:, N:2 * N]

        b0f = spare[0:1, D:2 * D]
        b0s = spare[0:1, 2 * D:3 * D].bitcast(F16).rearrange("p (v d) -> p v d", v=2)
        bb = sb("bb", [P, 3, D], F32)
        dwb = sb("dwb", [P, STEPS + 1], F32)
        hb = spare[:, 0:D]
        deg = sb("deg", [P, NT], F32)
        invdeg = sb("invdeg", [P, NT], F32)
        winv = sb("winv", [P, STEPS, NT], F32)
        cnt = sb("cnt", [P, NT], F32)
        cnt1 = sb("cnt1", [P, NT], F32)
        gsc = sb("gsc", [P, NT], F32)
        nan = sb("nan", [P, NT], F32)
        st = sb("st", [P, 2, 6], F32)
        mv = sb("mv", [P, 2, 2], F32)
        std = sb("std", [P, NT], F32)
        rstd = sb("rstd", [P, NT], F32)
        nmr = sb("nmr", [P, NT], F32)
        abT = sb("abT", [P, KT, VCOL + H], F32)
        wa = sb("wa", [P, 2, KT, VCOL + H], F16)
        wbc = sb("wbc", [P, KT], F32)
        abc = sb("abc", [H, 1], F32)
        crow = sb("crow", [H, 3], F32)
        vc = sb("vc", [P, 2, NT * H], F32)
        wxh = xTs[:].rearrange("p v k n -> p (v k n)").bitcast(F32)[:, 0:2 * NT * (DH + 1)].rearrange(
            "p (q t d) -> p q t d", q=2, t=NT)
        rden = sb("rden", [P, 2, 4], F32)
        nv = sb("nv", [P, NT, H], F32)
        qc = sb("qc", [P, H, OS], F32)
        rdf = sb("rdf", [P, 2, OS], F32)
        ln16 = sb("ln16", [P, 1], F32)
        st8 = sb("st8", [P, NT, 12], F32)
        mv8 = sb("mv8", [P, NT, 2], F32)
        mcol = sb("mcol", [P, NT, H], F32)
        wm = sb("wm", [P, NT], F32)
        lim = sb("lim", [P, 4], F32)
        rows = tep[0:H]
        zrow, mrow, _, _, z0, vrow, qrow = (rows[:, i, :] for i in range(7))
        urow = rows[:, 2:4, :]
        wrow = qrow
        usf = rows[:, 7, :].bitcast(F16).rearrange("p (v n) -> p v n", v=2)
        seen, most = tep[:, 2, :], tep[:, 3, :]
        us = adj[0:H].rearrange("p a b -> p (a b)")[:, 0:4 * N].rearrange(
            "p (v a n) -> p v a n", v=2, a=2)
        T, EX, PR = (tep[:, 2 * i:2 * i + 2, :] for i in range(3))
        oT = tep[0:DH + 1, 6, :]
        att = tep[:, 7, 0:HALF].rearrange("p (t d) -> p t d", d=DH)

        class Semaphores(dict):
            def __missing__(self, name):
                self[name] = sem(name)
                return self[name]

        S = Semaphores()

        def settle(pool):
            pool.wait_ge(S["const_ready"], 12)

        def flag(engine, i):
            return engine.value_load(flags[0:1, i:i + 1], min_val=0, max_val=1) > 0

        def bank16(t):
            return ps[:, t, :].bitcast(F16)

        block = ctx.enter_context(nc.Block())

        @block.sync
        def _(sp):
            sp.dma_start(e_dst, dst.rearrange("(g e) -> g e", e=GROUP)).then_inc(S["edges"], 16)
            sp.dma_start(e_src, src.rearrange("(g e) -> g e", e=GROUP)).then_inc(S["edges"], 16)
            sp.dma_start(xTraw, xT.rearrange("(k p) n -> p k n", p=P)).then_inc(S["xT_in"], 16)
            sp.dma_start(w0raw, W0.rearrange("(k p) n -> p k n", p=P)).then_inc(S["w_in0"], 16)
            sp.dma_start(b0f, b0.rearrange("(a d) -> a d", a=1)).then_inc(S["small_in"], 16)
            sp.dma_start(dwb[:], dw.rearrange("(a d) -> a d", a=1).broadcast_to([P, STEPS + 1])).then_inc(S["small_in"], 16)
            sp.dma_start(xcur[:], x.rearrange("(t p) d -> p t d", p=P)).then_inc(S["x_in"], 16)
            for i, b in enumerate((b1, b2, b3)):
                sp.dma_start(bb[:, i, :], b.rearrange("(a d) -> a d", a=1).broadcast_to([P, D])).then_inc(S["small_in"], 16)
            sp.dma_start(wbc[:], b3T).then_inc(S["small_in"], 16)
            sp.dma_start(abc[:], ab.rearrange("(h a) -> h a", a=1)).then_inc(S["small_in"], 16)
            sp.wait_ge(S["const_ready"], 9)
            step = VCOL + H + 2
            flat = abT[:].rearrange("p k c -> p (k c)")
            for q in range(2):
                for u in range(2):
                    c0 = VCOL * u + q
                    sp.dma_start(flat[q * DH:(q + 1) * DH, c0:c0 + 3 * step + 1:step],
                                 aw.rearrange("(j q) (u p) -> q u p j", q=2, p=DH)[q, u],
                                 allow_slow_non_contiguous=True).then_inc(S["small_in"], 16)
            sp.wait_ge(S["h_done"], NT)
            for n, w in enumerate((W1T, wc, wn, W3, W3T)):
                if n >= 2:
                    sp.wait_ge(S["w_lo"], n)
                sp.dma_start(stage[:, n % 2], w.rearrange("(k p) n -> p k n", p=P)).then_inc(S[f"w_in{n + 1}"], 16)
            for t in range(NT):
                sp.wait_ge(S["out_odd" if t % 2 else "out_even"], t // 2 + 1)
                sp.dma_start(out.rearrange("(t p) d -> t p d", p=P)[t], xcur[:, t, :]).then_inc(S["out_done"], 16)
            sp.wait_ge(S["out_done"], 16 * NT)
        SMALL = 16 * 11

        @block.gpsimd
        def _(pool):
            pool.iota(iota_lo[:], [[1, P]], base=0, channel_multiplier=0,
                      allow_small_or_imprecise_dtypes=True).then_inc(S["const_ready"], 1)
            pool.iota(iota_key[:], [[1, KEYS]], base=0, channel_multiplier=0,
                      allow_small_or_imprecise_dtypes=True).then_inc(S["const_ready"], 1)
            pool.memset(id32[:], 0.0).then_inc(S["const_ready"], 1)
            pool.memset(id16[:], 0.0).then_inc(S["const_ready"], 1)
            pool.memset(sel[:], 0.0).then_inc(S["const_ready"], 1)
            pool.memset(ones16[:], 1.0).then_inc(S["const_ready"], 1)
            pool.memset(epsc[:], EPS).then_inc(S["const_ready"], 1)
            pool.memset(ln16[:], LN16).then_inc(S["const_ready"], 1)
            pool.memset(abT[:], 0.0).then_inc(S["const_ready"], 1)
            pool.wait_ge(S["const_ready"], 9)
            for ident in (id32, id16):
                pool.affine_select(out=ident[:], in_=ident[:], compare_op=ALU.not_equal, fill=1.0, base=0,
                                   pattern=[[-1, P]], channel_multiplier=1).then_inc(S["const_ready"], 1)
            pool.affine_select(out=sel[:], in_=sel[:], compare_op=ALU.not_equal, fill=1.0, base=0,
                               pattern=[[-1, H + 1], [0, P]], channel_multiplier=1).then_inc(S["const_ready"], 1)
            pool.memset(c32[:, NT // 2:NT, :], 0.0).then_inc(S["c32z"], 1)

            def split_lo(n, name, raw):
                pool.wait_ge(S["w_hi"], n + 1)
                pool.tensor_tensor(ws[:, SLOT[name], 1], raw, ws[:, SLOT[name], 0], ALU.subtract).then_inc(S["w_lo"], 1)

            def source_hots(t):
                for half in range(0, NT, NT // 2):
                    part = slice(half, half + NT // 2)
                    if not (isinstance(t, int) and t == 0):
                        pool.wait_ge(S["hot_free"], t * NT + (half - 2))
                    pool.tensor_copy(slo_g[:, :, part], slo[:, :, bass.ds(t * NT + half, NT // 2)]).then_inc(S["slo_g"], 1)
                    pool.drain()
                    for i in range(half, half + NT // 2):
                        if i % 2:
                            pool.tensor_scalar(oh_lo0[:, i // 2, :], iota_lo[:], slo_g[:, 0, i:i + 1], None,
                                               ALU.is_equal).then_inc(S["lo_ready"], 1)
                        pool.tensor_scalar(oh_lo1[:, i, :], iota_lo[:], slo_g[:, 1, i:i + 1], None,
                                           ALU.is_equal).then_inc(S["lo_ready"], 1)

            def h_lower(t):
                pool.wait_ge(S["h_cp"], t + 2)
                settle(pool)
                pool.tensor_tensor(cur[:, 0, 1, t, :], hb, cur[:, 0, 0, t, :],
                                   ALU.subtract).then_inc(S["h_lo"], 1)
                pool.tensor_tensor(acc[:, t, :], hb, dwb[:, 0:1].broadcast_to([P, D]), ALU.mult).then_inc(S["acc0"], 1)

            pool.wait_ge(S["key_in"], 5)
            source_hots(0)
            source_hots(1)
            pool.wait_ge(S["xT_hi"], 1)
            pool.tensor_tensor(xTs[:, 1, 0:KT // 2], xTraw[:, 0:KT // 2], xTs[:, 0, 0:KT // 2], ALU.subtract).then_inc(S["xT_lo"], 1)
            split_lo(0, "W0", w0raw)
            pool.wait_ge(S["b0_ready"], 2)
            pool.tensor_tensor(b0s[:, 1, :], b0f, b0s[:, 0, :], ALU.subtract).then_inc(S["b0_ready"], 1)
            pool.wait_ge(S["small_in"], SMALL)
            source_hots(2)
            source_hots(3)
            with pool.Fori(1, HT) as r:
                h_lower(r - 1)
                source_hots(r * 2 + 2)
                source_hots(r * 2 + 3)
            with pool.Fori(HT - 1, NT) as t:
                h_lower(t)
            for n, name in enumerate(("W1", "wc", "wn", "W3")):
                split_lo(n + 1, name, stage[:, n % 2])

            for layer in range(3):
                with pool.Fori(0, NT) as t:
                    pool.wait_ge(S["x_ready"], t + (layer * NT + 1))
                    settle(pool)
                    pool.tensor_tensor(cur[:, 1, 1, t, :], xcur[:, t, :], cur[:, 1, 0, t, :],
                                       ALU.subtract).then_inc(S["x_lo"], 1)
                    if layer < 2:
                        pool.tensor_tensor(xcur[:, t, :], xcur[:, t, :], bb[:, layer, :],
                                           ALU.add).then_inc(S["xb_ready"], 1)
                if layer == 1:
                    pool.wait_ge(S["gather1_done"], NT)
                    for t in range(NT):
                        pool.tensor_scalar(cst[:, t, :], cst[:, t, :], -1.0, None, ALU.mult).then_inc(S["neg_ready"], 1)
            with pool.Fori(0, NT // 2) as r:
                for i in range(2):
                    t = r * 2 + i
                    pool.wait_ge(S["y_hi"], t + 1)
                    settle(pool)
                    pool.tensor_tensor(yh[:, t, 1], yf[:, i].rearrange("p h e d -> p h (e d)"), yh[:, t, 0],
                                       ALU.subtract).then_inc(S["y_lo"], 1)

            pool.wait_ge(S["mode"], 1)
            with pool.If(flag(pool, 2)):
                pool.wait_ge(S["wx_in"], NT + 2)
                pool.wait_ge(S["uf_ready"], 2)
                pool.memset(wxh[:, :, :, DH:DH + 1], 1.0).then_inc(S["ones_wxh"], 1)
                pool.wait_ge(S["ones_wxh"], 1)
                with pool.Fori(0, H // 2) as hp:
                    for q in range(2):
                        h = hp * 2 + q
                        pool.wait_ge(S["back_done"], h + 1)
                        pool.tensor_copy(wxh[:, q, :, 0:DH], wx[:, :, bass.ds(h * DH, DH)]).then_inc(S["wxh_ready"], 1)
            with pool.Else():
                def attend(h, q):
                    pool.wait_ge(S["att_in"], h + 2)
                    pool.wait_ge(S["den_ready"], h * 2 + 2)
                    settle(pool)
                    pool.tensor_tensor(attf, comb[:, q, 0:NT, 0:DH],
                                       rdf[:, q, 0:NT].unsqueeze(2).broadcast_to([P, NT, DH]),
                                       ALU.mult).then_inc(S["att_ready"], 1)
                    pool.wait_ge(S["att_ready"], h + 1)
                    settle(pool)
                    xs = xcur[:, :, bass.ds(h * DH, DH)]
                    pool.tensor_tensor(xs, xs, attf, ALU.add).then_inc(S["att_in"], 1)
                with pool.Fori(0, H // 2 - 1) as hp:
                    for q in range(2):
                        attend(hp * 2 + q, q)
                attend(H - 2, 0)

        @block.scalar
        def _(act):
            def copy(o, i, scale=1.0, **kw):
                return act.activation(o, i, ACT.Copy, scale=scale, **kw)

            act.wait_ge(S["xT_in"], 16)
            copy(xTs[:, 0], xTraw).then_inc(S["xT_hi"], 1)

            def split_hi(n, name, raw):
                act.wait_ge(S[f"w_in{n}"], 16)
                copy(raw, raw, WSCALE).then_inc(S["w64"], 1)
                act.wait_ge(S["w64"], n + 1)
                copy(ws[:, SLOT[name], 0], raw).then_inc(S["w_hi"], 1)
            split_hi(0, "W0", w0raw)
            act.wait_ge(S["small_in"], SMALL)
            copy(b0f, b0f, WSCALE).then_inc(S["b0_ready"], 1)
            act.wait_ge(S["b0_ready"], 1)
            copy(b0s[:, 0, :], b0f).then_inc(S["b0_ready"], 1)
            act.sem_inc(S["h_cp"], 1)
            act.sem_inc(S["h_lo"], 1)

            def h_upper(t, bank):
                act.wait_ge(S["h_done"], t + 1)
                copy(cur[:, 0, 0, t, :], ps[:, bank, :], 1 / WSCALE).then_inc(S["h_hi"], 1)
                act.wait_ge(S["acc0"], t + 1)
                copy(hb, ps[:, bank, :], 1 / WSCALE).then_inc(S["h_cp"], 1)

            with act.Fori(0, HT) as t:
                h_upper(t, 2)
            act.wait_ge(S["counted"], 1)
            for j in range(CA):
                copy(cst[:, j, :], c32[:, j, :]).then_inc(S["cst_ready"], 1)
            for t in range(HT, NT - 2):
                h_upper(t, t - 1)
            for r in range(2):
                for a in range(NT // 2):
                    act.wait_ge(S["ct_done"], r * (NT // 2) + (a + 1))
                    copy(cts[:, r * (NT // 2) + a, :], bank16(a % 2)).then_inc(S["cts_ready"], 1)
                h_upper(r + (NT - 2), r + (NT - 3))

            act.wait_ge(S["inv_r"], 1)
            for k in range(1, STEPS):
                for n in (2 * k - 1, 2 * k):
                    split_hi(n, ("W1", "wc", "wn", "W3")[n - 1], stage[:, (n - 1) % 2])
                with act.Fori(0, NT) as t:
                    act.wait_ge(S["step_done"], t + ((k - 1) * NT + 1))
                    copy(cur[:, k % 2, 0, t, :], ps[:, t, :], invdeg[:, bass.ds(t, 1)]).then_inc(S["step_hi"], 1)

            def norm(layer, t, i):
                n = t + (layer * NT + 1)
                act.wait_ge(S["moments"], n)
                act.activation(std[:, bass.ds(t, 1)], mv[:, i, 1:2], ACT.Sqrt, bias=epsc[:]).then_inc(S["std_ready"], 1)
                act.wait_ge(S["nmr_ready"], n)
                r, b = rstd[:, bass.ds(t, 1)], nmr[:, bass.ds(t, 1)]
                if layer < 3:
                    act.activation(cur[:, 1, 0, t, :], xcur[:, t, :], ACT.Identity, bias=b, scale=r).then_inc(S["x_hi"], 1)
                act.activation(xcur[:, t, :], xcur[:, t, :], ACT.Identity, bias=b, scale=r).then_inc(S["x_ready"], 1)

            def xT_evict(layer, t, i):
                act.wait_ge(S["xT_done"], t + (layer * NT + 1))
                copy(xTs[:, :, :, bass.ds(t * P, P)].rearrange("p v k n -> p (v k) n"),
                     bank16(i).rearrange("p (a n) -> p a n", n=P)).then_inc(S["xT_in2"], 1)

            def z_hi(layer, t, i):
                if layer == 2:
                    act.wait_ge(S["uvc_done"], t + 1)
                    act.wait_ge(S["y_lo"], t + 1)
                    for e, f in enumerate((1.0, SLOPE)):
                        act.activation(yf[:, i, :, e, DH], ps[:, 2 + i, VCOL:VCOL + H], ACT.Exp, scale=f / WSCALE,
                                       bias=ln16[:]).then_inc(S["exp_in"], 1)
                    act.wait_ge(S["y_ready3"], t + 1)
                    copy(yh[:, t, 0], yf[:, i].rearrange("p h e d -> p h (e d)")).then_inc(S["y_hi"], 1)
                else:
                    act.wait_ge(S["z_done"], t + (layer * NT + 1))
                    copy(cur[:, 0, 0, t, :], ps[:, 4 + i, :], 1 / WSCALE).then_inc(S["z_hi"], 1)

            act.activation(std[:, 0:1], epsc[:], ACT.Sqrt).then_inc(S["warm"], 1)
            act.wait_ge(S["warm"], 1)
            for layer in range(3):
                with act.Fori(0, NT // 2 - 2) as r:
                    for i in range(2):
                        norm(layer, r * 2 + i, i)
                norm(layer, NT - 4, 0)
                if layer == 0:
                    act.wait_ge(S["wa_done"], 1)
                xT_evict(layer, 0, 0)
                xT_evict(layer, 1, 1)
                norm(layer, NT - 3, 1)
                xT_evict(layer, 2, 0)
                if layer < 2:
                    z_hi(layer, 0, 0)
                norm(layer, NT - 2, 0)
                norm(layer, NT - 1, 1)
                if layer == 2:
                    act.activation(std[:, 0:1], epsc[:], ACT.Exp).then_inc(S["warm"], 1)
                    act.wait_ge(S["warm"], 2)
                    z_hi(layer, 0, 0)
                with act.Fori(0, NT // 2 - 2) as r:
                    for i in (1, 0):
                        t = r * 2 + (2 - i)
                        z_hi(layer, t, i)
                        xT_evict(layer, t + 2, i)
                xT_evict(layer, NT - 1, 1)
                z_hi(layer, NT - 3, 1)
                z_hi(layer, NT - 2, 0)
                if layer < 2:
                    z_hi(layer, NT - 1, 1)

            act.sem_inc(S["e_ready"], 2)
            act.wait_ge(S["uv_in"], 1)
            act.activation(qrow, z0, ACT.Exp, scale=1 - SLOPE).then_inc(S["q_row"], 1)

            def uf_evict(h, q):
                act.wait_ge(S["uf_done"], h + 1)
                act.wait_ge(S["cz_ready"], h * NT + NT)
                copy(uf[:, q], ps[:, 0:2, :].rearrange("p a n -> p (a n)")).then_inc(S["uf_ready"], 1)

            def y_head(h, q):
                act.wait_ge(S["head_done"], h + 1)
                copy(yq[q], yh[:, :, :, bass.ds(h, 1), :].rearrange("p t v h n -> p t v (h n)")).then_inc(S["yq_ready"], 1)

            act.wait_ge(S["uf_done"], 1)
            copy(uf0, ps[:, 0:2, :].rearrange("p a n -> p (a n)")).then_inc(S["uf_ready"], 1)
            z_hi(2, NT - 1, 1)
            act.wait_ge(S["wx_done"], NT)
            uf_evict(1, 1)
            act.wait_ge(S["y_lo"], NT + 2)
            y_head(0, 0)
            y_head(1, 1)
            act.wait_ge(S["mode"], 1)
            with act.If(flag(act, 2)):
                def u_copy(h, q):
                    act.wait_ge(S["u_done"], h + 1)
                    copy(ub[:, q], ps[:, 0:4, :].rearrange("p (v a) n -> p v (a n)", v=2)).then_inc(S["ub_ready"], 1)

                def exps(h, q, j):
                    n = h * NT + j
                    act.wait_ge(S["t_ready"], n + 1)
                    act.wait_ge(S["p_ready"], n + 1)
                    act.activation(EX[:, j % 2, :], T[:, j % 2, :], ACT.Exp,
                                   bias=vc[:, 1, bass.ds(j * H + h, 1)]).then_inc(S["e_ready"], 1)

                def o_evict(h):
                    act.wait_ge(S["p_free"], h * NT + (NT + 2))
                    act.wait_ge(S["back_done"], h + 2)
                    copy(oT, ps[0:DH + 1, 4:6, :].rearrange("p a n -> p (a n)")).then_inc(S["oT_in"], 1)

                u_copy(0, 0)
                with act.Fori(0, H // 2) as hp:
                    for q in range(2):
                        h = hp * 2 + q
                        for j in range(NT):
                            exps(h, q, j)
                            if j == 3:
                                u_copy(h + 1, 1 - q)
                        o_evict(h)
            with act.Else():
                with act.Fori(0, H // 2 - 1) as hp:
                    for q in range(2):
                        h = hp * 2 + q
                        uf_evict(h + 2, q)
                        y_head(h + 2, q)
            act.activation(std[:, 0:1], epsc[:], ACT.Sqrt).then_inc(S["warm"], 1)
            act.wait_ge(S["warm"], 3)
            act.wait_ge(S["mv8_in"], NT)
            act.activation(std[:], mv8[:, :, 1], ACT.Sqrt, bias=epsc[:]).then_inc(S["std8"], 1)
            act.wait_ge(S["scale8"], 1)
            for t in range(0, NT, 2):
                act.activation(xcur[:, t, :], xcur[:, t, :], ACT.Identity, bias=nmr[:, t:t + 1], scale=rstd[:, t:t + 1]).then_inc(S["out_even"], 1)

        @block.tensor
        def _(pe):
            mm = pe.matmul

            def three(bank, lhs, rhs, start=True, stop=True):
                for k in range(KT):
                    for n in range(3):
                        ins = part(bank, lhs, rhs, k, n, start, stop)
                return ins

            def part(bank, lhs, rhs, k, n, start=True, stop=True):
                a, b = ((0, 0), (0, 1), (1, 0))[n]
                return mm(bank, lhs(k)[a], rhs(k)[b], start=start and k == 0 and n == 0,
                          stop=stop and k == KT - 1 and n == 2)

            def cols(buf, t):
                return lambda k: [buf[:, v, k, bass.ds(t * P, P)] for v in range(2)]

            def weight(name):
                return lambda k: [ws[:, SLOT[name], v, k, :] for v in range(2)]

            pe.sem_inc(S["hot_free"], 2)
            pe.sem_inc(S["cts_ready"], 2)
            pe.sem_inc(S["p_free"], 2)
            pe.sem_inc(S["back_done"], 2)
            pe.wait_ge(S["const_ready"], 12)
            pe.wait_ge(S["idx"], 3)
            for c in range(NC):
                pe.transpose(ps[:, 2, c * NG:(c + 1) * NG], f_lo[:, c * P:(c + 1) * P], id32[0:NG, 0:NG])
                pe.transpose(ps[:, 3, c * NG:(c + 1) * NG], f_key[:, c * P:(c + 1) * P], id32[0:NG, 0:NG])
                pe.transpose(ps[:, 5, c * NG:(c + 1) * NG], f_far[:, c * P:(c + 1) * P], id32[0:NG, 0:NG])
            pe.transpose(ps[0:1, 4, NG:2 * NG], far_at[0:NG, 0:1], id32[0:NG, 0:NG])
            pe.transpose(ps[0:1, 4, 0:NG], base[:, 0:1], id32[0:NG, 0:NG]).then_inc(S["tr"], 1)

            pe.wait_ge(S["key_in"], 5)
            xw = [(k, n) for k in range(KT) for n in range(3)]

            def h_part(t, bank, n):
                part(ps[:, bank, :], cols(xTs, t), weight("W0"), *xw[n], stop=False)
                if n == len(xw) - 1:
                    for v in range(2):
                        ins = mm(ps[:, bank, :], ones16[0:1, :], b0s[:, v, :], start=False, stop=v == 1)
                    ins.then_inc(S["h_done"], 1)

            def groups(t, h_tile=None, first=0):
                for i in range(NT):
                    g = t * NT + i
                    pe.wait_ge(S["lo_ready"], t * (NT // 2 * 3) + (i // 2 * 3 + (3 if i % 2 else 1)))
                    pe.wait_ge(S["key_ready"], t * (NT // 2 * 5) + (i // 2 * 5 + (5 if i % 2 else 3)))
                    pe.wait_ge(S["win_free"], g + 1)
                    for c in range(NC):
                        b = i % 2 * NC + c
                        ins = mm(ps[:, i % 2, 0:KEYS], oh_lo1[:, i, :] if c else oh_lo0[:, i // 2, :] if i % 2 else oh_lo[:, b, :], oh_key[:, b, :], start=c == 0, stop=c == NC - 1)
                    ins.then_inc(S["hot_free"], 1)
                    if h_tile is not None and first + i < len(xw):
                        if first + i == 0:
                            pe.wait_ge(S["h_cp"], h_tile + 1)
                        h_part(h_tile, 2, first + i)

            groups(0)
            groups(1)
            pe.wait_ge(S["xT_lo"], 2)
            pe.wait_ge(S["w_lo"], 1)
            pe.wait_ge(S["b0_ready"], 3)
            with pe.Fori(0, HT) as r:
                groups(r * 2 + 2, r)
                groups(r * 2 + 3, r, NT)
            for t in range(HT, NT - 2):
                for n in range(len(xw)):
                    if t == HT and n == 0:
                        pe.wait_ge(S["h_cp"], t + 1)
                    h_part(t, t - 1, n)

            pe.wait_ge(S["far_in"], 3)
            with pe.If(flag(pe, 0)):
                pe.wait_ge(S["win_free"], NG + 2)
                pe.wait_ge(S["far_iota"], NT)
                pe.sem_inc(S["far_free"], 1)
                with pe.Fori(0, NT) as a:
                    for b in range(2):
                        mm(ps[:, b, :], sel[:, H, :], iota_n[0:H, 0:HALF], start=True, stop=False)
                    with pe.Fori(0, NC * (NG + 1)) as e:
                        n = a * (NC * (NG + 1)) + e
                        pe.wait_ge(S["far_hot"], n * 2 + 2)
                        for b in range(2):
                            ins = mm(ps[:, b, :], oh_lo[:, 0, :], oh_far[:, b * HALF:(b + 1) * HALF], start=False, stop=False)
                        ins.then_inc(S["far_free"], 1)
                    for b in range(2):
                        ins = mm(ps[:, b, :], sel[:, H, :], iota_n[0:H, 0:HALF], start=False, stop=True)
                    ins.then_inc(S["far_done"], 1)
                    pe.wait_ge(S["far_added"], a * 2 + 2)
            pe.wait_ge(S["cst_ready"], NT)
            pe.wait_ge(S["win_free"], NG + 2)
            with pe.Fori(0, 2) as r:
                for a in range(NT // 2):
                    t = r * (NT // 2) + a
                    pe.wait_ge(S["cts_ready"], t + 1)
                    for j in range(NT):
                        ins = pe.transpose(bank16(a % 2)[:, j * P:(j + 1) * P], cst[:, j, bass.ds(t * P, P)], id16[:])
                    ins.then_inc(S["ct_done"], 1)
                    for n in range(3 * a, 3 * a + 3):
                        h_part(r + (NT - 2), r + (NT - 3), n)
            pe.wait_ge(S["adj_ready"], NT)
            pe.wait_ge(S["cts_ready"], NT + 2)
            for t in range(NT):
                for j in range(NT):
                    ins = mm(ps[:, 7, t:t + 1], adj[:, j, t * P:(t + 1) * P], ones16[:, 0:1],
                             start=j == 0, stop=j == NT - 1)
            ins.then_inc(S["deg_done"], 1)

            def transposes(layer, t, i):
                pe.wait_ge(S["x_lo"], t + (layer * NT + 1))
                for v in range(2):
                    for k in range(KT):
                        a = v * KT + k
                        ins = pe.transpose(bank16(i)[:, a * P:(a + 1) * P], cur[:, 1, v, t, k * P:(k + 1) * P], id16[:])
                ins.then_inc(S["xT_done"], 1)

            def attention_vectors():
                pe.wait_ge(S["w_in5"], 16)
                pe.wait_ge(S["small_in"], SMALL)
                for k in range(KT):
                    for j in range(KT):
                        mm(ps[:, 7, k * 64:k * 64 + VCOL + H], stage[:, 0, j, k * P:(k + 1) * P], abT[:, j, :],
                           start=j == 0, stop=j == KT - 1)
                for v in range(2):
                    for j in range(KT):
                        ins = mm(ps[0:H, 7, 256:257], abT[:, j, VCOL * v:VCOL * v + H], wbc[:, j:j + 1],
                                 start=v == 0 and j == 0, stop=v == 1 and j == KT - 1)
                pe.transpose(ps[0:1, 7, 320:320 + P], far_at[:, 1:2], id32[:]).then_inc(S["wa_done"], 1)

            pe.wait_ge(S["h_lo"], NT + 1)
            pe.wait_ge(S["h_hi"], NT)
            for k in range(1, STEPS + 1):
                def step(t, first):
                    for j in range(NT):
                        if first and k > 1:
                            pe.wait_ge(S["step_lo"], (k - 2) * NT + j + 1)
                        for v in range(2):
                            ins = mm(ps[:, t, :], adj[:, j, bass.ds(t * P, P)], cur[:, (k - 1) % 2, v, j, :],
                                     start=j == 0 and v == 0, stop=j == NT - 1 and v == 1)
                    ins.then_inc(S["step_done"], 1)
                def free(t):
                    if k > 1:
                        pe.wait_ge(S["acc_r"], t + ((k - 2) * NT + 1))
                free(0)
                step(0, True)
                if k == STEPS:
                    free(NT - 1)
                    attention_vectors()
                with pe.Fori(1, NT - 1) as t:
                    free(t)
                    step(t, False)
                if k == 1:
                    pe.wait_ge(S["inv_r"], 1)
                elif k == STEPS:
                    pe.wait_ge(S["wa_lo"], 1)
                    pe.wait_ge(S["crow_r"], 1)
                    pe.wait_ge(S["big_in"], 1)
                    transposes(0, 0, 0)
                    transposes(0, 1, 1)
                free(NT - 1)
                step(NT - 1, False)

            def per_tile(layer, products, before_last=None):
                pe.wait_ge(S["y_ready"], layer * NT + 6)
                products(0, 0)
                with pe.Fori(0, NT // 2 - 2) as r:
                    for i in (1, 0):
                        t = r * 2 + (2 - i)
                        transposes(layer, t + 1, 1 - i)
                        products(t, i)
                transposes(layer, NT - 2, 0)
                pe.wait_ge(S["xT_in2"], layer * NT + NT - 2)
                transposes(layer, NT - 1, 1)
                products(NT - 3, 1)
                if before_last is not None:
                    before_last()
                products(NT - 2, 0)

            def product(layer, name, bank, done, free, n, t):
                pe.wait_ge(S["xT_in2"], t + (layer * NT + 1))
                pe.wait_ge(S[free], n)
                three(ps[:, bank, :], cols(xTs, t), weight(name)).then_inc(S[done], 1)

            def gather(layer, c16, left, done):
                pe.wait_ge(S["xT_in2"], (layer + 1) * NT)
                pe.wait_ge(S["y_ready"], (layer + 1) * NT)

                def tile(t, parts, first=False):
                    for c in parts:
                        for j in range(NT):
                            if first:
                                pe.wait_ge(S["z_lo"], layer * NT + j + 3)
                            for v in range(2):
                                ins = mm(ps[:, t, :], c[:, j, bass.ds(t * P, P)], cur[:, 0, v, j, :],
                                         start=c is c16 and j == 0 and v == 0,
                                         stop=c is parts[-1] and j == NT - 1 and v == 1)
                    ins.then_inc(S[done], 1)

                def tiles(parts):
                    tile(0, parts, True)
                    with pe.Fori(1, NT - 1) as t:
                        tile(t, parts)
                    transposes(layer + 1, 0, 0)
                    transposes(layer + 1, 1, 1)
                    tile(NT - 1, parts)

                pe.wait_ge(S["big_in"], 1)
                with pe.If(flag(pe, 1)):
                    if layer == 0:
                        pe.wait_ge(S["left_in"], NT)
                        with pe.Fori(0, NT) as t:
                            pe.wait_ge(S["left_t"], t + 1)
                            for j in range(NT):
                                ins = pe.transpose(bank16(7)[:, j * P:(j + 1) * P], c_left[:, j, bass.ds(t * P, P)], id16[:])
                            ins.then_inc(S["left_done"], 1)
                        pe.wait_ge(S["left_t"], NT + 1)
                    tiles((c16, left))
                with pe.Else():
                    tiles((c16,))

            def products1(t, i):
                product(0, "W1", 4 + i, "z_done", "z_lo", t + 1, t)
            per_tile(0, products1)
            products1(NT - 1, 1)
            gather(0, cst, c_left, "gather1_done")

            def products2(t, i):
                product(1, "wc", 2 + i, "alpha_done", "alpha_in", t + 1, t)
                product(1, "wn", 4 + i, "z_done", "z_lo", t + (NT + 1), t)
            per_tile(1, products2)
            products2(NT - 1, 1)
            pe.wait_ge(S["alpha_in"], NT + 2)
            gather(1, cts, ct_left, "gather2_done")

            def products3(t, i):
                product(2, "W3", 4 + i, "wx_done", "wx_in", t + 1, t)
                pe.wait_ge(S["nv_in"], t + 1)
                pe.wait_ge(S["exp_in"], t * 2 + 2)
                three(ps[:, 2 + i, 0:VCOL + H], cols(xTs, t), lambda k: [wa[:, v, k, :] for v in range(2)]).then_inc(S["uvc_done"], 1)

            def uf_spread(h):
                for a in range(2):
                    for v in range(2):
                        ins = mm(ps[:, a, :], sel[:, h, :], usf[:, v, a * HALF:(a + 1) * HALF], start=v == 0, stop=v == 1)
                ins.then_inc(S["uf_done"], 1)

            def scores_rows():
                pe.wait_ge(S["xT_in2"], 3 * NT)
                pe.wait_ge(S["y_ready"], 3 * NT)
                for half in range(2):
                    ins = three(ps[0:VCOL + H, 6 + half, :], lambda k: [wa[:, v, k, :] for v in range(2)],
                                lambda k: [xTs[:, v, k, half * HALF:(half + 1) * HALF] for v in range(2)])
                ins.then_inc(S["uv_done"], 1)

            pe.wait_ge(S["wa_lo"], 1)
            per_tile(2, products3, scores_rows)
            pe.wait_ge(S["usf_in"], 2)
            uf_spread(0)
            products3(NT - 1, 1)
            pe.wait_ge(S["uf_ready"], 1)
            uf_spread(1)
            pe.wait_ge(S["q_row"], 1)
            pe.wait_ge(S["nv_in"], NT - 1 + 2)
            pe.wait_ge(S["exp_in"], 2 * (NT - 1) + 2)
            for t in range(NT):
                ins = pe.transpose(ps[:, 2, t * H:(t + 1) * H], qrow[:, t * P:(t + 1) * P], id32[0:H, 0:H])
            ins.then_inc(S["q_done"], 1)
            pe.wait_ge(S["lim_in"], 1)
            pe.transpose(ps[0:1, 3, P:2 * P], lim[:, 0:1], id32[:]).then_inc(S["lim_done"], 1)
            pe.wait_ge(S["mode"], 1)
            with pe.If(flag(pe, 2)):
                pe.wait_ge(S["wx_in"], NT + 2)
                pe.wait_ge(S["uf_ready"], 2)
                pe.wait_ge(S["w_row"], 1)
                for j in range(NT):
                    ins = pe.transpose(ps[:, 0, j * H:(j + 1) * H], wrow[:, j * P:(j + 1) * P], id32[0:H, 0:H])
                ins.then_inc(S["w_done"], 1)
                with pe.Fori(0, H) as h:
                    pe.wait_ge(S["most_ready"], h + 1)
                    for t in range(NT):
                        ins = pe.transpose(ps[:, 2 + t // 4, t % 4 * P:(t % 4 + 1) * P], most[:, t * P:(t + 1) * P], id32[:])
                    ins.then_inc(S["most_done"], 1)
                pe.wait_ge(S["most_in"], H)
                for t in range(NT):
                    ins = pe.transpose(ps[0:H, t // 4, t % 4 * P:(t % 4 + 1) * P], mcol[:, t, :], id32[:])
                ins.then_inc(S["m_done"], 1)
                pe.wait_ge(S["m_in"], 1)
                for j in range(NT):
                    ins = pe.transpose(ps[:, 0, j * H:(j + 1) * H], vrow[:, j * P:(j + 1) * P], id32[0:H, 0:H])
                ins.then_inc(S["v_done"], 1)
                def u_spread(h):
                    for a in range(4):
                        for v in range(2):
                            ins = mm(ps[:, a, :], sel[:, h, :], us[:, v, a // 2, a % 2 * HALF:(a % 2 + 1) * HALF],
                                     start=v == 0, stop=v == 1)
                    ins.then_inc(S["u_done"], 1)

                def back(h):
                    pe.wait_ge(S["oT_in"], h + 1)
                    pe.wait_ge(S["back_free"], h + 1)
                    for t in range(NT):
                        ins = pe.transpose(ps[:, 6 + t // 4, t % 4 * (DH + 1):(t % 4 + 1) * (DH + 1)],
                                           oT[:, t * P:(t + 1) * P], id32[0:DH + 1, 0:DH + 1])
                    ins.then_inc(S["back_done"], 1)

                pe.wait_ge(S["us_lo"], 1)
                pe.wait_ge(S["wx_in"], NT + 2)
                pe.wait_ge(S["vc_ready"], 2)
                u_spread(0)
                with pe.Fori(0, H // 2) as hp:
                    for q in range(2):
                        h = hp * 2 + q
                        pe.wait_ge(S["wxh_ready"], h + 1)
                        for j in range(NT):
                            pe.wait_ge(S["p_ready"], h * NT + (j + 3))
                            for half in range(2):
                                ins = mm(ps[0:DH + 1, 4 + half, :], wxh[:, q, j, :], PR[:, j % 2, half * HALF:(half + 1) * HALF],
                                         start=j == 0, stop=j == NT - 1)
                            ins.then_inc(S["p_free"], 1)
                            if j == 2:
                                pe.wait_ge(S["ub_ready"], h + 1)
                                u_spread(h + 1)
                        back(h)
            with pe.Else():
                pe.wait_ge(S["wx_in"], NT + 2)
                pe.wait_ge(S["uv_in"], 1)
                for b in (4, 7):
                    mm(ps[:, b, 2 * YW:3 * YW], sel[:, H, :], usf[:, 0, 0:YW], start=True, stop=True)
                pe.wait_ge(S["y_lo"], NT + 2)
                pe.wait_ge(S["y_hi"], NT)
                pe.wait_ge(S["neg_ready"], NT)
                pe.wait_ge(S["q_in"], 1)

                def head(h, q, following):
                    if following:
                        pe.wait_ge(S["uf_ready"], h + 2)
                        uf_spread(h + 2)
                    pe.wait_ge(S["cz_ready"], h * NT + 3 * NT)
                    pe.wait_ge(S["comb_ready"], h * 2 + 2)
                    pe.wait_ge(S["yq_ready"], h + 1)
                    for t in range(NT):
                        o = ps[:, 2 + 3 * q + t // 3, t % 3 * YW:(t % 3 + 1) * YW]
                        for j in range(NT):
                            for v in range(2):
                                mm(o, cz[q][:, j, t * P:(t + 1) * P], yq[q][:, j, v, :],
                                   start=j == 0 and v == 0, stop=False)
                            for v in range(2):
                                ins = mm(o[:, DH + 1:YW], cst[:, j, t * P:(t + 1) * P], yq[q][:, j, v, DH + 1:YW],
                                         start=False, stop=j == NT - 1 and v == 1)
                    ins.then_inc(S["head_done"], 1)
                with pe.Fori(0, H // 2 - 1) as hp:
                    for q in range(2):
                        head(hp * 2 + q, q, True)
                head(H - 2, 0, False)
                head(H - 1, 1, False)

        @block.vector
        def _(dve):
            stt, ts, tt = dve.scalar_tensor_tensor, dve.tensor_scalar, dve.tensor_tensor
            dve.sem_inc(S["win_free"], 2)
            dve.sem_inc(S["acc0"], 1)
            dve.sem_inc(S["p_ready"], 2)
            dve.sem_inc(S["back_free"], 1)
            dve.sem_inc(S["z_lo"], 2)
            dve.sem_inc(S["alpha_in"], 2)
            dve.sem_inc(S["wx_in"], 2)
            dve.sem_inc(S["left_t"], 1)
            dve.sem_inc(S["y_lo"], 2)
            dve.sem_inc(S["nv_in"], 2)
            dve.sem_inc(S["exp_in"], 4)
            dve.sem_inc(S["cz_ready"], 2 * NT)
            dve.sem_inc(S["comb_ready"], 4)
            dve.sem_inc(S["att_in"], 2)
            dve.sem_inc(S["head_done"], 2)
            dve.sem_inc(S["most_free"], 1)
            links = [0]

            def link(ins):
                links[0] += 1
                ins.then_inc(S["link"], 1)
                dve.wait_ge(S["link"], links[0])

            dve.memset(c32[:, 0:NT // 2, :], 0.0).then_inc(S["c32z"], 1)
            dve.memset(key[:, :, NG:NG + 1], -1.0).then_inc(S["key_in"], 1)
            dve.memset(slo[:, :, NG:NG + 1], -1.0).then_inc(S["key_in"], 1)
            dve.memset(far[:, :, NG:NG + 1], -1.0).then_inc(S["far_in"], 1)
            dve.wait_ge(S["edges"], 32)
            ts(i_hi, e_src, 7, None, ALU.arith_shift_right).then_inc(S["ints"], 1)
            ts(i_lo, e_src, P - 1, None, ALU.bitwise_and).then_inc(S["ints"], 1)
            link(dve.tensor_copy(f_dst, e_dst))
            dve.wait_ge(S["ints"], 2)
            dve.tensor_copy(f_lo, i_lo).then_inc(S["idx"], 1)
            dve.tensor_copy(f_hi, i_hi).then_inc(S["ints"], 1)
            link(dve.tensor_reduce(base[:, 1:2], f_dst, AX, ALU.min))
            link(ts(base[:, 0:1], base[:, 1:2], float(N - WIN), None, ALU.min))
            link(ts(f_rel, f_dst, base[:, 0:1], None, ALU.subtract))
            ts(f_bad, f_rel, float(WIN), None, ALU.is_ge).then_inc(S["ints"], 1)
            dve.wait_ge(S["ints"], 4)
            link(stt(f_far, f_hi, float(N), f_dst, ALU.mult, ALU.add))
            link(stt(f_far, f_far, 1.0, f_bad, ALU.add, ALU.mult))
            ts(f_far, f_far, -1.0, None, ALU.add).then_inc(S["idx"], 1)
            link(dve.tensor_reduce(far_at[0:NG, 0:1], f_bad, AX, ALU.max))
            link(stt(f_hi, f_hi, float(WIN), f_rel, ALU.mult, ALU.add))
            stt(f_key, f_bad, 1000.0, f_hi, ALU.mult, ALU.add).then_inc(S["idx"], 1)
            dve.wait_ge(S["tr"], 1)
            dve.tensor_copy(slo[:, :, 0:NG], ps[:, 2, 0:E // P].rearrange("p (c g) -> p c g", c=NC)).then_inc(S["key_in"], 1)
            dve.tensor_copy(key[:, :, 0:NG], ps[:, 3, 0:E // P].rearrange("p (c g) -> p c g", c=NC)).then_inc(S["key_in"], 1)
            link(dve.tensor_copy(base_f[:], ps[0:1, 4, 0:NG]))
            by_two = base_f[:].rearrange("p (g two) -> p g two", two=2)
            stt(base_i[:], by_two[:, :, 1], float(N), by_two[:, :, 0], ALU.mult, ALU.add).then_inc(S["key_in"], 1)
            dve.tensor_copy(far[:, :, 0:NG], ps[:, 5, 0:E // P].rearrange("p (c g) -> p c g", c=NC)).then_inc(S["far_in"], 1)
            link(dve.tensor_reduce(f_flag[:, 0:1], ps[0:1, 4, NG:2 * NG], AX, ALU.max))
            dve.tensor_copy(flags[:, 0:1], f_flag[:, 0:1]).then_inc(S["far_in"], 1)
            dve.wait_ge(S["key_in"], 5)
            dve.wait_ge(S["const_ready"], 12)
            dve.wait_ge(S["c32z"], 2)

            def key_hot(g, i):
                dve.wait_ge(S["hot_free"], g + 1)
                if i % 2 == 0:
                    ts(oh_lo[:, 0, :], iota_lo[:], slo[:, 0, bass.ds(g, 1)], None,
                       ALU.is_equal).then_inc(S["key_ready"], 1)
                for c in range(NC):
                    ts(oh_key[:, i % 2 * NC + c, :], iota_key[:], key[:, c, bass.ds(g, 1)], None,
                       ALU.is_equal).then_inc(S["key_ready"], 1)

            def add_window(g, i, first):
                dve.wait_ge(S["hot_free"], g + 3)
                dve.wait_ge(S["win_free"], g + 2)
                c = c32[:, :, bass.ds(first, WIN)]
                tt(c, c, ps[:, i % 2, 0:KEYS].rearrange("p (a w) -> p a w", w=WIN), ALU.add).then_inc(S["win_free"], 1)

            def groups(t):
                for i in range(NT):
                    g = t * NT + i
                    if i % 2 == 0:
                        two = dve.value_load(base_i[0:1, bass.ds(t * (NT // 2) + i // 2, 1)], min_val=0, max_val=N * N - 1)
                    first = nc.s_assert_within(dve.snap(two & (N - 1) if i % 2 == 0 else two >> 10), 0, N - WIN, skip_runtime_bounds_check_because="bases are cut off at N - WIN")
                    key_hot(g + 1, i + 1)
                    add_window(g, i, first)

            key_hot(0, 0)
            groups(0)
            dve.wait_ge(S["xT_hi"], 1)
            tt(xTs[:, 1, KT // 2:], xTraw[:, KT // 2:], xTs[:, 0, KT // 2:], ALU.subtract).then_inc(S["xT_lo"], 1)
            with dve.Fori(1, NT) as t:
                groups(t)

            dve.wait_ge(S["win_free"], NG + 2)
            dve.wait_ge(S["far_in"], 3)
            with dve.If(flag(dve, 0)):
                for a in range(NT):
                    ts(iota_n[:, a * P:(a + 1) * P], iota_lo[:], float(a * P), None, ALU.add).then_inc(S["far_iota"], 1)
                dve.wait_ge(S["far_iota"], NT)
                cols_s = slo[:].rearrange("p c g -> p (c g)")
                cols_f = far.rearrange("p c g -> p (c g)")
                CHUNKS = NC * (NG + 1)
                with dve.Fori(0, NT) as a:
                    with dve.Fori(0, CHUNKS) as e:
                        n = a * CHUNKS + e
                        dve.wait_ge(S["far_free"], n + 1)
                        ts(oh_far, iota_n, cols_f[:, bass.ds(e, 1)], None, ALU.is_equal).then_inc(S["far_hot"], 1)
                        ts(oh_lo[:, 0, :], iota_lo[:], cols_s[:, bass.ds(e, 1)], None, ALU.is_equal).then_inc(S["far_hot"], 1)
                    dve.wait_ge(S["far_done"], a + 1)
                    ts(far, far, -float(N), None, ALU.add).then_inc(S["far_added"], 1)
                    tt(c32[:, a, :], c32[:, a, :], ps[:, 0:2, :].rearrange("p a n -> p (a n)"), ALU.add).then_inc(S["far_added"], 1)
                    dve.wait_ge(S["far_added"], a * 2 + 2)
            dve.sem_inc(S["counted"], 1)
            for j in range(CA, NT):
                dve.tensor_copy(cst[:, j, :], c32[:, j, :]).then_inc(S["cst_ready"], 1)

            def either(t):
                dve.wait_ge(S["cts_ready"], t + 3)
                tt(adj[:, t, :], cts[:, t, :], cst[:, t, :], ALU.add).then_inc(S["adj_sum"], 1)

            def one(t):
                dve.wait_ge(S["adj_sum"], t + 1)
                ts(adj[:, t, :], adj[:, t, :], 1.0, None, ALU.min).then_inc(S["adj_one"], 1)

            def diagonal(t):
                dve.wait_ge(S["adj_one"], t + 1)
                diag = adj[:, t, bass.ds(t * P, P)]
                tt(diag, diag, id16[:], ALU.add).then_inc(S["adj_ready"], 1)

            either(0)
            one(0)
            with dve.Fori(1, NT) as t:
                either(t)
                diagonal(t - 1)
                one(t)
            diagonal(NT - 1)
            dve.wait_ge(S["deg_done"], 1)
            link(ts(deg[:], ps[:, 7, 0:NT], 1.0, None, ALU.max))
            dve.reciprocal(invdeg[:], deg[:]).then_inc(S["inv_r"], 1)
            dve.wait_ge(S["inv_r"], 1)
            dve.wait_ge(S["small_in"], SMALL)
            for k in range(STEPS):
                ts(winv[:, k, :], invdeg[:], dwb[:, k + 1:k + 2], None, ALU.mult).then_inc(S["winv_r"], 1)
            dve.wait_ge(S["winv_r"], STEPS)
            dve.wait_ge(S["acc0"], NT + 1)
            dve.wait_ge(S["h_lo"], NT + 1)

            def scales(layer, t, i):
                c = bass.ds(t, 1)
                dve.wait_ge(S["std_ready"], t + (layer * NT + 1))
                dve.reciprocal(rstd[:, c], std[:, c]).then_inc(S["rstd_ready"], 1)
                dve.wait_ge(S["rstd_ready"], t + (layer * NT + 1))
                ts(nmr[:, c], mv[:, i, 0:1], rstd[:, c], -1.0, ALU.mult, ALU.mult).then_inc(S["nmr_ready"], 1)

            def moments(layer, t, i):
                dve.drain()
                dve.bn_stats(st[:, i, :], xcur[:, t, :]).then_inc(S["st_a"], 1)
                dve.drain()
                dve.bn_aggr(mv[:, i, :], st[:, i, :]).then_inc(S["moments"], 1)

            def z_lo(layer, t, i):
                dve.wait_ge(S["z_hi"], t + (layer * NT + 1))
                stt(cur[:, 0, 1, t, :], ps[:, 4 + i, :], 1 / WSCALE, cur[:, 0, 0, t, :],
                    ALU.mult, ALU.subtract).then_inc(S["z_lo"], 1)

            def products_in1(t, i):
                z_lo(0, t, i)

            def products_in2(t, i):
                dve.wait_ge(S["alpha_done"], t + 1)
                dve.wait_ge(S["xb_ready"], t + (NT + 1))
                stt(xcur[:, t, :], ps[:, 2 + i, :], 1 / WSCALE, xcur[:, t, :],
                    ALU.mult, ALU.add).then_inc(S["alpha_in"], 1)
                z_lo(1, t, i)

            def norm_loop(layer, total, next_tile=None):
                total(0)
                moments(layer, 0, 0)
                with dve.Fori(0, NT // 2 - 1) as r:
                    for i in (1, 0):
                        t = r * 2 + (2 - i)
                        total(t)
                        moments(layer, t, i)
                        scales(layer, t - 1, 1 - i)
                total(NT - 1)
                moments(layer, NT - 1, 1)
                scales(layer, NT - 2, 0)
                if next_tile is not None:
                    next_tile(0, 0)
                scales(layer, NT - 1, 1)

            for k in range(1, STEPS):
                if k == 2:
                    link(dve.tensor_reduce(cnt[:], c32[:], AX, ALU.add))
                    link(dve.tensor_reduce(far_at[:, 1:2], cnt[:], AX, ALU.max))
                    link(ts(cnt1[:], cnt[:], 1.0, None, ALU.max))
                    link(dve.reciprocal(gsc[:], cnt1[:]))
                    link(dve.reciprocal(nan[:], cnt[:]))
                    link(ts(nan[:], nan[:], 0.0, None, ALU.mult))
                with dve.Fori(0, NT) as t:
                    n = t + ((k - 1) * NT + 1)
                    dve.wait_ge(S["step_hi"], n)
                    stt(cur[:, k % 2, 1, t, :], ps[:, t, :], invdeg[:, bass.ds(t, 1)], cur[:, k % 2, 0, t, :],
                        ALU.mult, ALU.subtract).then_inc(S["step_lo"], 1)
                    stt(acc[:, t, :], ps[:, t, :], winv[:, k - 1, bass.ds(t, 1)], acc[:, t, :],
                        ALU.mult, ALU.add).then_inc(S["acc_r"], 1)

            def total0(t):
                dve.wait_ge(S["step_done"], t + ((STEPS - 1) * NT + 1))
                stt(acc[:, t, :], ps[:, t, :], winv[:, STEPS - 1, bass.ds(t, 1)], acc[:, t, :],
                    ALU.mult, ALU.add).then_inc(S["acc_r"], 1)
                dve.wait_ge(S["acc_r"], t + ((STEPS - 1) * NT + 1))
                stt(xcur[:, t, :], acc[:, t, :], 0.0, xcur[:, t, :], ALU.max, ALU.add).then_inc(S["y_ready"], 1)
            dve.wait_ge(S["x_in"], 16)
            dve.wait_ge(S["wa_done"], 1)
            link(dve.tensor_reduce(f_flag[:, 1:2], ps[0:1, 7, 320:320 + P], AX, ALU.max))
            ts(flags[:, 1:2], f_flag[:, 1:2], EXACT, None, ALU.is_gt).then_inc(S["big_in"], 1)
            link(ts(abT[:], ps[:, 7, 0:256].rearrange("p (k c) -> p k c", c=64)[:, :, 0:VCOL + H], WSCALE, None, ALU.mult))
            link(dve.tensor_copy(wa[:, 0], abT[:]))
            tt(wa[:, 1], abT[:], wa[:, 0], ALU.subtract).then_inc(S["wa_lo"], 1)
            tt(crow[:, 0:1], ps[0:H, 7, 256:257], abc[:], ALU.add).then_inc(S["crow_r"], 1)

            norm_loop(0, total0, products_in1)

            products_in1(1, 1)
            with dve.Fori(1, NT // 2) as r:
                for i in range(2):
                    products_in1(r * 2 + i, i)

            dve.wait_ge(S["big_in"], 1)
            with dve.If(flag(dve, 1)):
                dve.wait_ge(S["y_ready"], NT)
                with dve.Fori(0, NT) as t:
                    tt(c_left[:, t, :], c32[:, t, :], cst[:, t, :], ALU.subtract).then_inc(S["left_in"], 1)
                with dve.Fori(0, NT) as t:
                    dve.wait_ge(S["left_done"], t + 1)
                    dve.tensor_copy(ct_left[:, t, :], bank16(7)).then_inc(S["left_t"], 1)

            def total1(t):
                dve.wait_ge(S["gather1_done"], t + 1)
                dve.wait_ge(S["xb_ready"], t + 1)
                tt(xcur[:, t, :], ps[:, t, :], xcur[:, t, :], ALU.add).then_inc(S["y_ready"], 1)
            norm_loop(1, total1, products_in2)

            products_in2(1, 1)
            with dve.Fori(1, NT // 2) as r:
                for i in range(2):
                    products_in2(r * 2 + i, i)
            dve.wait_ge(S["alpha_in"], NT + 2)

            def total2(t):
                dve.wait_ge(S["gather2_done"], t + 1)
                stt(xcur[:, t, :], ps[:, t, :], gsc[:, bass.ds(t, 1)], xcur[:, t, :],
                    ALU.mult, ALU.add).then_inc(S["y_ready"], 1)
            norm_loop(2, total2)

            def wx_evict(t, i):
                dve.wait_ge(S["wx_done"], t + 1)
                stt(wx[:, t, :], ps[:, 4 + i, :], 1 / WSCALE, bb[:, 2, :], ALU.mult, ALU.add).then_inc(S["wx_in"], 1)
                dve.wait_ge(S["exp_in"], t * 2 + 6)
                ts(nv[:, t, :], ps[:, 2 + i, VCOL:VCOL + H], -1 / WSCALE, None, ALU.mult).then_inc(S["nv_in"], 1)
                dve.wait_ge(S["wx_in"], t + 3)
                tt(yf[:, i, :, :, 0:DH], wx[:, t, :].rearrange("p (h d) -> p h d", h=H).unsqueeze(2).broadcast_to([P, H, 2, DH]),
                   yf[:, i, :, :, DH:DH + 1].broadcast_to([P, H, 2, DH]), ALU.mult).then_inc(S["y_ready3"], 1)
                dve.tensor_reduce(wm[:, bass.ds(t, 1)], wx[:, t, :], AX, ALU.max, apply_absolute_value=True).then_inc(S["wm_in"], 1)
            def mask(h, q, j, u=None):
                if j == 0:
                    dve.wait_ge(S["uf_ready"], h + 1)
                    dve.wait_ge(S["head_done"], h + 1)
                stt(cz[q][:, j, :], uf[:, q] if u is None else u, nv[:, j, bass.ds(h, 1)], c32[:, j, :],
                    ALU.is_gt, ALU.mult).then_inc(S["cz_ready"], 1)

            with dve.Fori(0, NT // 2 - 1) as r:
                for i in range(2):
                    wx_evict(r * 2 + i, i)

            uv = ps[:, 6:8, :].rearrange("p a n -> p (a n)")
            dve.wait_ge(S["uv_done"], 1)
            ts(z0, uv[0:H], 1 / WSCALE, crow[:, 0:1], ALU.mult, ALU.add).then_inc(S["uv_in"], 1)
            dve.wait_ge(S["uv_in"], 1)
            dve.tensor_copy(usf[:, 0], z0).then_inc(S["usf_in"], 1)
            dve.wait_ge(S["usf_in"], 1)
            tt(usf[:, 1], z0, usf[:, 0], ALU.subtract).then_inc(S["usf_in"], 1)
            wx_evict(NT - 2, 0)
            dve.wait_ge(S["nv_in"], NT + 1)
            mask(0, 0, 0, uf0)
            mask(0, 0, 1, uf0)
            wx_evict(NT - 1, 1)

            dve.wait_ge(S["wm_in"], NT)
            dve.wait_ge(S["nv_in"], NT + 2)
            dve.tensor_reduce(lim[:, 1:2], wm[:], AX, ALU.max).then_inc(S["lim_a"], 1)
            dve.tensor_reduce(lim[:, 2:3], nv[:].rearrange("p t h -> p (t h)"), AX, ALU.max, apply_absolute_value=True).then_inc(S["lim_a"], 1)
            mask(0, 0, 2, uf0)
            dve.wait_ge(S["lim_a"], 2)
            ts(lim[:, 0:1], lim[:, 1:2], 1 / WXMAX, None, ALU.mult).then_inc(S["lim_a"], 1)
            dve.wait_ge(S["q_done"], 1)
            dve.memset(qc[:, :, NT:OS], 1.0).then_inc(S["qz"], 1)
            dve.tensor_copy(qc[:, :, 0:NT], ps[:, 2, 0:NT * H].rearrange("p (t h) -> p h t", h=H)).then_inc(S["q_in"], 1)
            mask(0, 0, 3, uf0)
            dve.wait_ge(S["lim_a"], 3)
            stt(lim[:, 0:1], lim[:, 2:3], 1 / VMAX, lim[:, 0:1], ALU.mult, ALU.max).then_inc(S["lim_a"], 1)
            dve.wait_ge(S["q_in"], 1)
            dve.wait_ge(S["qz"], 1)
            dve.tensor_reduce(lim[:, 1:2], qc[:].rearrange("p h t -> p (h t)"), AX, ALU.max).then_inc(S["lim_a"], 1)
            dve.tensor_reduce(lim[:, 3:4], qc[:].rearrange("p h t -> p (h t)"), AX, ALU.min).then_inc(S["lim_a"], 1)
            mask(0, 0, 4, uf0)
            dve.wait_ge(S["lim_a"], 6)
            stt(lim[:, 0:1], lim[:, 1:2], 1 / QMAX, lim[:, 0:1], ALU.mult, ALU.max).then_inc(S["lim_a"], 1)
            ts(lim[:, 2:3], lim[:, 3:4], QMIN, None, ALU.is_lt).then_inc(S["lim_a"], 1)
            mask(0, 0, 5, uf0)
            dve.wait_ge(S["lim_a"], 8)
            stt(lim[:, 0:1], lim[:, 2:3], 2.0, lim[:, 0:1], ALU.mult, ALU.max).then_inc(S["lim_in"], 1)
            mask(0, 0, 6, uf0)
            dve.wait_ge(S["lim_done"], 1)
            link(dve.tensor_reduce(lim[0:1, 1:2], ps[0:1, 3, P:2 * P], AX, ALU.max))
            link(stt(lim[0:1, 2:3], f_flag[:, 1:2], 1 / EXACT, lim[0:1, 1:2], ALU.mult, ALU.max))
            ts(flags[:, 2:3], lim[0:1, 2:3], 1.0, None, ALU.is_gt).then_inc(S["mode"], 1)
            mask(0, 0, NT - 1, uf0)
            dve.wait_ge(S["mode"], 1)
            with dve.If(flag(dve, 2)):
                dve.wait_ge(S["y_lo"], NT + 2)
                dve.wait_ge(S["yq_ready"], 2)
                dve.wait_ge(S["q_in"], 1)
                glinks = [0]

                def glink(ins):
                    glinks[0] += 1
                    ins.then_inc(S["glink"], 1)
                    dve.wait_ge(S["glink"], glinks[0])

                glink(ts(vrow, uv[VCOL:VCOL + H], 1 / WSCALE, None, ALU.mult))
                glink(dve.tensor_reduce(crow[:, 1:2], vrow, AX, ALU.min))
                ts(wrow, vrow, crow[:, 1:2], 1.0, ALU.subtract, ALU.add).then_inc(S["w_row"], 1)
                dve.wait_ge(S["w_done"], 1)
                wcol = vc[:, 0, :]
                glink(dve.tensor_copy(wcol, ps[:, 0, 0:NT * H]))
                with dve.Fori(0, H) as h:
                    dve.wait_ge(S["most_free"], h + 1)
                    dve.memset(most, 0.0).then_inc(S["most_a"], 1)
                    for j in range(NT):
                        dve.wait_ge(S["most_a"], h * (2 * NT + 1) + (2 * j + 1))
                        ts(seen, c32[:, j, :], 1.0, wcol[:, bass.ds(j * H + h, 1)], ALU.min, ALU.mult).then_inc(S["most_a"], 1)
                        dve.wait_ge(S["most_a"], h * (2 * NT + 1) + (2 * j + 2))
                        tt(most, most, seen, ALU.max).then_inc(S["most_a"], 1)
                    dve.wait_ge(S["most_a"], h * (2 * NT + 1) + (2 * NT + 1))
                    dve.sem_inc(S["most_ready"], 1)
                    dve.wait_ge(S["most_done"], h + 1)
                    dve.tensor_reduce(mcol[:, :, bass.ds(h, 1)].rearrange("p t a -> p (t a)"),
                                      ps[:, 2:4, :].rearrange("p a (b n) -> p (a b) n", n=P), AX, ALU.max).then_inc(S["most_in"], 1)
                    dve.wait_ge(S["most_in"], h + 1)
                    dve.sem_inc(S["most_free"], 1)
                dve.wait_ge(S["m_done"], 1)
                glink(ts(mrow, ps[0:H, 0:2, :].rearrange("p a n -> p (a n)"), crow[:, 1:2], -1.0, ALU.add, ALU.add))
                glink(tt(zrow, z0, mrow, ALU.add))
                ins = stt(mrow, zrow, SLOPE, zrow, ALU.mult, ALU.max)
                ins.then_inc(S["m_in"], 1)
                dve.wait_ge(S["m_in"], 1)
                glink(tt(urow[:, 0, :], z0, mrow, ALU.subtract))
                glink(stt(urow[:, 1, :], z0, SLOPE, mrow, ALU.mult, ALU.subtract))
                glink(dve.tensor_copy(us[:, 0], urow))
                tt(us[:, 1], urow, us[:, 0], ALU.subtract).then_inc(S["us_lo"], 1)
                dve.wait_ge(S["v_done"], 1)
                for i, f in enumerate((1 - SLOPE, SLOPE)):
                    ts(vc[:, i, :], ps[:, 0, 0:NT * H], f, None, ALU.mult).then_inc(S["vc_ready"], 1)
                dve.wait_ge(S["us_lo"], 1)
                dve.wait_ge(S["vc_ready"], 2)

                def scores(h, q, j):
                    if j == 0:
                        dve.wait_ge(S["ub_ready"], h + 1)
                    dve.wait_ge(S["e_ready"], h * NT + (j + 1))
                    stt(T[:, j % 2, :], ub[:, q, 0, :], vc[:, 0, bass.ds(j * H + h, 1)], ub[:, q, 1, :],
                        ALU.add, ALU.max).then_inc(S["t_ready"], 1)

                def weights(h, j):
                    n = h * NT + j
                    dve.wait_ge(S["e_ready"], n + 3)
                    dve.wait_ge(S["p_free"], n + 1)
                    stt(PR[:, j % 2, :], EX[:, j % 2, :], 2.0, c32[:, j, :], ALU.min, ALU.mult).then_inc(S["p_ready"], 1)

                def head_out(h):
                    o = ps[:, 6:8, 0:4 * (DH + 1)].rearrange("p a (b d) -> p a b d", b=4)
                    dve.wait_ge(S["back_done"], h + 3)
                    ts(rden[:], o[:, :, :, DH], 1e-37, None, ALU.max).then_inc(S["rd_r"], 1)
                    dve.wait_ge(S["rd_r"], h * 2 + 1)
                    dve.reciprocal(rden[:], rden[:]).then_inc(S["rd_r"], 1)
                    dve.wait_ge(S["rd_r"], h * 2 + 2)
                    tt(att.rearrange("p (a b) d -> p a b d", a=2), o[:, :, :, 0:DH],
                       rden[:].unsqueeze(3).broadcast_to([P, 2, 4, DH]), ALU.mult).then_inc(S["back_free"], 1)
                    dve.wait_ge(S["back_free"], h + 2)
                    xs = xcur[:, :, bass.ds(h * DH, DH)]
                    tt(xs, xs, att, ALU.add).then_inc(S["att_added"], 1)

                scores(0, 0, 0)
                with dve.Fori(0, H // 2) as hp:
                    for q in range(2):
                        h = hp * 2 + q
                        for j in range(NT):
                            if j < NT - 1:
                                scores(h, q, j + 1)
                            else:
                                scores(h + 1, 1 - q, 0)
                            weights(h, j)
                        head_out(h)
                dve.wait_ge(S["att_added"], H)
                for t in range(NT):
                    dve.bn_stats(st8[:, t, 0:6], xcur[:, t, 0:D - DH]).then_inc(S["st8_in"], 1)
            with dve.Else():
                def combine(h, q, n):
                    o = ps[:, 2 + 3 * q:5 + 3 * q, 0:3 * YW].rearrange("p a (b d) -> p a b d", b=3)
                    c = comb[:, q].rearrange("p (a b) d -> p a b d", a=3)
                    if n == 0:
                        dve.wait_ge(S["head_done"], h + 3)
                        dve.wait_ge(S["att_in"], h + 1)
                        qh = qc[:, bass.ds(h, 1), :].rearrange("p o (a b) -> p (o a) b", a=3)
                        tt(c, o[:, :, :, 0:DH + 1], qh.unsqueeze(3).broadcast_to([P, 3, 3, DH + 1]),
                           ALU.mult).then_inc(S["comb_ready"], 1)
                    if n == 1:
                        dve.wait_ge(S["comb_ready"], h * 2 + 5)
                        tt(c, c, o[:, :, :, DH + 1:YW], ALU.subtract).then_inc(S["comb_ready"], 1)
                    if n == 2:
                        dve.wait_ge(S["comb_ready"], h * 2 + 6)
                        ts(rdf[:, q], comb[:, q, :, DH], 1e-37, None, ALU.max).then_inc(S["den_ready"], 1)
                    if n == 3:
                        dve.wait_ge(S["den_ready"], h * 2 + 1)
                        dve.reciprocal(rdf[:, q], rdf[:, q]).then_inc(S["den_ready"], 1)

                dve.wait_ge(S["y_lo"], NT + 2)
                dve.wait_ge(S["cz_ready"], 3 * NT)
                for j in range(NT):
                    mask(1, 1, j)
                with dve.Fori(0, H // 2 - 1) as hp:
                    for q in range(2):
                        h = hp * 2 + q
                        for j in range(NT):
                            mask(h + 2, q, j)
                            if j < 4:
                                combine(h, q, j)
                for n in range(4):
                    combine(H - 2, 0, n)
                dve.wait_ge(S["att_in"], H + 1)
                for t in range(NT):
                    dve.bn_stats(st8[:, t, 0:6], xcur[:, t, 0:D - DH]).then_inc(S["st8_in"], 1)
                for n in range(4):
                    combine(H - 1, 1, n)
                dve.wait_ge(S["den_ready"], 2 * H)
                last = comb[:, 1, 0:NT, 0:DH]
                tt(last, last, rdf[:, 1, 0:NT].unsqueeze(2).broadcast_to([P, NT, DH]), ALU.mult).then_inc(S["last_in"], 1)
                dve.wait_ge(S["last_in"], 1)
                xs = xcur[:, :, D - DH:D]
                tt(xs, xs, last, ALU.add).then_inc(S["last_in"], 1)
                dve.drain()
            for t in range(NT):
                dve.bn_stats(st8[:, t, 6:12], xcur[:, t, D - DH:D]).then_inc(S["st8_in"], 1)
            dve.drain()
            for t in range(NT):
                dve.bn_aggr(mv8[:, t, :], st8[:, t, :]).then_inc(S["mv8_in"], 1)
            dve.wait_ge(S["std8"], 1)
            link(dve.reciprocal(rstd[:], std[:]))
            link(tt(rstd[:], rstd[:], nan[:], ALU.add))
            stt(nmr[:], mv8[:, :, 0], -1.0, rstd[:], ALU.mult, ALU.mult).then_inc(S["scale8"], 1)
            dve.wait_ge(S["scale8"], 1)
            for t in range(1, NT, 2):
                ts(xcur[:, t, :], xcur[:, t, :], rstd[:, t:t + 1], nmr[:, t:t + 1], ALU.mult, ALU.add).then_inc(S["out_odd"], 1)


def kernel(**inputs):
    import numpy as np
    import concourse.bacc as bacc
    from concourse.bass_utils import run_bass_kernel_spmd

    g = {k: np.asarray(v) for k, v in inputs.items()}
    laid = {
        "x": g["x"], "xT": g["x"].T, "src": g["src"], "dst": g["dst"],
        "W0": g["L0_gnn_W"], "b0": g["L0_gnn_b"], "dw": g["L0_gnn_diffusion_weights"],
        "W1T": g["L1_gnn_W"].T, "b1": g["L1_gnn_b"],
        "wc": g["L2_gnn_wc"], "wn": g["L2_gnn_wn"], "b2": g["L2_gnn_bias"],
        "W3": g["L3_gnn_Ws"].transpose(1, 0, 2).reshape(D, D),
        "W3T": g["L3_gnn_Ws"].transpose(0, 2, 1).reshape(D, D),
        "b3": g["L3_gnn_Wb"].reshape(D), "b3T": g["L3_gnn_Wb"].reshape(KT, P).T, "aw": g["L3_gnn_a_w"], "ab": g["L3_gnn_a_b"],
    }
    laid = {k: np.ascontiguousarray(v) for k, v in laid.items()}
    nc = bacc.Bacc("TRN2", target_bir_lowering=False, num_devices=1)
    aps = {k: nc.dram_tensor(f"in_{k}", v.shape, mybir.dt.from_np(v.dtype), kind="ExternalInput").ap()
           for k, v in laid.items()}
    out = nc.dram_tensor("out", (N, D), F32, kind="ExternalOutput").ap()
    build(nc, **aps, out=out)
    r = run_bass_kernel_spmd(nc, [{f"in_{k}": v for k, v in laid.items()}], core_ids=[0])
    return r.results[0]["out"]
```
